# Optimizing a Trainium2 kernel written in Bass

```python
import numpy as np
import jax
import jax.numpy as jnp

def _softmax(x, axis=-1):
    return jax.nn.softmax(x, axis=axis)

def _gelu(x):
    return jax.nn.gelu(x, approximate=True)

def _silu(x):
    return jax.nn.silu(x)

def _sigmoid(x):
    return jax.nn.sigmoid(x)

def _layernorm(x, axis=-1, eps=1e-05):
    m = jnp.mean(x, axis=axis, keepdims=True)
    v = jnp.var(x, axis=axis, keepdims=True)
    return (x - m) / jnp.sqrt(v + eps)

def _scatter_add(tgt, idx, src, axis=0):
    return tgt.at[idx].add(src)

def _segment_sum(src, seg, n):
    return jax.ops.segment_sum(src, seg, n)
kernel_name = 'mk_decoder_postln_d2_seqx_r8_8a0f2f'

def setup_inputs(seed: int=0):
    np.random.seed(seed)
    _w = jnp.asarray

    def _rec_inputs():
        import jax
        import jax.numpy as jnp
        _rk = jax.random.key(seed)
        x = -0.0002928 + 1 * jax.random.normal(jax.random.fold_in(_rk, 1), (16, 64, 256), jnp.float32)
        _lenS = 64 - jax.random.randint(jax.random.fold_in(_rk, 7), (16,), 0, max(1, 64 // 4) + 1, jnp.int32)
        _lenS2 = 64 - jax.random.randint(jax.random.fold_in(_rk, 8), (16,), 0, max(1, 64 // 4) + 1, jnp.int32)
        _ctx_2048P = jax.random.normal(jax.random.fold_in(_rk, 11), (16, 16, 256), jnp.float32)
        _ctx_2048c = jax.random.dirichlet(jax.random.fold_in(_rk, 511), 0.3 * jnp.ones((16,), jnp.float32), (16, 64))
        _ctx_2048t = jnp.einsum('bsk,bkd->bsd', _ctx_2048c, _ctx_2048P)
        _ctx_2048t = _ctx_2048t * jax.lax.rsqrt(jnp.mean(jnp.square(_ctx_2048t)) + 1e-12) * 0.953939
        ctx_2048 = -1.39393e-06 + 0.999914 * (_ctx_2048t + 0.3 * jax.random.normal(jax.random.fold_in(_rk, 611), (16, 64, 256), jnp.float32))
        _validS = jnp.arange(64)[None, :] < _lenS[:, None]
        _validS2 = jnp.arange(64)[None, :] < _lenS2[:, None]
        _causal = jnp.tril(jnp.ones((64, 64), dtype=bool))
        mask_BxS2_ik0 = jnp.where(jnp.broadcast_to(_validS2[:, :], (16, 64)), 0, 1).astype(jnp.int32)
        return (x, ctx_2048, mask_BxS2_ik0)
    x, ctx_2048, mask_BxS2_ik0 = _rec_inputs()

    def _L0_attn_setup():
        import jax, jax.numpy as jnp
        import numpy as np
        D_MODEL = 256
        N_QUERY = 4
        N_HEAD = 8
        D_HEAD = D_MODEL // (N_QUERY * N_HEAD)
        D_KV = D_HEAD * N_HEAD
        BATCH, SEQ = (2, 256)
        key = jax.random.key(seed)
        ks = jax.random.split(key, 5)
        w_scale = 1.0 / np.sqrt(D_MODEL).astype(np.float32)
        x = jax.random.normal(ks[0], (BATCH, SEQ, D_MODEL), jnp.float32)
        Wq = jax.random.normal(ks[1], (D_MODEL, D_MODEL), jnp.float32) * w_scale
        Wk = jax.random.normal(ks[2], (D_KV, D_MODEL), jnp.float32) * w_scale
        Wv = jax.random.normal(ks[3], (D_KV, D_MODEL), jnp.float32) * w_scale
        memory = jax.random.normal(ks[4], (D_KV, D_KV), jnp.float32) * 0.02
        memory_norm = jnp.ones((D_KV, 1), jnp.float32)
        memory_weight = jnp.ones((1,), jnp.float32)
        return dict(x=x, Wq=Wq, Wk=Wk, Wv=Wv, memory=memory, memory_norm=memory_norm, memory_weight=memory_weight)
    _L0_attn_all = _L0_attn_setup()
    _L0_attn_in = {k: v for k, v in _L0_attn_all.items() if k in ('Wq', 'Wk', 'Wv', 'memory', 'memory_norm', 'memory_weight')}
    del _L0_attn_all

    def _L0_xattn_setup():
        import math
        import jax, jax.numpy as jnp
        import numpy as np
        N_HEADS = 8
        CHANNELS = 64
        K_CH = CHANNELS // N_HEADS
        THETA = 10000.0

        def _rope_freqs(length, dim):
            inv_freq = 1.0 / THETA ** (jnp.arange(0, dim, 2, dtype=jnp.float32) / dim)
            f = jnp.arange(length, dtype=jnp.float32)[:, None] * inv_freq[None, :]
            return jnp.concatenate([f, f], axis=-1)

        def _apply_rotary(pos, t):
            half = t.shape[-1] // 2
            rot = jnp.concatenate([-t[..., half:], t[..., :half]], axis=-1)
            return t * jnp.cos(pos) + rot * jnp.sin(pos)

        def _proj(inp, W, b):
            return jnp.einsum('oc,bct->bot', W, inp) + b[None, :, None]
        key = jax.random.key(seed)
        ks = jax.random.split(key, 10)
        B, C, T = (4, CHANNELS, 256)
        bound = math.sqrt(6.0 / (C + C))

        def w(k):
            return jax.random.uniform(k, (C, C), jnp.float32, -bound, bound)
        return {'x': jax.random.normal(ks[0], (B, C, T), jnp.float32), 'c': jax.random.normal(ks[1], (B, C, T), jnp.float32), 'Wq': w(ks[2]), 'bq': jnp.zeros((C,), jnp.float32), 'Wk': w(ks[3]), 'bk': jnp.zeros((C,), jnp.float32), 'Wv': w(ks[4]), 'bv': jnp.zeros((C,), jnp.float32), 'Wo': w(ks[5]), 'bo': jnp.zeros((C,), jnp.float32)}
    _L0_xattn_all = _L0_xattn_setup()
    _L0_xattn_in = {k: v for k, v in _L0_xattn_all.items() if k in ('Wq', 'bq', 'Wk', 'bk', 'Wv', 'bv', 'Wo', 'bo')}
    del _L0_xattn_all

    def _L0_ffn_setup():
        import jax, jax.numpy as jnp
        import numpy as np
        TOP_K = 2

        def _gelu(v):
            return jax.nn.gelu(v, approximate=False)
        key = jax.random.key(seed)
        ks = jax.random.split(key, 7)
        B, T, D, I, E = (2, 256, 256, 1024, 8)
        s = 0.02
        return {'x': jax.random.normal(ks[0], (B, T, D), jnp.float32), 'rw1': jax.random.normal(ks[1], (D, D // 2), jnp.float32) * s, 'rw2': jax.random.normal(ks[2], (D // 2, E), jnp.float32) * s, 'w1': jax.random.normal(ks[3], (E, D, I), jnp.float32) * s, 'b1': jax.random.normal(ks[4], (E, I), jnp.float32) * s, 'w2': jax.random.normal(ks[5], (E, I, D), jnp.float32) * s, 'b2': jax.random.normal(ks[6], (E, D), jnp.float32) * s}
    _L0_ffn_all = _L0_ffn_setup()
    _L0_ffn_in = {k: v for k, v in _L0_ffn_all.items() if k in ('rw1', 'rw2', 'w1', 'b1', 'w2', 'b2')}
    del _L0_ffn_all

    def _L1_attn_setup():
        import jax, jax.numpy as jnp
        import numpy as np
        B, N, D, H = (2, 256, 256, 16)
        HD = D // H
        CHUNK = 64
        BASE = 10000.0

        def _l2norm(x, eps=1e-06):
            return x * jax.lax.rsqrt(jnp.sum(x * x, axis=-1, keepdims=True) + eps)

        def _rope(x):
            n, d = (x.shape[1], x.shape[-1])
            inv = 1.0 / BASE ** (jnp.arange(0, d, 2, dtype=jnp.float32) / d)
            th = jnp.arange(n, dtype=jnp.float32)[:, None] * inv
            cos = jnp.cos(th)[None, :, None, :]
            sin = jnp.sin(th)[None, :, None, :]
            x1, x2 = jnp.split(x, 2, axis=-1)
            return jnp.concatenate([x1 * cos - x2 * sin, x1 * sin + x2 * cos], axis=-1)

        def _kernel_regression(k, v, beta):
            b, n, h, dk = k.shape
            dv = v.shape[-1]
            nc = n // CHUNK
            Kc = k.reshape(b, nc, CHUNK, h, dk).transpose(1, 0, 3, 2, 4)
            Vc = v.reshape(b, nc, CHUNK, h, dv).transpose(1, 0, 3, 2, 4)
            Bc = beta.reshape(b, nc, CHUNK, h).transpose(1, 0, 3, 2)
            eye = jnp.eye(CHUNK, dtype=k.dtype)

            def step(S, inp):
                K, V, bt = inp
                A = jnp.tril(jnp.einsum('bhik,bhjk->bhij', K, K) * bt[:, :, None, :], -1)
                rhs = V - jnp.einsum('bhck,bhkv->bhcv', K, S)
                Vn = jax.scipy.linalg.solve_triangular(eye + A, rhs, lower=True)
                S = S + jnp.einsum('bhck,bhcv->bhkv', K * bt[..., None], Vn)
                return (S, Vn)
            S0 = jnp.zeros((b, h, dk, dv), k.dtype)
            S, Vn = jax.lax.scan(step, S0, (Kc, Vc, Bc))
            v_new = Vn.transpose(1, 0, 3, 2, 4).reshape(b, n, h, dv)
            return (v_new, S)
        key = jax.random.key(seed)
        ks = jax.random.split(key, 6)
        s = 0.02
        return {'x': jax.random.normal(ks[0], (B, N, D), jnp.float32), 'Wq': jax.random.normal(ks[1], (D, D), jnp.float32) * s, 'Wk': jax.random.normal(ks[2], (D, D), jnp.float32) * s, 'Wv': jax.random.normal(ks[3], (D, D), jnp.float32) * s, 'Wo': jax.random.normal(ks[4], (D, D), jnp.float32) * s, 'Wb': jax.random.normal(ks[5], (D, H), jnp.float32) * s}
    _L1_attn_all = _L1_attn_setup()
    _L1_attn_in = {k: v for k, v in _L1_attn_all.items() if k in ('Wq', 'Wk', 'Wv', 'Wo', 'Wb')}
    del _L1_attn_all

    def _L1_xattn_setup():
        import jax, jax.numpy as jnp
        import numpy as np
        import math
        H = 256
        NH = 16
        HD = H // NH
        EPS_LN = 1e-05
        RES_SCALE_MAX = 0.3

        def _nan_clean(x, lim=10000.0):
            return jnp.nan_to_num(x, nan=0.0, posinf=lim, neginf=-lim)
        key = jax.random.key(seed)
        ks = jax.random.split(key, 12)
        B, S, T = (4, 256, 32)
        std = 1.0 / math.sqrt(H)
        return {'hidden_states': jax.random.normal(ks[0], (B, S, H), jnp.float32), 'audio_tokens': jax.random.normal(ks[1], (B, T, H), jnp.float32), 'attention_mask': jax.random.randint(ks[2], (B, T), 0, 2, jnp.int32), 'Wq': jax.random.normal(ks[3], (H, H), jnp.float32) * std, 'bq': jnp.zeros((H,), jnp.float32), 'Wk': jax.random.normal(ks[4], (H, H), jnp.float32) * std, 'bk': jnp.zeros((H,), jnp.float32), 'Wv': jax.random.normal(ks[5], (H, H), jnp.float32) * std, 'bv': jnp.zeros((H,), jnp.float32), 'Wo': jax.random.normal(ks[6], (H, H), jnp.float32) * std, 'bo': jnp.zeros((H,), jnp.float32), 'ln_gamma': jnp.ones((H,), jnp.float32), 'ln_beta': jnp.zeros((H,), jnp.float32), 'residual_scale': jnp.float32(0.05)}
    _L1_xattn_all = _L1_xattn_setup()
    _L1_xattn_in = {k: v for k, v in _L1_xattn_all.items() if k in ('Wq', 'bq', 'Wk', 'bk', 'Wv', 'bv', 'Wo', 'bo', 'ln_gamma', 'ln_beta', 'residual_scale')}
    del _L1_xattn_all

    def _L1_ffn_setup():
        import jax, jax.numpy as jnp
        import numpy as np
        B, S, H, I, E, F, K, R, TOPK = (1, 128, 256, 176, 64, 8, 8, 8, 6)
        ISH = 2 * I

        def _fused_linear(x, W, qa, qb, scale, w):
            out = x @ W.T
            a = jnp.einsum('th,krh->tkr', x, qa)
            b = jnp.einsum('tkr,khr->tkh', a, qb)
            mix = jnp.einsum('tkh,tk->th', b, w)
            return out + scale[None, :] * mix

        def _moe_forward(hidden_states, gate_weight, inv_mapping, mask_up_W, gate_W, gate_qa, gate_qb, gate_scale, up_W, up_qa, up_qb, up_scale, down_W, down_qa, down_qb, down_scale, sh_gate_W, sh_up_W, sh_down_W):
            b, s, h = hidden_states.shape
            x = hidden_states.reshape(-1, h)
            T = x.shape[0]
            scores = jax.nn.softmax(x @ gate_weight.T, axis=-1)
            topk_w, topk_idx = jax.lax.top_k(scores, TOPK)
            w_dense = jnp.zeros((T, E), x.dtype).at[jnp.arange(T)[:, None], topk_idx].add(topk_w)
            flat = w_dense[:, inv_mapping]
            scalar = flat.sum(-1)
            soft = jax.nn.softmax(jnp.where(flat == 0, -1000000000.0, flat), axis=-1)

            def expert(muW, gW, gqa, gqb, gs, uW, uqa, uqb, us, dW, dqa, dqb, ds, w):
                xe = x + w @ muW.T
                gate = jax.nn.silu(_fused_linear(xe, gW, gqa, gqb, gs, w))
                up = _fused_linear(xe, uW, uqa, uqb, us, w)
                return _fused_linear(gate * up, dW, dqa, dqb, ds, w)
            outs = jax.vmap(expert, in_axes=(0,) * 13 + (1,))(mask_up_W, gate_W, gate_qa, gate_qb, gate_scale, up_W, up_qa, up_qb, up_scale, down_W, down_qa, down_qb, down_scale, soft)
            y = jnp.einsum('fth,tf->th', outs, scalar).reshape(b, s, h)
            sh = jax.nn.silu(hidden_states @ sh_gate_W.T) * (hidden_states @ sh_up_W.T) @ sh_down_W.T
            return y + sh
        key = jax.random.key(seed)
        ks = jax.random.split(key, 20)
        g = lambda k, shape, s=0.02: jax.random.normal(k, shape, jnp.float32) * s
        return {'hidden_states': jax.random.normal(ks[0], (B, S, H), jnp.float32), 'gate_weight': g(ks[1], (E, H)), 'inv_mapping': jnp.arange(E, dtype=jnp.int32).reshape(F, K), 'mask_up_W': g(ks[2], (F, H, K)), 'gate_W': g(ks[3], (F, I, H)), 'gate_qa': g(ks[4], (F, K, R, H)), 'gate_qb': g(ks[5], (F, K, I, R)), 'gate_scale': jnp.full((F, I), 0.1, jnp.float32), 'up_W': g(ks[6], (F, I, H)), 'up_qa': g(ks[7], (F, K, R, H)), 'up_qb': g(ks[8], (F, K, I, R)), 'up_scale': jnp.full((F, I), 0.1, jnp.float32), 'down_W': g(ks[9], (F, H, I)), 'down_qa': g(ks[10], (F, K, R, I)), 'down_qb': g(ks[11], (F, K, H, R)), 'down_scale': jnp.full((F, H), 0.1, jnp.float32), 'sh_gate_W': g(ks[12], (ISH, H)), 'sh_up_W': g(ks[13], (ISH, H)), 'sh_down_W': g(ks[14], (H, ISH))}
    _L1_ffn_all = _L1_ffn_setup()
    _L1_ffn_in = {k: v for k, v in _L1_ffn_all.items() if k in ('gate_weight', 'inv_mapping', 'mask_up_W', 'gate_W', 'gate_qa', 'gate_qb', 'gate_scale', 'up_W', 'up_qa', 'up_qb', 'up_scale', 'down_W', 'down_qa', 'down_qb', 'down_scale', 'sh_gate_W', 'sh_up_W', 'sh_down_W')}
    del _L1_ffn_all
    return {'x': x, 'ctx_2048': ctx_2048, 'mask_BxS2_ik0': mask_BxS2_ik0, 'L0_attn_Wq': _L0_attn_in['Wq'], 'L0_attn_Wk': _L0_attn_in['Wk'], 'L0_attn_Wv': _L0_attn_in['Wv'], 'L0_attn_memory': _L0_attn_in['memory'], 'L0_attn_memory_norm': _L0_attn_in['memory_norm'], 'L0_attn_memory_weight': _L0_attn_in['memory_weight'], 'L0_xattn_Wq': _L0_xattn_in['Wq'], 'L0_xattn_bq': _L0_xattn_in['bq'], 'L0_xattn_Wk': _L0_xattn_in['Wk'], 'L0_xattn_bk': _L0_xattn_in['bk'], 'L0_xattn_Wv': _L0_xattn_in['Wv'], 'L0_xattn_bv': _L0_xattn_in['bv'], 'L0_xattn_Wo': _L0_xattn_in['Wo'], 'L0_xattn_bo': _L0_xattn_in['bo'], 'L0_ffn_rw1': _L0_ffn_in['rw1'], 'L0_ffn_rw2': _L0_ffn_in['rw2'], 'L0_ffn_w1': _L0_ffn_in['w1'], 'L0_ffn_b1': _L0_ffn_in['b1'], 'L0_ffn_w2': _L0_ffn_in['w2'], 'L0_ffn_b2': _L0_ffn_in['b2'], 'L1_attn_Wq': _L1_attn_in['Wq'], 'L1_attn_Wk': _L1_attn_in['Wk'], 'L1_attn_Wv': _L1_attn_in['Wv'], 'L1_attn_Wo': _L1_attn_in['Wo'], 'L1_attn_Wb': _L1_attn_in['Wb'], 'L1_xattn_Wq': _L1_xattn_in['Wq'], 'L1_xattn_bq': _L1_xattn_in['bq'], 'L1_xattn_Wk': _L1_xattn_in['Wk'], 'L1_xattn_bk': _L1_xattn_in['bk'], 'L1_xattn_Wv': _L1_xattn_in['Wv'], 'L1_xattn_bv': _L1_xattn_in['bv'], 'L1_xattn_Wo': _L1_xattn_in['Wo'], 'L1_xattn_bo': _L1_xattn_in['bo'], 'L1_xattn_ln_gamma': _L1_xattn_in['ln_gamma'], 'L1_xattn_ln_beta': _L1_xattn_in['ln_beta'], 'L1_xattn_residual_scale': _L1_xattn_in['residual_scale'], 'L1_ffn_gate_weight': _L1_ffn_in['gate_weight'], 'L1_ffn_inv_mapping': _L1_ffn_in['inv_mapping'], 'L1_ffn_mask_up_W': _L1_ffn_in['mask_up_W'], 'L1_ffn_gate_W': _L1_ffn_in['gate_W'], 'L1_ffn_gate_qa': _L1_ffn_in['gate_qa'], 'L1_ffn_gate_qb': _L1_ffn_in['gate_qb'], 'L1_ffn_gate_scale': _L1_ffn_in['gate_scale'], 'L1_ffn_up_W': _L1_ffn_in['up_W'], 'L1_ffn_up_qa': _L1_ffn_in['up_qa'], 'L1_ffn_up_qb': _L1_ffn_in['up_qb'], 'L1_ffn_up_scale': _L1_ffn_in['up_scale'], 'L1_ffn_down_W': _L1_ffn_in['down_W'], 'L1_ffn_down_qa': _L1_ffn_in['down_qa'], 'L1_ffn_down_qb': _L1_ffn_in['down_qb'], 'L1_ffn_down_scale': _L1_ffn_in['down_scale'], 'L1_ffn_sh_gate_W': _L1_ffn_in['sh_gate_W'], 'L1_ffn_sh_up_W': _L1_ffn_in['sh_up_W'], 'L1_ffn_sh_down_W': _L1_ffn_in['sh_down_W']}

def reference(x, ctx_2048, mask_BxS2_ik0, L0_attn_Wq, L0_attn_Wk, L0_attn_Wv, L0_attn_memory, L0_attn_memory_norm, L0_attn_memory_weight, L0_xattn_Wq, L0_xattn_bq, L0_xattn_Wk, L0_xattn_bk, L0_xattn_Wv, L0_xattn_bv, L0_xattn_Wo, L0_xattn_bo, L0_ffn_rw1, L0_ffn_rw2, L0_ffn_w1, L0_ffn_b1, L0_ffn_w2, L0_ffn_b2, L1_attn_Wq, L1_attn_Wk, L1_attn_Wv, L1_attn_Wo, L1_attn_Wb, L1_xattn_Wq, L1_xattn_bq, L1_xattn_Wk, L1_xattn_bk, L1_xattn_Wv, L1_xattn_bv, L1_xattn_Wo, L1_xattn_bo, L1_xattn_ln_gamma, L1_xattn_ln_beta, L1_xattn_residual_scale, L1_ffn_gate_weight, L1_ffn_inv_mapping, L1_ffn_mask_up_W, L1_ffn_gate_W, L1_ffn_gate_qa, L1_ffn_gate_qb, L1_ffn_gate_scale, L1_ffn_up_W, L1_ffn_up_qa, L1_ffn_up_qb, L1_ffn_up_scale, L1_ffn_down_W, L1_ffn_down_qa, L1_ffn_down_qb, L1_ffn_down_scale, L1_ffn_sh_gate_W, L1_ffn_sh_up_W, L1_ffn_sh_down_W):
    import jax
    import jax.numpy as jnp

    def _L0_attn_ref(x, Wq, Wk, Wv, memory, memory_norm, memory_weight):
        import jax, jax.numpy as jnp
        import numpy as np
        D_MODEL = 256
        N_QUERY = 4
        N_HEAD = 8
        D_HEAD = D_MODEL // (N_QUERY * N_HEAD)
        D_KV = D_HEAD * N_HEAD
        BATCH, SEQ = (2, 256)
        b, s, d = x.shape
        q = x @ Wq.T
        k = x @ Wk.T
        v = x @ Wv.T
        qh = q.reshape(b, s, N_QUERY, N_HEAD, D_HEAD)
        kh = k.reshape(b, s, N_HEAD, D_HEAD)
        vh = v.reshape(b, s, N_HEAD, D_HEAD)
        scale = np.float32(1.0 / np.sqrt(np.float32(D_HEAD)))
        scores = jnp.einsum('bsqhd,bthd->bqhst', qh, kh) * scale
        probs = jax.nn.softmax(scores, axis=-1)
        a_dot = jnp.einsum('bqhst,bthd->bsqhd', probs, vh)
        a_dot = a_dot.reshape(b, s, N_QUERY * N_HEAD, D_HEAD)
        sigma_q = jax.nn.elu(q.reshape(b, s, N_QUERY, D_KV))
        a_mem = sigma_q @ memory / (sigma_q @ memory_norm)
        a_mem = a_mem.reshape(b, s, N_QUERY * N_HEAD, D_HEAD)
        w = jax.nn.sigmoid(memory_weight)
        out = a_dot * (1.0 - w) + a_mem * w
        return out.reshape(b, s, D_MODEL)

    def _L0_xattn_ref(x, c, Wq, bq, Wk, bk, Wv, bv, Wo, bo):
        import math
        import jax, jax.numpy as jnp
        import numpy as np
        N_HEADS = 8
        CHANNELS = 64
        K_CH = CHANNELS // N_HEADS
        THETA = 10000.0

        def _rope_freqs(length, dim):
            inv_freq = 1.0 / THETA ** (jnp.arange(0, dim, 2, dtype=jnp.float32) / dim)
            f = jnp.arange(length, dtype=jnp.float32)[:, None] * inv_freq[None, :]
            return jnp.concatenate([f, f], axis=-1)

        def _apply_rotary(pos, t):
            half = t.shape[-1] // 2
            rot = jnp.concatenate([-t[..., half:], t[..., :half]], axis=-1)
            return t * jnp.cos(pos) + rot * jnp.sin(pos)

        def _proj(inp, W, b):
            return jnp.einsum('oc,bct->bot', W, inp) + b[None, :, None]
        b, _, t_t = x.shape
        t_s = c.shape[2]
        q_emb = _rope_freqs(t_t, K_CH)
        k_emb = _rope_freqs(t_s, K_CH)

        def split_heads(t):
            return t.reshape(b, N_HEADS, K_CH, t.shape[2]).transpose(0, 1, 3, 2)
        q = split_heads(_proj(x, Wq, bq))
        k = split_heads(_proj(c, Wk, bk))
        v = split_heads(_proj(c, Wv, bv))
        q = _apply_rotary(q_emb, q)
        k = _apply_rotary(k_emb, k)
        scores = jnp.einsum('bhtc,bhsc->bhts', q, k) / math.sqrt(K_CH)
        p_attn = jax.nn.softmax(scores, axis=-1)
        out = jnp.einsum('bhts,bhsc->bhtc', p_attn, v)
        out = out.transpose(0, 1, 3, 2).reshape(b, N_HEADS * K_CH, t_t)
        return _proj(out, Wo, bo)

    def _L0_ffn_ref(x, rw1, rw2, w1, b1, w2, b2):
        import jax, jax.numpy as jnp
        import numpy as np
        TOP_K = 2

        def _gelu(v):
            return jax.nn.gelu(v, approximate=False)
        logits = _gelu(x @ rw1) @ rw2
        probs = jax.nn.softmax(logits, axis=-1)
        wgt, idx = jax.lax.top_k(probs, TOP_K)
        E = w1.shape[0]
        out = jnp.zeros_like(x)
        for e in range(E):
            Ye = _gelu(x @ w1[e] + b1[e]) @ w2[e] + b2[e]
            Ce = _gelu(b1[e]) @ w2[e] + b2[e]
            for k in range(TOP_K):
                mask = idx[..., k] == e
                active = jnp.any(mask).astype(x.dtype)
                term = jnp.where(mask[..., None], Ye, Ce)
                out = out + active * wgt[..., k:k + 1] * term
        return out

    def _L1_attn_ref(x, Wq, Wk, Wv, Wo, Wb):
        import jax, jax.numpy as jnp
        import numpy as np
        B, N, D, H = (2, 256, 256, 16)
        HD = D // H
        CHUNK = 64
        BASE = 10000.0

        def _l2norm(x, eps=1e-06):
            return x * jax.lax.rsqrt(jnp.sum(x * x, axis=-1, keepdims=True) + eps)

        def _rope(x):
            n, d = (x.shape[1], x.shape[-1])
            inv = 1.0 / BASE ** (jnp.arange(0, d, 2, dtype=jnp.float32) / d)
            th = jnp.arange(n, dtype=jnp.float32)[:, None] * inv
            cos = jnp.cos(th)[None, :, None, :]
            sin = jnp.sin(th)[None, :, None, :]
            x1, x2 = jnp.split(x, 2, axis=-1)
            return jnp.concatenate([x1 * cos - x2 * sin, x1 * sin + x2 * cos], axis=-1)

        def _kernel_regression(k, v, beta):
            b, n, h, dk = k.shape
            dv = v.shape[-1]
            nc = n // CHUNK
            Kc = k.reshape(b, nc, CHUNK, h, dk).transpose(1, 0, 3, 2, 4)
            Vc = v.reshape(b, nc, CHUNK, h, dv).transpose(1, 0, 3, 2, 4)
            Bc = beta.reshape(b, nc, CHUNK, h).transpose(1, 0, 3, 2)
            eye = jnp.eye(CHUNK, dtype=k.dtype)

            def step(S, inp):
                K, V, bt = inp
                A = jnp.tril(jnp.einsum('bhik,bhjk->bhij', K, K) * bt[:, :, None, :], -1)
                rhs = V - jnp.einsum('bhck,bhkv->bhcv', K, S)
                Vn = jax.scipy.linalg.solve_triangular(eye + A, rhs, lower=True)
                S = S + jnp.einsum('bhck,bhcv->bhkv', K * bt[..., None], Vn)
                return (S, Vn)
            S0 = jnp.zeros((b, h, dk, dv), k.dtype)
            S, Vn = jax.lax.scan(step, S0, (Kc, Vc, Bc))
            v_new = Vn.transpose(1, 0, 3, 2, 4).reshape(b, n, h, dv)
            return (v_new, S)
        b, n, d = x.shape
        q = (x @ Wq).reshape(b, n, H, HD)
        k = _l2norm((x @ Wk).reshape(b, n, H, HD))
        v = (x @ Wv).reshape(b, n, H, HD)
        beta = 2.0 * jax.nn.sigmoid(x @ Wb)
        q = _rope(q)
        k = _rope(k)
        v, _state = _kernel_regression(k, v, beta)
        k = k * beta[..., None]
        scale = HD ** (-0.5)
        scores = jnp.einsum('bqhd,bkhd->bhqk', q, k) * scale
        mask = jnp.tril(jnp.ones((n, n), bool))
        scores = jnp.where(mask, scores, -jnp.inf)
        attn = jax.nn.softmax(scores, axis=-1)
        out = jnp.einsum('bhqk,bkhd->bqhd', attn, v).reshape(b, n, d)
        return out @ Wo

    def _L1_xattn_ref(hidden_states, audio_tokens, attention_mask, Wq, bq, Wk, bk, Wv, bv, Wo, bo, ln_gamma, ln_beta, residual_scale):
        import jax, jax.numpy as jnp
        import numpy as np
        import math
        H = 256
        NH = 16
        HD = H // NH
        EPS_LN = 1e-05
        RES_SCALE_MAX = 0.3

        def _nan_clean(x, lim=10000.0):
            return jnp.nan_to_num(x, nan=0.0, posinf=lim, neginf=-lim)
        B, S, _ = hidden_states.shape
        T = audio_tokens.shape[1]
        hs = _nan_clean(hidden_states).astype(jnp.float32)
        at = _nan_clean(audio_tokens).astype(jnp.float32)

        def proj(x, W, b, L):
            y = x @ W.T + b
            return y.reshape(B, L, NH, HD).transpose(0, 2, 1, 3)
        q = _nan_clean(proj(hs, Wq, bq, S))
        k = _nan_clean(proj(at, Wk, bk, T))
        v = _nan_clean(proj(at, Wv, bv, T))
        scale = max(math.sqrt(HD), 1e-08)
        scores = jnp.einsum('bhsd,bhtd->bhst', q, k) / scale
        scores = jnp.clip(scores, -50.0, 50.0)
        scores = jnp.nan_to_num(scores, nan=0.0, posinf=50.0, neginf=-50.0)
        attend = (attention_mask.astype(jnp.float32) > 0.5)[:, None, None, :]
        scores = jnp.where(attend, scores, -10000.0)
        scores = jnp.clip(scores, -50.0, 50.0)
        probs = jax.nn.softmax(scores, axis=-1)
        probs = jnp.nan_to_num(probs, nan=0.0, posinf=1.0, neginf=0.0)
        probs = probs / (probs.sum(axis=-1, keepdims=True) + 1e-08)
        ctx = jnp.einsum('bhst,bhtd->bhsd', probs, v)
        ctx = ctx.transpose(0, 2, 1, 3).reshape(B, S, H)
        delta = _nan_clean(ctx @ Wo.T + bo)
        rs = jnp.clip(residual_scale, 0.0, RES_SCALE_MAX)
        delta = rs * delta
        mu = delta.mean(axis=-1, keepdims=True)
        var = jnp.mean((delta - mu) ** 2, axis=-1, keepdims=True)
        delta = (delta - mu) / jnp.sqrt(var + EPS_LN) * ln_gamma + ln_beta
        return delta

    def _L1_ffn_ref(hidden_states, gate_weight, inv_mapping, mask_up_W, gate_W, gate_qa, gate_qb, gate_scale, up_W, up_qa, up_qb, up_scale, down_W, down_qa, down_qb, down_scale, sh_gate_W, sh_up_W, sh_down_W):
        import jax, jax.numpy as jnp
        import numpy as np
        B, S, H, I, E, F, K, R, TOPK = (1, 128, 256, 176, 64, 8, 8, 8, 6)
        ISH = 2 * I

        def _fused_linear(x, W, qa, qb, scale, w):
            out = x @ W.T
            a = jnp.einsum('th,krh->tkr', x, qa)
            b = jnp.einsum('tkr,khr->tkh', a, qb)
            mix = jnp.einsum('tkh,tk->th', b, w)
            return out + scale[None, :] * mix

        def _moe_forward(hidden_states, gate_weight, inv_mapping, mask_up_W, gate_W, gate_qa, gate_qb, gate_scale, up_W, up_qa, up_qb, up_scale, down_W, down_qa, down_qb, down_scale, sh_gate_W, sh_up_W, sh_down_W):
            b, s, h = hidden_states.shape
            x = hidden_states.reshape(-1, h)
            T = x.shape[0]
            scores = jax.nn.softmax(x @ gate_weight.T, axis=-1)
            topk_w, topk_idx = jax.lax.top_k(scores, TOPK)
            w_dense = jnp.zeros((T, E), x.dtype).at[jnp.arange(T)[:, None], topk_idx].add(topk_w)
            flat = w_dense[:, inv_mapping]
            scalar = flat.sum(-1)
            soft = jax.nn.softmax(jnp.where(flat == 0, -1000000000.0, flat), axis=-1)

            def expert(muW, gW, gqa, gqb, gs, uW, uqa, uqb, us, dW, dqa, dqb, ds, w):
                xe = x + w @ muW.T
                gate = jax.nn.silu(_fused_linear(xe, gW, gqa, gqb, gs, w))
                up = _fused_linear(xe, uW, uqa, uqb, us, w)
                return _fused_linear(gate * up, dW, dqa, dqb, ds, w)
            outs = jax.vmap(expert, in_axes=(0,) * 13 + (1,))(mask_up_W, gate_W, gate_qa, gate_qb, gate_scale, up_W, up_qa, up_qb, up_scale, down_W, down_qa, down_qb, down_scale, soft)
            y = jnp.einsum('fth,tf->th', outs, scalar).reshape(b, s, h)
            sh = jax.nn.silu(hidden_states @ sh_gate_W.T) * (hidden_states @ sh_up_W.T) @ sh_down_W.T
            return y + sh
        return _moe_forward(hidden_states, gate_weight, inv_mapping, mask_up_W, gate_W, gate_qa, gate_qb, gate_scale, up_W, up_qa, up_qb, up_scale, down_W, down_qa, down_qb, down_scale, sh_gate_W, sh_up_W, sh_down_W)
    x = _layernorm(x + _L0_attn_ref(x, L0_attn_Wq, L0_attn_Wk, L0_attn_Wv, L0_attn_memory, L0_attn_memory_norm, L0_attn_memory_weight), axis=-1)
    x = _layernorm(x + _L0_xattn_ref(x, ctx_2048, L0_xattn_Wq, L0_xattn_bq, L0_xattn_Wk, L0_xattn_bk, L0_xattn_Wv, L0_xattn_bv, L0_xattn_Wo, L0_xattn_bo), axis=-1)
    x = _layernorm(x + _L0_ffn_ref(x, L0_ffn_rw1, L0_ffn_rw2, L0_ffn_w1, L0_ffn_b1, L0_ffn_w2, L0_ffn_b2), axis=-1)
    x = _layernorm(x + _L1_attn_ref(x, L1_attn_Wq, L1_attn_Wk, L1_attn_Wv, L1_attn_Wo, L1_attn_Wb), axis=-1)
    x = _layernorm(x + _L1_xattn_ref(x, ctx_2048, mask_BxS2_ik0, L1_xattn_Wq, L1_xattn_bq, L1_xattn_Wk, L1_xattn_bk, L1_xattn_Wv, L1_xattn_bv, L1_xattn_Wo, L1_xattn_bo, L1_xattn_ln_gamma, L1_xattn_ln_beta, L1_xattn_residual_scale), axis=-1)
    x = _layernorm(x + _L1_ffn_ref(x, L1_ffn_gate_weight, L1_ffn_inv_mapping, L1_ffn_mask_up_W, L1_ffn_gate_W, L1_ffn_gate_qa, L1_ffn_gate_qb, L1_ffn_gate_scale, L1_ffn_up_W, L1_ffn_up_qa, L1_ffn_up_qb, L1_ffn_up_scale, L1_ffn_down_W, L1_ffn_down_qa, L1_ffn_down_qb, L1_ffn_down_scale, L1_ffn_sh_gate_W, L1_ffn_sh_up_W, L1_ffn_sh_down_W), axis=-1)
    return x

_drawn_inputs = setup_inputs


def setup_inputs(seed=0):
    import zlib

    import numpy as np

    out = dict(_drawn_inputs(seed))
    spreads = {'L0_attn_memory_norm': (1.0, 0.2),
     'L0_xattn_bq': (0.0, 0.555),
     'L0_xattn_bk': (0.0, 0.8),
     'L0_xattn_bv': (0.0, 0.8),
     'L0_xattn_bo': (0.0, 0.8),
     'L1_xattn_bq': (0.0, 0.1),
     'L1_xattn_bk': (0.0, 0.8),
     'L1_xattn_bv': (0.0, 0.1),
     'L1_xattn_bo': (0.0, 0.1),
     'L1_xattn_ln_gamma': (1.0, 0.2),
     'L1_xattn_ln_beta': (0.0, 0.1),
     'L1_ffn_gate_scale': (0.10000000149011612, 0.6),
     'L1_ffn_up_scale': (0.10000000149011612, 0.6),
     'L1_ffn_down_scale': (0.10000000149011612, 0.6)}
    factors = {'L0_ffn_rw1': 4.311,
     'L0_ffn_rw2': 4.228,
     'L0_ffn_w1': 3.744,
     'L0_ffn_b1': 8.0,
     'L0_ffn_w2': 3.536,
     'L0_ffn_b2': 5.117,
     'L1_attn_Wq': 8.0,
     'L1_attn_Wk': 5.458,
     'L1_attn_Wb': 8.0,
     'L1_ffn_gate_weight': 8.0,
     'L1_ffn_mask_up_W': 8.0,
     'L1_ffn_gate_W': 8.0,
     'L1_ffn_gate_qa': 8.0,
     'L1_ffn_gate_qb': 8.0,
     'L1_ffn_up_W': 8.0,
     'L1_ffn_up_qa': 8.0,
     'L1_ffn_up_qb': 8.0,
     'L1_ffn_down_W': 8.0,
     'L1_ffn_down_qa': 8.0,
     'L1_ffn_down_qb': 8.0,
     'L1_ffn_sh_gate_W': 2.899,
     'L1_ffn_sh_up_W': 2.858,
     'L1_ffn_sh_down_W': 2.84}
    for name, (base, spread) in spreads.items():
        noise = np.random.default_rng([zlib.crc32(name.encode()), seed]).standard_normal(out[name].shape)
        drawn = base * np.exp(spread * noise) if base else spread * noise
        out[name] = jnp.asarray(drawn.astype(out[name].dtype))
    for name, factor in factors.items():
        out[name] = (out[name] * factor).astype(out[name].dtype)
    return out
```

```python
from contextlib import ExitStack

import numpy as np

import concourse.bass as bass
from concourse import mybir

F32 = mybir.dt.float32
F16 = mybir.dt.float16
BF16 = mybir.dt.bfloat16
I32 = mybir.dt.int32
ALU = mybir.AluOpType
ACT = mybir.ActivationFunctionType
AX = mybir.AxisListType

P = 128
B, S, D = 16, 64, 256
NT = B * S // P
KC = D // P
XT_AFTER = (0, 2, 3, 4, 5)
BANK = 512
EPS = 1e-5

NQ, H0, DH0, DKV = 4, 8, 8, 64
HX, DHX = 8, 8
E0, I0 = 8, 1024
IC0 = I0 // P
ROW_TILES = 2 * NT + E0 - 1
B1_ROWS = 64 + E0
H1, DH1 = 16, 16
E1, FX, KX, RX, I1, TOP1 = 64, 8, 8, 8, 176, 6
IH = I1 // 2
ISH = 2 * I1

PACKS = {
    "consts": [("ident", P, (P,)), ("ones", P, (P,)), ("headmask0", 72, (H0,)), ("headmask1", P, (8,)),
               ("cosx", P, (D,)), ("sinx", P, (D,)), ("rotx", P, (P,)), ("rep", P, (2, P)),
               ("lo_q", P, (1,)), ("lo_k", P, (1,)), ("selmax", P, (HX, P)),
               ("cos1", P, (DH1,)), ("sin1", P, (DH1,)), ("causal", P, (S,)),
               ("reset8", P, (NT * E0,)), ("reset64", P, (NT * E1,)), ("row", P, (1,)),
               ("b1_rows", P, (E0,)), ("before", P, (P,)), ("full_tiles", P, (NT,)), ("tile_no", P, (ROW_TILES,)),
               ("spread", E1, (FX, P))],
    "w_attn0": [("wq", P, (KC, D)), ("wk", P, (KC, DKV)), ("wv", P, (KC, DKV)), ("mem", DKV, (DKV + 1,)),
                ("memw", P, (1,))],
    "w_xattn0": [("wq", P, (P,)), ("wk", P, (P,)), ("wv", P, (S,)), ("wo", S, (S,)), ("bq", P, (1,)),
                 ("bk", P, (1,)), ("bo", P, (1,)), ("bv", P, (S,))],
    "w_route0": [("rw1", P, (KC, P)), ("rw2", P, (E0,)), ("b1", P, (E0, IC0))],
    "w_attn1": [("wqk", P, (KC, 2 * D)), ("wvb", P, (KC, D + H1)), ("wo", P, (KC, D))],
    "w_xattn1": [("wq", P, (KC, D)), ("wk", P, (KC, D)), ("wv", P, (KC, D)), ("wo", P, (KC, D)),
                 ("bq", P, (KC,)), ("bk", P, (KC,)), ("bv", P, (D,)), ("bo", P, (D,)),
                 ("gamma", P, (D,)), ("beta", P, (D,)), ("scale", P, (1,))],
    "w_ffn1": [("gate", P, (KC, E1)), ("mask_up", E1, (FX, D)),
               ("shg", P, (KC, ISH)), ("shu", P, (KC, ISH)), ("shd", IH, (4, D))],
}
EXPERT = [("gw", P, (KC, I1)), ("uw", P, (KC, I1)), ("qa", P, (KC, P)), ("qb", P, (I1,)), ("qs", P, (I1,)),
          ("dw", IH, (2, D)), ("dqa", IH, (2, KX * RX)), ("dqb", KX * RX, (D,)), ("ds", P, (D,))]


def columns(parts):
    return sum(int(np.prod(shape)) for _, _, shape in parts)


def views(ap, parts):
    out, at = {}, 0
    for name, rows, shape in parts:
        n = int(np.prod(shape))
        v = ap[0:rows, at:at + n]
        if len(shape) == 2:
            v = v.rearrange("p (a b) -> p a b", b=shape[1])
        out[name] = v
        at += n
    return out


class Signal:

    def __init__(self, sem, base=0, before=None):
        self.sem, self.n, self.base, self.before = sem, base, base, before

    def by(self, instruction):
        instruction.then_inc(self.sem, 1)
        self.n += 1
        return self.n


class Arena:

    def __init__(self, tensor, size):
        self.t, self.size, self.at = tensor, size, 0

    def take(self, *shape, dtype=F32):
        n = int(np.prod(shape))
        words = n if dtype in (F32, I32, mybir.dt.uint32) else (n + 1) // 2
        words += words % 2
        assert self.at + words <= self.size, (self.at, words)
        v = self.t[:, self.at:self.at + words]
        if dtype != F32:
            v = v.bitcast(dtype)
        v = v[:, 0:n]
        self.at += words
        if len(shape) == 2:
            v = v.rearrange("p (a b) -> p a b", b=shape[1])
        elif len(shape) == 3:
            v = v.rearrange("p (a b c) -> p a b c", b=shape[1], c=shape[2])
        elif len(shape) == 4:
            v = v.rearrange("p (a b c d) -> p a b c d", b=shape[1], c=shape[2], d=shape[3])
        return v


def wide(ap, axis, n):
    v = ap.unsqueeze(axis)
    shape = list(v.shape)
    shape[axis] = n
    return v.to_broadcast(shape)


def build(nc, a):
    ctx = ExitStack()
    with ctx:
        def signal(name):
            return Signal(ctx.enter_context(nc.semaphore(name)))

        renamed = []

        def again(name, old, total):
            renamed.append((name, Signal(old.sem, total, old)))
            return renamed[-1][1]

        ARENA = 48000
        arena = Arena(ctx.enter_context(nc.sbuf_tensor("arena", [P, ARENA], F32)), ARENA)
        psum = ctx.enter_context(nc.psum_tensor("psum", [P, 8 * BANK], F32))

        def bank(i, n=1):
            return psum[:, i * BANK:(i + n) * BANK]

        x = arena.take(NT, D)
        xt = arena.take(KC, B * S)
        con = arena.take(columns(PACKS["consts"]))
        c = views(con, PACKS["consts"])
        ctok = arena.take(NT, D)
        mean_var = arena.take(NT, 2)
        stats = arena.take(NT, 6)
        rstd = arena.take(NT)
        std = arena.take(NT)
        blank = arena.take(D)
        keep = arena.at

        loaded = {n: signal(f"loaded_{n}") for n in list(PACKS) + ["x", "ctx"]}
        dve_step, act_step, pool_step = signal("dve_step"), signal("act_step"), signal("pool_step")
        xt_ps, xt_sb = signal("xt_ps"), signal("xt_sb")
        x_norm, ln_var, ln_std = signal("x_norm"), signal("ln_var"), signal("ln_std")
        out_done = signal("out_done")

        arena.at = keep
        w_a0 = arena.take(columns(PACKS["w_attn0"]))
        a0 = views(w_a0, PACKS["w_attn0"])
        q4 = arena.take(B, NQ, S)
        sig = arena.take(NQ, B * S)
        kt0 = arena.take(B * S)
        kb0 = arena.take(B, H0, S)
        vb0 = arena.take(B, 4, 2 * (DH0 + 1))
        am = arena.take(NT, D)
        pt0 = arena.take(2, 4, D)
        nm0 = arena.take(2, 2, H0)
        rs0 = arena.take(NQ * H0)
        rm0 = arena.take(NQ)
        t0 = arena.take(NQ * H0, DH0)
        gate0 = arena.take(4)
        q_ps, q_sb, v_ps, v_sb, kb_ready = (signal(n) for n in ("q_ps", "q_sb", "v_ps", "v_sb", "kb_ready"))
        elu_min, elu_exp, elu_ready = signal("elu_min"), signal("elu_exp"), signal("elu_ready")
        gate_exp, mem_ps, mem_read = signal("gate_exp"), signal("mem_ps"), signal("mem_read")
        a0_ps, a0_max, nmt0_ps, nmt0_sb = (signal(n) for n in ("a0_ps", "a0_max", "nmt0_ps", "nmt0_sb"))
        b0_ps, pt0_ready, o0_ps, o0_read = (signal(n) for n in ("b0_ps", "pt0_ready", "o0_ps", "o0_read"))

        arena.at = keep
        w_x0 = arena.take(columns(PACKS["w_xattn0"]))
        x0 = views(w_x0, PACKS["w_xattn0"])
        qs = arena.take(2, D)
        rope_a, rope_b = arena.take(2, D), arena.take(2, D)
        qr = arena.take(2, D)
        hi16 = arena.take(2, 2, 2 * D, dtype=F16)
        stack = {n: arena.take(B, 2, D, dtype=F16) for n in "kq"}
        vx = arena.take(B, 2, HX, DHX + 1)
        selm = arena.take(HX, P, dtype=BF16)
        nmx = arena.take(2, 2, HX)
        nmxb = arena.take(2, 2, HX, dtype=BF16)
        nmtx = arena.take(2, D, dtype=BF16)
        ptx = arena.take(2, 2, D)
        rsx = arena.take(2, 2, HX)
        onx = arena.take(2, 2, S)
        otx = arena.take(2, D)
        ident16 = arena.take(P, dtype=BF16)
        pj_ps, pj_sb, rot_ps, qr_ready, rep_ps, hi_ready, st_ready = (
            signal(n) for n in ("pj_ps", "pj_sb", "rot_ps", "qr_ready", "rep_ps", "hi_ready", "st_ready"))
        vx_ps, vx_sb, selm_ready = signal("vx_ps"), signal("vx_sb"), signal("selm_ready")
        ax_ps, ax_max, nmx_ready, nmtx_ps, nmtx_sb = (
            signal(n) for n in ("ax_ps", "ax_max", "nmx_ready", "nmtx_ps", "nmtx_sb"))
        bx_ps, ptx_ready, ox_ps, pvx_done, onx_ready, otx_ps, otx_sb, yx_ps, yx_read = (
            signal(n) for n in ("bx_ps", "ptx_ready", "ox_ps", "pvx_done", "onx_ready", "otx_ps", "otx_sb", "yx_ps",
                                "yx_read"))
        arena.at = keep
        w_r0 = arena.take(columns(PACKS["w_route0"]))
        r0 = views(w_r0, PACKS["w_route0"])
        r1 = arena.take(B * S)
        prob = arena.take(NT, E0)
        pmax = arena.take(NT)
        top8 = arena.take(NT, 8)
        first = arena.take(NT * E0)
        both = arena.take(NT * E0)
        tie = arena.take(NT * E0)
        rank = arena.take(NT * E0)
        more = arena.take(NT)
        marks = arena.take(NT, 2 * E0)
        earlier = arena.take(NT, E0)
        active = arena.take(2 * E0)
        gates = arena.take(NT, E0)
        weight_c = arena.take(NT, 2 * E0)
        slot_a = arena.take(NT, E0)
        b1g = arena.take(E0, IC0)
        level0 = arena.take(NT, E0)
        count0 = arena.take(E0)
        over0 = arena.take(E0, NT)
        tiles0 = arena.take(E0)
        end0 = arena.take(E0)
        row0 = arena.take(E0)
        place = arena.take(NT, E0)
        placed = arena.take(NT, 2 * E0)
        slot_row = arena.take(NT * 2)
        slot_row_i = arena.take(NT * 2, dtype=mybir.dt.uint32)
        past = arena.take(ROW_TILES, E0 - 1)
        tile_e = arena.take(ROW_TILES)
        tile_e_i = arena.take(ROW_TILES, dtype=I32)
        cet = arena.take(KC * E0)
        ceb = arena.take(D)
        xs = arena.take(2, D)
        xst = arena.take(2, KC, P)
        ys = arena.take(2, D)
        wct = r1
        assert arena.at <= ARENA - E0 * 2 * KC * I0
        arena.at = ARENA - E0 * 2 * KC * I0
        w12 = arena.take(E0, 2 * KC * I0)
        w1v = w12[:, :, 0:KC * I0].rearrange("p e (k i) -> p e k i", k=KC)
        w2v = w12[:, :, KC * I0:2 * KC * I0].rearrange("p e (c d) -> p e c d", c=IC0)
        back = w12[:, 0, :].rearrange("p (n d) -> p n d", d=D)
        hid = xt.rearrange("p k (r n) -> p (k r) n", n=I0)
        hidt = ctok.rearrange("p (r c) d -> p r (c d)", r=2)
        b1_row, b1_rest = hidt[0:B1_ROWS, 0, :], hidt[0:B1_ROWS, 1, :]
        sel_cols = c["selmax"].rearrange("p a b -> p (a b)")
        b1_terms = sel_cols[0:B1_ROWS, 0:I0 // 2].bitcast(BF16)
        b1_pick = sel_cols[0:B1_ROWS, I0 // 2:I0 // 2 + E0 * P // 2].bitcast(BF16)\
            .rearrange("p (e t) -> p e t", e=E0)
        w12_in = signal("w12_in")
        b1_in, b2_in = signal("b1_in"), signal("b2_in")
        blank_rows = signal("blank_rows")
        r1_ps, r1_sb, lg_ps, p_exp, p_sub = (
            signal(n) for n in ("r1_ps", "r1_sb", "lg_ps", "p_exp", "p_sub"))
        marks_ready, cnt_ps, wc_ready, wct_ps, wct_sb = (
            signal(n) for n in ("marks_ready", "cnt_ps", "wc_ready", "wct_ps", "wct_sb"))
        b1_gelu, ce_ps, cet_sb, cer_ps, ceb_sb, const_ps, const_read = (
            signal(n) for n in ("b1_gelu", "ce_ps", "cet_sb", "cer_ps", "ceb_sb", "const_ps", "const_read"))
        place_ready = again("place_ready", q_ps, 6)
        tiles_ready = again("tiles_ready", q_sb, 6)
        sorted_out = signal("sorted_out")
        xs_in = [again("xs_in_even", a0_max, 2 * B), signal("xs_in_odd")]
        xst_ps = again("xst_ps", mem_ps, NT)
        xst_sb = again("xst_sb", nmt0_ps, B)
        up_ps = again("up_ps", nmt0_sb, B)
        hid_ready = again("hid_ready", b0_ps, B)
        hidt_ps = again("hidt_ps", pt0_ready, B)
        hidt_sb = again("hidt_sb", o0_ps, B)
        down_ps = again("down_ps", a0_ps, 2 * B)
        ys_ready = signal("ys_ready")
        ys_out = [again("ys_out_even", kb_ready, NT), signal("ys_out_odd")]
        back_in = signal("back_in")
        b1_ready = again("b1_ready", gate_exp, 1)
        arena.at = keep
        w_a1 = arena.take(columns(PACKS["w_attn1"]))
        a1 = views(w_a1, PACKS["w_attn1"])
        qk1 = arena.take(NT, 2 * D)
        vz1 = arena.take(NT, D + H1)
        sq1 = arena.take(2, D)
        rk1 = arena.take(NT, H1)
        std1 = arena.take(NT, H1)
        beta1 = arena.take(NT, H1)
        turn_a, turn_b = arena.take(2 * D), arena.take(2 * D)
        rq1 = arena.take(2, 2 * D)
        kw1 = arena.take(2, D)
        ft1 = arena.take(4, KC, B * S)
        spread1 = arena.take(B * 8 * 34)
        kb1 = spread1[:, 0:4 * KC * 8 * S].rearrange("p (b k h t) -> p b k h t", b=4, k=KC, h=8)
        part1 = lambda v: v.rearrange("p (g c i) -> p g c i", g=2, i=S)
        flat_qk1 = qk1.rearrange("p a b -> p (a b)")
        bh1 = [part1(v) for v in (ft1[:, 2, :, :].rearrange("p k n -> p (k n)"), flat_qk1[:, KC * B * S:],
                                  ft1[:, 3, :, :].rearrange("p k n -> p (k n)"))]
        vn1 = part1(vz1.rearrange("p a b -> p (a b)")[:, 0:2 * DH1 * S])
        state1, outer1 = arena.take(2, DH1, DH1), arena.take(2, DH1, DH1)
        seen1 = arena.take(2, DH1)
        sm1 = arena.take(2, 2 * D)
        mx1 = arena.take(2, 8)
        pt1 = arena.take(2 * NT, 2 * D)
        vnt1 = flat_qk1[:, 0:KC * B * S].rearrange("p (k n) -> p k n", k=KC)
        vb1 = spread1.rearrange("p (b q c) -> p b q c", b=B, q=8)
        on1 = arena.take(2, D)
        ot1 = arena.take(2, KC, P)
        rs1 = arena.take(2, H1)
        (pj1_ps, pj1_sb, ss_part, ss_ready, ss_std, bz_exp, turned1, tr1_ps, ft_sb, turned_out, bh_in, kb1_ready, a1_ps,
         sm_ready, sm_exp, pt_ps, pt_sb, regressed, solved_out, vnt_in, vb1_ps, vb1_sb, o1_ps, on1_ready, ot1_ps,
         ot1_sb, y1_ps, y1_read, blank1) = (signal(n) for n in (
             "pj1_ps", "pj1_sb", "ss_part", "ss_ready", "ss_std", "bz_exp", "turned1", "tr1_ps", "ft_sb", "turned_out",
             "bh_in", "kb1_ready", "a1_ps", "sm_ready", "sm_exp", "pt_ps", "pt_sb", "regressed", "solved_out", "vnt_in",
             "vb1_ps", "vb1_sb", "o1_ps", "on1_ready", "ot1_ps", "ot1_sb", "y1_ps", "y1_read", "blank1"))
        turned_v = a["turned"].rearrange("n c (b i) -> n b c i", i=S)
        solved_v = a["solved"].rearrange("c (b i) -> b c i", i=S)
        arena.at = keep
        w_x1 = arena.take(columns(PACKS["w_xattn1"]))
        x1 = views(w_x1, PACKS["w_xattn1"])
        ct5 = arena.take(KC, B * S)
        k5, q5 = arena.take(KC, B * S), arena.take(KC, B * S)
        kb5 = arena.take(4 * KC, 8, S)
        vb5 = arena.take(B, 8, 34)
        s5, pt5 = arena.take(2, 2 * D), arena.take(2, 2 * D)
        mask5 = arena.take(B, dtype=I32)
        attend5, off5 = arena.take(B), arena.take(B)
        on5, ot5 = arena.take(2, D), arena.take(2, KC, P)
        rs5 = arena.take(2, H1)
        delta5 = arena.take(NT, D)
        scale5 = arena.take(2)
        (mask_in, ct_ps, ct_sb, kq5_ps, kq5_sb, v5_ps, v5_sb, blank5, kb5_ready, b5_ps, s5_ready, pt5_ready, o5_ps,
         on5_ready, ot5_ps, ot5_sb, y5_ps, y5_read) = (signal(n) for n in (
             "mask_in", "ct_ps", "ct_sb", "kq5_ps", "kq5_sb", "v5_ps", "v5_sb", "blank5", "kb5_ready", "b5_ps",
             "s5_ready", "pt5_ready", "o5_ps", "on5_ready", "ot5_ps", "ot5_sb", "y5_ps", "y5_read"))
        arena.at = keep
        w_f1 = arena.take(columns(PACKS["w_ffn1"]))
        f1 = views(w_f1, PACKS["w_ffn1"])
        w_e = arena.take(2, columns(EXPERT))
        ex = [views(w_e[:, i, :], EXPERT) for i in range(2)]
        prob6, mark6 = arena.take(NT, E1), arena.take(NT * E1)
        tie6, rank6 = arena.take(NT * E1), arena.take(NT * E1)
        peak6, more6 = arena.take(NT * FX), arena.take(NT)
        top6 = arena.take(NT, 8)
        map_i, map_f = arena.take(FX * KX, dtype=I32), arena.take(FX * KX)
        wd6 = arena.take(B * S)
        flat6 = arena.take(NT * FX, KX)
        mix6 = arena.take(NT * FX, KX)
        total6 = arena.take(NT * FX)
        wt6 = arena.take(B * S)
        xe6 = arena.take(2, KC, BANK)
        we6 = arena.take(3, BANK)
        aw6 = arena.take(2, BANK)
        adw6 = arena.take(BANK)
        g6, h6 = arena.take(4, BANK), arena.take(4, BANK)
        qb6 = arena.take(2, I1)
        dqb6 = arena.take(2, D)
        hs6 = arena.take(4, BANK)
        experts_in = [signal("experts_in_even"), signal("experts_in_odd")]
        map_in = signal("map_in")
        lg6_ps = again("lg6_ps", pj_ps, 2 * NT)
        wd6_ps = again("wd6_ps", rot_ps, 2 * NT)
        flat6_ps = again("flat6_ps", rep_ps, 2 * B)
        wt6_ps = again("wt6_ps", vx_ps, B)
        sh_ps = again("sh_ps", ax_ps, B * HX)
        sho_ps = again("sho_ps", nmtx_ps, B)
        mid_ps = again("mid_ps", bx_ps, B * HX)
        out6_ps = again("out6_ps", pvx_done, B * HX)
        p6_sub = again("p6_sub", qr_ready, 2 * NT)
        wd6_ready = again("wd6_ready", st_ready, 2 * B)
        sel6_ready = again("sel6_ready", vx_sb, B)
        m6_sub = again("m6_sub", ax_max, B * HX)
        mix6_ready = again("mix6_ready", nmx_ready, B)
        sh_h = again("sh_h", onx_ready, B)
        sho_read = again("sho_read", yx_read, B)
        mid_dve = again("mid_dve", v_sb, 2)
        qb6_ready = again("qb6_ready", mem_read, NT)
        out6_read = again("out6_read", elu_min, 1)
        p6_exp = again("p6_exp", pj_sb, 2 * NT)
        wd6_sb = again("wd6_sb", hi_ready, 2 * B)
        m6_exp = again("m6_exp", nmtx_sb, B)
        wt6_sb = again("wt6_sb", ptx_ready, B * HX)
        sh_silu = again("sh_silu", otx_sb, B)
        mid_act = again("mid_act", elu_exp, 1)

        STEPS = 2 * FX
        ring, by_dve, by_act = {}, {}, {}
        for step in range(-1, STEPS + 1):
            for kind, n, engine in ((("x", 0), step + 1, "D"), (("x", 1), step + 1, "D"), (("w", 0), step + 1, "A"),
                                    (("d", 0), step - 1, "D"), (("a", 0), step + 1, "D"), (("g", 0), step, "A"),
                                    (("g", 1), step, "A"), (("u", 0), step, "D"), (("u", 1), step, "D")):
                if 0 <= n < STEPS:
                    ring[kind, n] = len(ring)
                    (by_dve if engine == "D" else by_act)[kind, n] = len(by_dve if engine == "D" else by_act)
        order = list(ring)

        def bank_free(pe, key):
            if ring[key] >= 4:
                before = order[ring[key] - 4]
                if before in by_dve:
                    pe.wait_ge(mid_dve.sem, mid_dve.base + by_dve[before] + 1)
                else:
                    pe.wait_ge(mid_act.sem, mid_act.base + by_act[before] + 1)

        def a_steps():
            return [[0, 1], [2], [3, 4], [5], [6, 7], [], [], []]

        block = ctx.enter_context(nc.Block())

        @block.sync
        def _(sp):
            def fetch_expert(e):
                sp.dma_start(w12[:, e, 0:KC * I0].rearrange("p (k i) -> p k i", k=KC), a["w1"][e]).then_inc(w12_in.sem, 16)
                sp.dma_start(w12[:, e, KC * I0:].rearrange("p (c d) -> p c d", c=IC0), a["w2"][e]).then_inc(w12_in.sem, 16)

            sp.dma_start(x, a["x"].rearrange("(j p) d -> p j d", p=P)).then_inc(loaded["x"].sem, 16)
            for n in ("consts",):
                sp.dma_start(con, a[n]).then_inc(loaded[n].sem, 16)
            sp.dma_start(w_a0, a["w_attn0"]).then_inc(loaded["w_attn0"].sem, 16)
            sp.dma_start(ctok, a["ctx"].rearrange("(j p) d -> p j d", p=P)).then_inc(loaded["ctx"].sem, 16)
            sp.wait_ge(pool_step.sem, 1)
            sp.dma_start(a["sorted"].rearrange("(r p) d -> p r d", p=P), wide(blank, 1, ROW_TILES))\
              .then_inc(blank_rows.sem, 16)
            for e in (7, 6, 5):
                fetch_expert(e)
            sp.wait_ge(x_norm.sem, NT)
            sp.dma_start(w_x0, a["w_xattn0"]).then_inc(loaded["w_xattn0"].sem, 16)
            for e in (4,):
                fetch_expert(e)
            sp.wait_ge(x_norm.sem, 2 * NT)
            sp.dma_start(w_r0, a["w_route0"]).then_inc(loaded["w_route0"].sem, 16)
            sp.wait_ge(blank_rows.sem, 16 + 1)
            for i in range(3):
                sp.dma_start(b1_row[32 * i:32 * i + E0, :], a["b1"]).then_inc(b1_in.sem, 16)
            sp.dma_start(ceb[E0:2 * E0, :], a["b2"]).then_inc(b2_in.sem, 16)
            for e in (3, 2, 1, 0):
                fetch_expert(e)
            sp.wait_ge(sorted_out.sem, 16 * 2 * NT)
            for r in range(ROW_TILES + 4):
                if r < ROW_TILES:
                    if r >= 2:
                        sp.wait_ge(xst_ps.sem, xst_ps.base + r - 1)
                    sp.dma_start(xs[:, r % 2, :], a["sorted"][r * P:(r + 1) * P, :]).then_inc(xs_in[r % 2].sem, 16)
                q = r - 4
                if q >= 0:
                    sp.wait_ge(ys_ready.sem, q + 1)
                    sp.dma_start(a["returned"][q * P:(q + 1) * P, :], ys[:, q % 2, :])\
                      .then_inc(ys_out[q % 2].sem, 16)
            sp.wait_ge(down_ps.sem, down_ps.base + ROW_TILES)
            sp.dma_start(ctok, a["ctx"].rearrange("(j p) d -> p j d", p=P)).then_inc(loaded["ctx"].sem, 16)
            sp.wait_ge(x_norm.sem, 3 * NT)
            sp.dma_start(w_a1, a["w_attn1"]).then_inc(loaded["w_attn1"].sem, 16)
            sp.wait_ge(ft_sb.sem, 2 * NT)
            for n in range(3):
                sp.dma_start(a["turned"][n].rearrange("(k p) t -> p k t", p=P), ft1[:, 1 + n, :, :])\
                  .then_inc(turned_out.sem, 16)
            sp.wait_ge(turned_out.sem, 48)
            for n in range(3):
                for b in range(B):
                    r0 = (b % 8) * H1
                    sp.dma_start(bh1[n][r0:r0 + H1, b // 8, :, :], turned_v[(1, 0, 2)[n], b])\
                      .then_inc(bh_in.sem, 16)
            sp.wait_ge(regressed.sem, 1)
            for b in range(B):
                r0 = (b % 8) * H1
                sp.dma_start(solved_v[b], vn1[r0:r0 + H1, b // 8, :, :]).then_inc(solved_out.sem, 16)
            sp.wait_ge(solved_out.sem, 16 * B)
            sp.dma_start(vnt1, a["solved"].rearrange("(k p) t -> p k t", p=P)).then_inc(vnt_in.sem, 16)
            sp.wait_ge(x_norm.sem, 4 * NT)
            sp.dma_start(w_x1, a["w_xattn1"]).then_inc(loaded["w_xattn1"].sem, 16)
            sp.dma_start(mask5, a["mask"]).then_inc(mask_in.sem, 16)
            sp.wait_ge(x_norm.sem, 5 * NT)
            sp.dma_start(w_f1, a["w_ffn1"]).then_inc(loaded["w_ffn1"].sem, 16)
            sp.dma_start(map_i[0:E1, :], a["mapping"]).then_inc(map_in.sem, 16)
            for f in range(FX):
                if f >= 2:
                    sp.wait_ge(out6_ps.sem, out6_ps.base + NT * (f - 1))
                sp.dma_start(w_e[:, f % 2, :], a["experts"][f]).then_inc(experts_in[f % 2].sem, 16)
            sp.wait_ge(x_norm.sem, NT * 6)
            sp.dma_start(a["out"].rearrange("(j p) d -> p j d", p=P), x).then_inc(out_done.sem, 16)
            sp.wait_ge(out_done.sem, 16)

        @block.gpsimd
        def _(pool):
            def do(instruction, s=pool_step):
                pool.wait_ge(s.sem, s.by(instruction))

            do(pool.memset(blank, 0.0))
            do(pool.memset(kt0[64:72, :], 1.0))
            do(pool.memset(vb0[:, :, :, :], 0.0))
            v = vb0.rearrange("p b q (r c) -> p (b q) r c", r=2)
            do(pool.memset(v[0:64, :, 0, DH0:DH0 + 1], 1.0))
            do(pool.memset(v[64:128, :, 1, DH0:DH0 + 1], 1.0))
            pool.wait_ge(loaded["consts"].sem, 16)
            for j in range(NT):
                pool.wait_ge(q_sb.sem, 5 + j // 4)
                keys = kt0[0:72, j * P:(j + 1) * P].rearrange("p (b t) -> p b t", b=2)
                for i in range(2):
                    last = pool.tensor_tensor(
                        out=kb0[0:72, 2 * j + i, :, :], in0=wide(keys[:, i, :], 1, H0),
                        in1=wide(c["headmask0"], 2, S), op=ALU.mult)
                kb_ready.by(last)
            pool.wait_ge(x_norm.sem, NT)
            do(pool.memset(vx.rearrange("p b s h c -> p (b s h) c")[:, :, DHX:DHX + 1], 1.0))
            do(pool.tensor_copy(selm, c["selmax"]), selm_ready)
            pool.wait_ge(x_norm.sem, 2 * NT)
            do(pool.memset(b1_row, 0.0), blank_rows)
            for e in range(E0):
                last = pool.tensor_copy(b1_pick[:, e, :], c["b1_rows"][0:B1_ROWS, e:e + 1].to_broadcast([B1_ROWS, P]))
            do(last)
            pool.wait_ge(b1_in.sem, 48)
            do(pool.tensor_copy(b1_terms, b1_row))
            do(pool.tensor_tensor(out=b1_rest, in0=b1_row, in1=b1_terms, op=ALU.subtract))
            pool.tensor_copy(b1_terms[32:64, :], b1_rest[32:64, :])
            do(pool.tensor_copy(b1_terms[64:B1_ROWS, :], b1_rest[64:B1_ROWS, :]))
            do(pool.tensor_tensor(out=b1_rest[64:B1_ROWS, :], in0=b1_rest[64:B1_ROWS, :],
                                  in1=b1_terms[64:B1_ROWS, :], op=ALU.subtract))
            do(pool.tensor_copy(b1_terms[64:B1_ROWS, :], b1_rest[64:B1_ROWS, :]), b1_ready)
            pool.wait_ge(blank_rows.sem, 16 + 1)
            pool.wait_ge(place_ready.sem, place_ready.base + 1)
            for n in range(2 * NT):
                pool.indirect_dma_start(a["sorted"], bass.IndirectOffsetOnAxis(ap=slot_row_i[:, n:n + 1], axis=0),
                                        x[:, n // 2, :], None).then_inc(sorted_out.sem, 16)
            pool.wait_ge(ys_out[0].sem, ys_out[0].base + 16 * (ROW_TILES - ROW_TILES // 2))
            pool.wait_ge(ys_out[1].sem, ys_out[1].base + 16 * (ROW_TILES // 2))
            for n in range(2 * NT):
                pool.indirect_dma_start(back[:, n, :], None, a["returned"],
                                        bass.IndirectOffsetOnAxis(ap=slot_row_i[:, n:n + 1], axis=0))\
                    .then_inc(back_in.sem, 16)
            for j in range(NT):
                pool.wait_ge(ft_sb.sem, 2 * j + 1)
                if j >= 2:
                    pool.wait_ge(a1_ps.sem, 2 * (j - 1))
                for i in range(4):
                    b, k = 2 * j + i // 2, i % 2
                    last = pool.tensor_tensor(out=kb1[:, b % 4, k, :, :], in0=wide(ft1[:, 1, k, b * S:(b + 1) * S], 1, 8),
                                              in1=wide(c["headmask1"], 2, S), op=ALU.mult)
                kb1_ready.by(last)
            pool.wait_ge(a1_ps.sem, 2 * NT)
            do(pool.memset(vb1.rearrange("p b q c -> p (b q c)"), 0.0), blank1)
            v = vb1.rearrange("p b q (r c) -> p (b q) r c", r=2)
            do(pool.memset(v[0:64, :, 0, DH1:DH1 + 1], 1.0), blank1)
            do(pool.memset(v[64:128, :, 1, DH1:DH1 + 1], 1.0), blank1)
            pool.wait_ge(x_norm.sem, 4 * NT)
            do(pool.memset(vb5.rearrange("p b q c -> p (b q c)"), 0.0), blank5)
            v = vb5.rearrange("p b q (r c) -> p (b q) r c", r=2)
            do(pool.memset(v[0:64, :, 0, DH1:DH1 + 1], 1.0), blank5)
            do(pool.memset(v[64:128, :, 1, DH1:DH1 + 1], 1.0), blank5)
            for b in range(B):
                pool.wait_ge(kq5_sb.sem, 2 * (b // 8) + 2)
                if b >= 4:
                    pool.wait_ge(b5_ps.sem, b - 3)
                for k in range(KC):
                    last = pool.tensor_tensor(out=kb5[:, (b % 4) * KC + k, :, :],
                                              in0=wide(k5[:, k, b * S:(b + 1) * S], 1, 8),
                                              in1=wide(c["headmask1"], 2, S), op=ALU.mult)
                kb5_ready.by(last)


        @block.tensor
        def _(pe):
            ident = c["ident"]

            def turn_x(use):
                for j in range(NT):
                    t = use * NT + j
                    if use == 0:
                        pe.wait_ge(loaded["x"].sem, 16)
                        pe.wait_ge(loaded["consts"].sem, 16)
                    else:
                        pe.wait_ge(x_norm.sem, NT * (XT_AFTER[use] - 1) + j + 1)
                    if t >= 2:
                        pe.wait_ge(xt_sb.sem, t - 1)
                    for k in range(KC):
                        last = pe.transpose(bank(t % 2)[:, k * P:(k + 1) * P], x[:, j, k * P:(k + 1) * P], ident)
                    xt_ps.by(last)

            turn_x(0)
            pe.wait_ge(loaded["w_attn0"].sem, 16)
            for u in range(6):
                n, pair = (u // 2, u % 2) if u < 4 else (u - 4, None)
                pe.wait_ge(xt_sb.sem, 4 * n + 4)
                if u >= 2:
                    pe.wait_ge(q_sb.sem, u - 1)
                for k in range(KC):
                    w = a0["wk"][:, k, :] if pair is None else a0["wq"][:, k, pair * P:(pair + 1) * P]
                    m = DKV if pair is None else P
                    last = pe.matmul(bank(2 + u % 2)[0:m, :], w, xt[:, k, n * BANK:(n + 1) * BANK],
                                     start=(k == 0), stop=(k == KC - 1))
                q_ps.by(last)
            for b in range(B):
                for r in range(2):
                    for k in range(KC):
                        last = pe.matmul(bank(4 + b // 8)[64 * r:64 * r + 64, (b % 8) * 32:(b % 8 + 1) * 32],
                                         xt[:, k, b * S:(b + 1) * S],
                                         a0["wv"][:, k, :].rearrange("p (q r c) -> p q r c", r=2, c=DH0)[:, :, r, :],
                                         start=(k == 0), stop=(k == KC - 1))
                if b % 8 == 7:
                    v_ps.by(last)
            for j in range(NT):
                pe.wait_ge(elu_ready.sem, 1)
                if j >= 2:
                    pe.wait_ge(mem_read.sem, j - 1)
                for g in range(NQ):
                    last = pe.matmul(bank(6 + j % 2)[:, g * 65:(g + 1) * 65], sig[0:DKV, g, j * P:(j + 1) * P],
                                     a0["mem"], start=True, stop=True)
                mem_ps.by(last)

            def first_scores0(b):
                pe.wait_ge(kb_ready.sem, b // 2 + 1)
                for pair in range(2):
                    if b >= 2:
                        pe.wait_ge(a0_max.sem, 2 * (b - 2) + pair + 1)
                    a0_ps.by(pe.matmul(bank(2 * (b % 2) + pair), q4[0:DKV, b, 2 * pair:2 * pair + 2, :],
                                       kb0[0:DKV, b, :, :], start=True, stop=True))

            def scores0(b):
                pe.wait_ge(a0_max.sem, 2 * b + 2)
                if b >= 1:
                    pe.wait_ge(nmt0_sb.sem, b)
                for pair in range(2):
                    last = pe.transpose(bank(4)[0:H0, pair * P:(pair + 1) * P], nm0[:, b % 2, pair, :], ident)
                nmt0_ps.by(last)
                pe.wait_ge(nmt0_sb.sem, b + 1)
                if b >= 1:
                    pe.wait_ge(pt0_ready.sem, b)
                for hp in range(4):
                    last = pe.matmul(bank(5, 2)[:, hp * D:(hp + 1) * D], kb0[0:72, b, 2 * hp:2 * hp + 2, :],
                                     q4[0:72, b, :, :], start=True, stop=True)
                b0_ps.by(last)

            def values0(b):
                j, half = b // 2, 64 * (b % 2)
                pe.wait_ge(pt0_ready.sem, b + 1)
                if b % 2 == 0 and j >= 1:
                    pe.wait_ge(o0_read.sem, j)
                for g in range(NQ):
                    for hp in range(4):
                        at = (g * 4 + hp) * 18
                        last = pe.matmul(bank(7)[half:half + 64, at:at + 18], pt0[:, b % 2, hp, g * S:(g + 1) * S],
                                         vb0[:, b, hp, :], start=True, stop=True)
                o0_ps.by(last)

            pe.wait_ge(q_sb.sem, 6)
            pe.wait_ge(v_sb.sem, 2)
            pe.wait_ge(mem_read.sem, NT)
            first_scores0(0)
            for b in range(B):
                if b + 1 < B:
                    first_scores0(b + 1)
                scores0(b)
                if b >= 1:
                    values0(b - 1)
            values0(B - 1)

            def project(u):
                side, j = ("k", u) if u < NT else ("q", u - NT)
                if u == 0:
                    pe.wait_ge(loaded["ctx"].sem, 16)
                    pe.wait_ge(loaded["w_xattn0"].sem, 16)
                if side == "q":
                    pe.wait_ge(x_norm.sem, j + 1)
                if u >= 2:
                    pe.wait_ge(pj_sb.sem, u - 1)
                src = ctok if side == "k" else x
                pj_ps.by(pe.matmul(bank(u % 2)[:, 0:D], x0["w" + side], src[:, j, :], start=True, stop=True))

            def rotate(u):
                pe.wait_ge(pj_sb.sem, u + 1)
                if u >= 2:
                    pe.wait_ge(qr_ready.sem, u - 1)
                rot_ps.by(pe.matmul(bank(2 + u % 2)[:, 0:D], c["rotx"], qs[:, u % 2, :], start=True, stop=True))

            def replicate(u):
                pe.wait_ge(qr_ready.sem, u + 1)
                for p in range(2):
                    if u >= 2:
                        pe.wait_ge(st_ready.sem, 2 * (u - 2) + p + 1)
                    for g in range(2):
                        last = pe.matmul(bank(4 + 2 * (u % 2) + p)[:, g * D:(g + 1) * D],
                                         c["rep"][64 * p:64 * p + 64, g, :], qr[64 * p:64 * p + 64, u % 2, :],
                                         start=True, stop=True)
                    rep_ps.by(last)

            def head_rows(h):
                return 32 * (h % 4), 32 * (h % 4) + 32, h // 4

            def first_scores_x(b, h):
                u = b * HX + h
                r0, r1, g = head_rows(h)
                if u >= 2:
                    pe.wait_ge(ax_max.sem, u - 1)
                for tc in range(2):
                    last = pe.matmul(bank(u % 2)[:, tc * D:(tc + 1) * D], stack["q"][r0:r1, b, g, tc * P:(tc + 1) * P],
                                     stack["k"][r0:r1, b, g, :], start=True, stop=True, tile_position=(r0, 0))
                ax_ps.by(last)

            def turn_max(b):
                pe.wait_ge(nmx_ready.sem, b + 1)
                if b >= 1:
                    pe.wait_ge(nmtx_sb.sem, b)
                for tc in range(2):
                    last = pe.transpose(bank(4).bitcast(BF16)[0:HX, tc * P:(tc + 1) * P], nmxb[:, b % 2, tc, :],
                                        ident16)
                nmtx_ps.by(last)

            def scores_x(b, h):
                u = b * HX + h
                r0, r1, g = head_rows(h)
                if h == 0:
                    pe.wait_ge(nmtx_sb.sem, b + 1)
                if u >= 2:
                    pe.wait_ge(ptx_ready.sem, u - 1)
                for sc in range(2):
                    out = bank(2 + u % 2)[:, sc * D:(sc + 1) * D]
                    pe.matmul(out, stack["k"][r0:r1, b, g, sc * P:(sc + 1) * P], stack["q"][r0:r1, b, g, :],
                              start=True, stop=False, tile_position=(r0, 0))
                    last = pe.matmul(out, selm[r0:r0 + HX, h, :], nmtx[r0:r0 + HX, b % 2, :],
                                     start=False, stop=True, tile_position=(r0, 0))
                bx_ps.by(last)

            def values_x(b, h):
                u = b * HX + h
                pe.wait_ge(ptx_ready.sem, u + 1)
                if h == 0 and b >= 2:
                    pe.wait_ge(onx_ready.sem, b - 1)
                for tc in range(2):
                    at = (tc * HX + h) * 9
                    for sc in range(2):
                        last = pe.matmul(bank(5 + b % 2)[:, at:at + 9], ptx[:, u % 2, sc, tc * P:(tc + 1) * P],
                                         vx[:, b, sc, h, :], start=(sc == 0), stop=(sc == 1))
                pvx_done.by(last)

            def turn_out_x(b):
                pe.wait_ge(onx_ready.sem, b + 1)
                if b >= 1:
                    pe.wait_ge(yx_read.sem, b)
                for tc in range(2):
                    last = pe.transpose(bank(7)[0:S, tc * P:(tc + 1) * P], onx[:, b % 2, tc, :], ident)
                otx_ps.by(last)

            def out_x(b):
                half = 64 * (b % 2)
                pe.wait_ge(otx_sb.sem, b + 1)
                yx_ps.by(pe.matmul(bank(7)[half:half + 64, D:2 * D], x0["wo"], otx[0:S, b % 2, :],
                                   start=True, stop=True))

            for j in range(NT):
                if j == 0:
                    pe.wait_ge(loaded["ctx"].sem, 16)
                    pe.wait_ge(loaded["w_xattn0"].sem, 16)
                    pe.wait_ge(x_norm.sem, NT)
                for p in range(2):
                    if j >= 2:
                        pe.wait_ge(vx_sb.sem, 2 * (j - 2) + p + 1)
                    for sc in range(2):
                        last = pe.matmul(bank(2 * (j % 2) + p)[:, sc * S:(sc + 1) * S],
                                         ctok[64 * p:64 * p + 64, j, sc * P:(sc + 1) * P],
                                         x0["wv"][64 * p:64 * p + 64, :], start=True, stop=True)
                    vx_ps.by(last)
            pe.wait_ge(vx_sb.sem, 2 * NT)
            for u in range(2 * NT + 2):
                if u < 2 * NT:
                    project(u)
                if 1 <= u <= 2 * NT:
                    rotate(u - 1)
                if u >= 2:
                    replicate(u - 2)
            pe.wait_ge(st_ready.sem, 4 * NT)
            pe.wait_ge(selm_ready.sem, 2)
            for h in range(HX):
                first_scores_x(0, h)
            turn_max(0)
            for b in range(B):
                for h in range(HX):
                    if b + 1 < B:
                        for n in a_steps()[h]:
                            first_scores_x(b + 1, n)
                        if h == 6:
                            turn_max(b + 1)
                    if h == 2 and b >= 1:
                        turn_out_x(b - 1)
                    if h == 4 and b >= 1:
                        out_x(b - 1)
                    scores_x(b, h)
                    if b or h:
                        values_x(*divmod(b * HX + h - 1, HX))
            values_x(B - 1, HX - 1)
            turn_out_x(B - 1)
            out_x(B - 1)
            def turn_rows(r):
                pe.wait_ge(xs_in[r % 2].sem, xs_in[r % 2].base + 16 * (r // 2 + 1))
                if r >= 2:
                    pe.wait_ge(xst_sb.sem, xst_sb.base + r - 1)
                for k in range(KC):
                    last = pe.transpose(bank(6 + r % 2)[:, k * P:(k + 1) * P], xs[:, r % 2, k * P:(k + 1) * P], ident)
                xst_ps.by(last)

            def up(r):
                e = pe.value_load(tile_e_i[0:1, r:r + 1], min_val=0, max_val=E0 - 1)
                pe.wait_ge(xst_sb.sem, xst_sb.base + r + 1)
                for n in range(2):
                    if r >= 1:
                        pe.wait_ge(hid_ready.sem, hid_ready.base + 2 * (r - 1) + n + 1)
                    cols = slice(n * BANK, (n + 1) * BANK)
                    pe.matmul(bank(n), b1_pick[:, bass.ds(e, 1), :].rearrange("p a t -> p (a t)"), b1_terms[:, cols],
                              start=True, stop=False)
                    for k in range(KC):
                        last = pe.matmul(bank(n), xst[:, r % 2, k, :], w1v[:, bass.ds(e, 1), k, cols],
                                         start=False, stop=(k == KC - 1))
                    up_ps.by(last)

            def turn_hidden(r):
                for n in range(2):
                    pe.wait_ge(hid_ready.sem, hid_ready.base + 2 * r + n + 1)
                    if r >= 1:
                        pe.wait_ge(hidt_sb.sem, hidt_sb.base + 2 * (r - 1) + n + 1)
                    for i in range(4):
                        at = n * BANK + i * P
                        last = pe.transpose(bank(2 + n)[:, i * P:(i + 1) * P], hid[:, r % 2, at:at + P], ident)
                    hidt_ps.by(last)

            def down(r):
                e = pe.value_load(tile_e_i[0:1, r:r + 1], min_val=0, max_val=E0 - 1)
                if r >= 2:
                    pe.wait_ge(ys_ready.sem, r - 1)
                for ic in range(IC0):
                    if ic % 4 == 0:
                        pe.wait_ge(hidt_sb.sem, hidt_sb.base + 2 * r + ic // 4 + 1)
                    last = pe.matmul(bank(4 + r % 2)[:, 0:D], hidt[:, r % 2, ic * P:(ic + 1) * P],
                                     w2v[:, bass.ds(e, 1), ic, :], start=(ic == 0), stop=(ic == IC0 - 1))
                down_ps.by(last)

            turn_x(1)
            pe.wait_ge(loaded["w_route0"].sem, 16)
            for n in range(2):
                pe.wait_ge(xt_sb.sem, NT + 4 * n + 4)
                for k in range(KC):
                    last = pe.matmul(bank(2 + n), r0["rw1"][:, k, :], xt[:, k, n * BANK:(n + 1) * BANK],
                                     start=(k == 0), stop=(k == KC - 1))
                r1_ps.by(last)
            for j in range(NT):
                pe.wait_ge(r1_sb.sem, j // 4 + 1)
                last = pe.matmul(bank(4)[:, j * E0:(j + 1) * E0], r1[:, j * P:(j + 1) * P], r0["rw2"],
                                 start=True, stop=True)
            lg_ps.by(last)
            pe.wait_ge(marks_ready.sem, 1)
            for j in range(NT):
                last = pe.matmul(bank(5)[:, 0:2 * E0], c["ones"], marks[:, j, :], start=(j == 0),
                                 stop=(j == NT - 1))
            pe.matmul(bank(6)[:, 0:NT * E0], c["before"], both, start=True, stop=False)
            last = pe.matmul(bank(6)[:, 0:NT * E0], c["ones"], earlier, start=False, stop=True)
            cnt_ps.by(last)
            pe.wait_ge(b1_gelu.sem, 1)
            pe.wait_ge(w12_in.sem, 16 * 2 * E0)
            for e in range(E0):
                for k in range(KC):
                    at = k * E0 + e
                    for ic in range(IC0):
                        last = pe.matmul(bank(7)[:, at:at + 1], w2v[:, e, ic, k * P:(k + 1) * P],
                                         b1g[:, e, ic:ic + 1], start=(ic == 0), stop=(ic == IC0 - 1))
            ce_ps.by(last)
            pe.wait_ge(wc_ready.sem, 1)
            for i in range(2):
                for t in range(4):
                    last = pe.transpose(bank(2 + i)[0:2 * E0, t * P:(t + 1) * P], weight_c[:, 4 * i + t, :], ident)
                wct_ps.by(last)
            pe.wait_ge(cet_sb.sem, 1)
            for k in range(KC):
                last = pe.transpose(bank(4)[0:E0, k * P:(k + 1) * P], cet[:, k * E0:(k + 1) * E0], ident)
            cer_ps.by(last)
            pe.wait_ge(tiles_ready.sem, tiles_ready.base + 1)
            pe.wait_ge(b1_ready.sem, b1_ready.base + 1)
            pe.wait_ge(wct_sb.sem, 2)
            pe.wait_ge(ceb_sb.sem, 1)
            turn_rows(0)
            for r in range(ROW_TILES + 2):
                if r + 1 < ROW_TILES:
                    turn_rows(r + 1)
                if r < ROW_TILES:
                    up(r)
                if 1 <= r <= ROW_TILES:
                    turn_hidden(r - 1)
                if r >= 2:
                    down(r - 2)
            pe.wait_ge(b2_in.sem, 16)
            for j in range(NT):
                if j >= 2:
                    pe.wait_ge(const_read.sem, j - 1)
                const_ps.by(pe.matmul(bank(j % 2)[:, 0:D], wct[0:2 * E0, j * P:(j + 1) * P], ceb[0:2 * E0, :],
                                      start=True, stop=True))
            turn_x(2)
            pe.wait_ge(loaded["w_attn1"].sem, 16)
            for j in range(NT):
                pe.wait_ge(xt_sb.sem, 2 * NT + j + 1)
                if j >= 2:
                    pe.wait_ge(pj1_sb.sem, j - 1)
                for k in range(KC):
                    pe.matmul(bank(2 + 2 * (j % 2)), xt[:, k, j * P:(j + 1) * P], a1["wqk"][:, k, :],
                              start=(k == 0), stop=(k == KC - 1))
                for k in range(KC):
                    last = pe.matmul(bank(3 + 2 * (j % 2))[:, 0:D + H1], xt[:, k, j * P:(j + 1) * P],
                                     a1["wvb"][:, k, :], start=(k == 0), stop=(k == KC - 1))
                pj1_ps.by(last)
            for j in range(NT):
                pe.wait_ge(turned1.sem, j + 1)
                for half in range(2):
                    if j >= 1:
                        pe.wait_ge(ft_sb.sem, 2 * (j - 1) + half + 1)
                    src = ((rq1[:, j % 2, 0:D], kw1[:, j % 2, :]), (rq1[:, j % 2, D:2 * D], vz1[:, j, 0:D]))[half]
                    for i in range(4):
                        last = pe.transpose(bank(6 + half)[:, i * P:(i + 1) * P],
                                            src[i // 2][:, (i % 2) * P:(i % 2 + 1) * P], ident)
                    tr1_ps.by(last)

            def scores1(w):
                j, k = divmod(w, 2)
                pe.wait_ge(kb1_ready.sem, j + 1)
                if w >= 2:
                    pe.wait_ge(sm_ready.sem, w - 1)
                for p in range(2):
                    b = 2 * j + p
                    last = pe.matmul(bank(2 + w % 2)[64 * p:64 * p + 64, :], ft1[:, 0, k, b * S:(b + 1) * S],
                                     kb1[:, b % 4, k, :, :], start=True, stop=True)
                a1_ps.by(last)

            def turn_probs1(w):
                pe.wait_ge(sm_exp.sem, w + 1)
                if w >= 2:
                    pe.wait_ge(pt_sb.sem, w - 1)
                for i in range(4):
                    last = pe.transpose(bank(4 + w % 2)[:, i * P:(i + 1) * P], sm1[:, w % 2, i * P:(i + 1) * P],
                                        ident)
                pt_ps.by(last)

            pe.wait_ge(ft_sb.sem, 2 * NT)
            for w in range(2 * NT + 1):
                if w < 2 * NT:
                    scores1(w)
                if w >= 1:
                    turn_probs1(w - 1)

            pe.wait_ge(vnt_in.sem, 16)
            for b in range(B):
                if b >= 8 and b % 4 == 0:
                    pe.wait_ge(vb1_sb.sem, b // 4 - 1)
                for r in range(2):
                    for k in range(KC):
                        at = (b % 4) * P + k * 64
                        last = pe.matmul(bank(6 + b // 4 % 2)[64 * r:64 * r + 64, at:at + 64],
                                         vnt1[:, k, b * S:(b + 1) * S],
                                         ident.rearrange("p (q r c) -> p q r c", r=2, c=DH1)[:, :, r, :],
                                         start=True, stop=True)
                if b % 4 == 3:
                    vb1_ps.by(last)

            def values1(j):
                pe.wait_ge(vb1_sb.sem, j // 2 + 1)
                if j >= 2:
                    pe.wait_ge(on1_ready.sem, j - 1)
                for p in range(2):
                    for q in range(8):
                        at = q // 4 * 0 + q * 34
                        last = pe.matmul(bank(j % 2)[64 * p:64 * p + 64, at:at + 34],
                                         pt1[:, 2 * j + q // 4, (q % 4) * P + 64 * p:(q % 4) * P + 64 * p + 64],
                                         vb1[:, 2 * j + p, q, :], start=True, stop=True)
                o1_ps.by(last)

            def turn_out1(j):
                pe.wait_ge(on1_ready.sem, j + 1)
                if j >= 2:
                    pe.wait_ge(ot1_sb.sem, j - 1)
                for k in range(KC):
                    last = pe.transpose(bank(2 + j % 2)[:, k * P:(k + 1) * P], on1[:, j % 2, k * P:(k + 1) * P],
                                        ident)
                ot1_ps.by(last)

            def out1(j):
                pe.wait_ge(ot1_sb.sem, j + 1)
                if j >= 2:
                    pe.wait_ge(y1_read.sem, j - 1)
                for k in range(KC):
                    last = pe.matmul(bank(4 + j % 2)[:, 0:D], ot1[:, j % 2, k, :], a1["wo"][:, k, :],
                                     start=(k == 0), stop=(k == KC - 1))
                y1_ps.by(last)

            pe.wait_ge(pt_sb.sem, 2 * NT)
            for j in range(NT + 2):
                if j < NT:
                    values1(j)
                if 1 <= j <= NT:
                    turn_out1(j - 1)
                if j >= 2:
                    out1(j - 2)
            pe.wait_ge(x_norm.sem, 4 * NT)
            pe.wait_ge(loaded["ctx"].sem, 32)
            for j in range(NT):
                if j >= 2:
                    pe.wait_ge(ct_sb.sem, j - 1)
                for k in range(KC):
                    last = pe.transpose(bank(6 + j % 2)[:, k * P:(k + 1) * P], ctok[:, j, k * P:(k + 1) * P], ident)
                ct_ps.by(last)
            turn_x(3)
            pe.wait_ge(loaded["w_xattn1"].sem, 16)
            for u in range(8):
                n, m = u // 2 % 2, u % 2
                if u < 4:
                    pe.wait_ge(ct_sb.sem, 4 * n + 4)
                else:
                    pe.wait_ge(xt_sb.sem, 3 * NT + 4 * n + 4)
                if u >= 2:
                    pe.wait_ge(kq5_sb.sem, u - 1)
                w, src = (x1["wk"], ct5) if u < 4 else (x1["wq"], xt)
                for k in range(KC):
                    last = pe.matmul(bank(2 + u % 2), w[:, k, m * P:(m + 1) * P],
                                     src[:, k, n * BANK:(n + 1) * BANK], start=(k == 0), stop=(k == KC - 1))
                kq5_ps.by(last)
            for b in range(B):
                if b % 4 == 0 and b >= 8:
                    pe.wait_ge(v5_sb.sem, b // 4 - 1)
                for r in range(2):
                    for k in range(KC):
                        last = pe.matmul(bank(4 + b // 4 % 2)[64 * r:64 * r + 64, (b % 4) * P:(b % 4 + 1) * P],
                                         ct5[:, k, b * S:(b + 1) * S],
                                         x1["wv"][:, k, :].rearrange("p (q r c) -> p q r c", r=2, c=DH1)[:, :, r, :],
                                         start=(k == 0), stop=(k == KC - 1))
                if b % 4 == 3:
                    v5_ps.by(last)

            def scores5(b):
                pe.wait_ge(kb5_ready.sem, b + 1)
                if b >= 2:
                    pe.wait_ge(s5_ready.sem, b - 1)
                for q in range(8):
                    last = pe.matmul(bank(4 + b % 2)[:, q * S:(q + 1) * S],
                                     kb5[:, (b % 4) * KC + q // 4, 2 * (q % 4):2 * (q % 4) + 2, :],
                                     q5[:, q // 4, b * S:(b + 1) * S], start=True, stop=True)
                b5_ps.by(last)

            def values5(b):
                j, half = b // 2, 64 * (b % 2)
                pe.wait_ge(pt5_ready.sem, b + 1)
                if j >= 2 and b % 2 == 0:
                    pe.wait_ge(on5_ready.sem, j - 1)
                for q in range(8):
                    last = pe.matmul(bank(6 + j % 2)[half:half + 64, q * 34:(q + 1) * 34],
                                     pt5[:, b % 2, q * S:(q + 1) * S], vb5[:, b, q, :], start=True, stop=True)
                o5_ps.by(last)

            def turn_out5(j):
                pe.wait_ge(on5_ready.sem, j + 1)
                if j >= 2:
                    pe.wait_ge(ot5_sb.sem, j - 1)
                for k in range(KC):
                    last = pe.transpose(bank(j % 2)[:, k * P:(k + 1) * P], on5[:, j % 2, k * P:(k + 1) * P], ident)
                ot5_ps.by(last)

            def out5(j):
                pe.wait_ge(ot5_sb.sem, j + 1)
                if j >= 2:
                    pe.wait_ge(y5_read.sem, j - 1)
                for k in range(KC):
                    last = pe.matmul(bank(2 + j % 2)[:, 0:D], ot5[:, j % 2, k, :], x1["wo"][:, k, :],
                                     start=(k == 0), stop=(k == KC - 1))
                y5_ps.by(last)

            pe.wait_ge(kq5_sb.sem, 8)
            pe.wait_ge(v5_sb.sem, 4)
            scores5(0)
            for b in range(B + 4):
                if b + 1 < B:
                    scores5(b + 1)
                if b < B:
                    values5(b)
                if b % 2 == 0 and 2 <= b <= B:
                    turn_out5(b // 2 - 1)
                if b % 2 == 0 and b >= 4:
                    out5(b // 2 - 2)
            def gate_up(lhs_gate, lhs_up, c4, n):
                for i, w in enumerate((lhs_gate, lhs_up)):
                    v = (n * 4 + c4) * 2 + i
                    if v >= 4:
                        w_before = v - 4
                        pe.wait_ge((sh_silu, sh_h)[i].sem, (sh_silu, sh_h)[i].base + w_before // 2 + 1)
                    for k in range(KC):
                        last = pe.matmul(bank(v % 4)[0:IH, :], w[:, k, c4 * IH:(c4 + 1) * IH],
                                         xt[:, k, n * BANK:(n + 1) * BANK], start=(k == 0), stop=(k == KC - 1))
                    sh_ps.by(last)

            def fuse_in(n):
                f, half = n // 2, n % 2
                if half == 0:
                    pe.wait_ge(experts_in[f % 2].sem, 16 * (f // 2 + 1))
                cols = slice(half * BANK, (half + 1) * BANK)
                for k in range(KC):
                    bank_free(pe, (("x", k), n))
                    mid_ps.by(pe.matmul(bank(ring[("x", k), n] % 4), f1["mask_up"][:, f, k * P:(k + 1) * P],
                                        wt6[0:E1, cols], start=True, stop=True))
                bank_free(pe, (("w", 0), n))
                mid_ps.by(pe.matmul(bank(ring[("w", 0), n] % 4), c["spread"][:, f, :], wt6[0:E1, cols],
                                    start=True, stop=True))

            def ranks(n):
                pe.wait_ge(mid_dve.sem, mid_dve.base + by_dve[("x", 1), n] + 1)
                bank_free(pe, (("a", 0), n))
                for k in range(KC):
                    last = pe.matmul(bank(ring[("a", 0), n] % 4), ex[n // 2 % 2]["qa"][:, k, :], xe6[:, n % 2, k, :],
                                     start=(k == 0), stop=(k == KC - 1))
                mid_ps.by(last)

            def features(n):
                e, half = ex[n // 2 % 2], n % 2
                for kind, w, r0 in (("g", "gw", 0), ("u", "uw", 64)):
                    for i in range(2):
                        key = ((kind, i), n)
                        bank_free(pe, key)
                        out = bank(ring[key] % 4)[0:IH, :]
                        for k in range(KC):
                            pe.matmul(out, e[w][:, k, i * IH:(i + 1) * IH], xe6[:, half, k, :], start=(k == 0),
                                      stop=False)
                        if kind == "g" and i == 0:
                            pe.wait_ge(mid_dve.sem, mid_dve.base + by_dve[("a", 0), n] + 1)
                            pe.wait_ge(qb6_ready.sem, qb6_ready.base + 2 * (n // 2) + 2)
                        mid_ps.by(pe.matmul(out, qb6[r0:r0 + 64, n // 2 % 2, i * IH:(i + 1) * IH],
                                            aw6[r0:r0 + 64, half, :], start=False, stop=True))

            def outputs(n):
                e, half = ex[n // 2 % 2], n % 2
                key = (("d", 0), n)
                bank_free(pe, key)
                pe.wait_ge(mid_dve.sem, mid_dve.base + by_dve[("u", 1), n] + 1)
                for i in range(2):
                    last = pe.matmul(bank(ring[key] % 4)[0:64, :], e["dqa"][:, i, :], h6[0:IH, 2 * half + i, :],
                                     start=(i == 0), stop=(i == 1))
                mid_ps.by(last)
                for t in range(4):
                    if n >= 1:
                        pe.wait_ge(out6_read.sem, out6_read.base + 4 * (n - 1) + t + 1)
                    else:
                        pe.wait_ge(sho_read.sem, sho_read.base + 5 + t)
                    out = bank(4 + t)[:, 0:D]
                    for i in range(2):
                        pe.matmul(out, h6[0:IH, 2 * half + i, t * P:(t + 1) * P], e["dw"][:, i, :], start=(i == 0),
                                  stop=False)
                    if t == 0:
                        pe.wait_ge(mid_dve.sem, mid_dve.base + by_dve[key] + 1)
                    out6_ps.by(pe.matmul(out, adw6[0:64, t * P:(t + 1) * P], dqb6[0:64, n // 2 % 2, :], start=False,
                                         stop=True))

            turn_x(4)
            pe.wait_ge(loaded["w_ffn1"].sem, 16)
            for j in range(NT):
                pe.wait_ge(xt_sb.sem, 4 * NT + j + 1)
                for k in range(KC):
                    last = pe.matmul(bank(2)[:, j * E1:(j + 1) * E1], xt[:, k, j * P:(j + 1) * P],
                                     f1["gate"][:, k, :], start=(k == 0), stop=(k == KC - 1))
            lg6_ps.by(last)
            pe.wait_ge(wd6_ready.sem, wd6_ready.base + 1)
            for j in range(NT):
                last = pe.transpose(bank(4 + j // 4)[0:E1, (j % 4) * P:(j % 4 + 1) * P], prob6[:, j, :], ident)
                if j % 4 == 3:
                    wd6_ps.by(last)
            pe.wait_ge(wd6_sb.sem, wd6_sb.base + 2)
            pe.wait_ge(sel6_ready.sem, sel6_ready.base + 1)
            for j in range(NT):
                last = pe.matmul(bank(6)[:, j * E1:(j + 1) * E1], wd6[0:E1, j * P:(j + 1) * P], map_f[0:E1, :],
                                 start=True, stop=True)
            flat6_ps.by(last)
            pe.wait_ge(mix6_ready.sem, mix6_ready.base + 1)
            for j in range(NT):
                last = pe.transpose(bank(4 + j // 4)[0:E1, (j % 4) * P:(j % 4 + 1) * P],
                                    mix6.rearrange("p (j f) k -> p j (f k)", f=FX)[:, j, :], ident)
                if j % 4 == 3:
                    wt6_ps.by(last)
            pe.wait_ge(wt6_sb.sem, wt6_sb.base + 2)
            for n in range(2):
                for c4 in range(4):
                    gate_up(f1["shg"], f1["shu"], c4, n)
                pe.wait_ge(sh_h.sem, sh_h.base + 4 * (n + 1))
                for t in range(4):
                    if n >= 1:
                        pe.wait_ge(sho_read.sem, sho_read.base + t + 1)
                    for c4 in range(4):
                        last = pe.matmul(bank(4 + t)[:, 0:D], hs6[0:IH, c4, t * P:(t + 1) * P],
                                         f1["shd"][:, c4, :], start=(c4 == 0), stop=(c4 == 3))
                    sho_ps.by(last)
            for step in range(-1, STEPS + 1):
                if step + 1 < STEPS:
                    fuse_in(step + 1)
                if step >= 1:
                    outputs(step - 1)
                if step + 1 < STEPS:
                    ranks(step + 1)
                if 0 <= step < STEPS:
                    features(step)

        @block.scalar
        def _(act):
            def do(instruction, s=act_step):
                act.wait_ge(s.sem, s.by(instruction))

            def copy_xt(use):
                for j in range(NT):
                    t = use * NT + j
                    act.wait_ge(xt_ps.sem, t + 1)
                    xt_sb.by(act.activation(xt[:, :, j * P:(j + 1) * P],
                                            bank(t % 2)[:, 0:D].rearrange("p (k n) -> p k n", k=KC), ACT.Copy))

            def ln_sqrt(use):
                act.wait_ge(ln_var.sem, use + 1)
                ln_std.by(act.activation(std, rstd, ACT.Sqrt))

            copy_xt(0)
            for u in range(6):
                n, pair = (u // 2, u % 2) if u < 4 else (u - 4, None)
                act.wait_ge(q_ps.sem, u + 1)
                src = bank(2 + u % 2)
                at = slice(n * BANK, (n + 1) * BANK)
                if pair is None:
                    last = act.activation(kt0[0:DKV, at], src[0:DKV, :], ACT.Copy)
                else:
                    act.activation(q4[0:DKV, 8 * n:8 * n + 8, 2 * pair, :],
                                   src[0:DKV, :].rearrange("p (b s) -> p b s", s=S), ACT.Copy)
                    last = act.activation(q4[0:DKV, 8 * n:8 * n + 8, 2 * pair + 1, :],
                                          src[DKV:P, :].rearrange("p (b s) -> p b s", s=S), ACT.Copy)
                q_sb.by(last)
            act.wait_ge(loaded["w_attn0"].sem, 16)
            gate_exp.by(act.activation(gate0[:, 0:1], a0["memw"], ACT.Exp, scale=-1.0))
            act.wait_ge(elu_min.sem, 1)
            elu_exp.by(act.activation(sig[0:DKV, :, :], sig[0:DKV, :, :], ACT.Exp))
            for b in range(B):
                act.wait_ge(nmt0_ps.sem, b + 1)
                nmt0_sb.by(act.activation(q4[DKV:DKV + H0, b, :, :],
                                          bank(4)[0:H0, 0:D].rearrange("p (g s) -> p g s", g=NQ), ACT.Copy))
                act.wait_ge(b0_ps.sem, b + 1)
                if b >= 2:
                    act.wait_ge(o0_ps.sem, b - 1)
                pt0_ready.by(act.activation(pt0[:, b % 2, :, :].rearrange("p a b -> p (a b)"), bank(5, 2), ACT.Exp,
                                            scale=float(DH0) ** -0.5))
            ln_sqrt(0)

            def hi_part(u):
                for p in range(2):
                    act.wait_ge(rep_ps.sem, 2 * u + p + 1)
                    if u >= 2:
                        act.wait_ge(st_ready.sem, 2 * (u - 2) + p + 1)
                    hi_ready.by(act.activation(hi16[:, u % 2, p, :], bank(4 + 2 * (u % 2) + p), ACT.Copy))

            act.wait_ge(loaded["w_xattn0"].sem, 16)
            for u in range(2 * NT + 2):
                if u < 2 * NT:
                    act.wait_ge(pj_ps.sem, u + 1)
                    if u >= 2:
                        act.wait_ge(qr_ready.sem, u - 1)
                    pj_sb.by(act.activation(qs[:, u % 2, :], bank(u % 2)[:, 0:D], ACT.Identity,
                                            bias=x0["bk" if u < NT else "bq"]))
                if u >= 2:
                    hi_part(u - 2)

            def copy_max(b):
                act.wait_ge(nmtx_ps.sem, b + 1)
                if b >= 2:
                    act.wait_ge(bx_ps.sem, HX * (b - 1))
                for i in range(4):
                    last = act.activation(nmtx[32 * i:32 * i + HX, b % 2, :], bank(4).bitcast(BF16)[0:HX, 0:D],
                                          ACT.Copy)
                nmtx_sb.by(last)

            def copy_out(b):
                act.wait_ge(otx_ps.sem, b + 1)
                otx_sb.by(act.activation(otx[0:S, b % 2, :], bank(7)[0:S, 0:D], ACT.Copy))

            copy_max(0)
            for b in range(B):
                for h in range(HX):
                    u = b * HX + h
                    if h == 6 and b + 1 < B:
                        copy_max(b + 1)
                    if h == 2 and b >= 1:
                        copy_out(b - 1)
                    act.wait_ge(bx_ps.sem, u + 1)
                    if u >= 2:
                        act.wait_ge(pvx_done.sem, u - 1)
                    ptx_ready.by(act.activation(ptx[:, u % 2, :, :].rearrange("p a b -> p (a b)"),
                                                bank(2 + u % 2), ACT.Exp, scale=float(DHX) ** -0.5))
            copy_out(B - 1)
            ln_sqrt(1)
            copy_xt(1)
            act.wait_ge(loaded["w_route0"].sem, 16)
            b1_gelu.by(act.activation(b1g, r0["b1"], ACT.Gelu))
            for n in range(2):
                act.wait_ge(r1_ps.sem, n + 1)
                r1_sb.by(act.activation(r1[:, n * BANK:(n + 1) * BANK], bank(2 + n), ACT.Gelu))
            act.wait_ge(p_sub.sem, 1)
            p_exp.by(act.activation(prob, prob, ACT.Exp))
            for i in range(2):
                act.wait_ge(wct_ps.sem, i + 1)
                wct_sb.by(act.activation(wct[0:2 * E0, i * BANK:(i + 1) * BANK], bank(2 + i)[0:2 * E0, :],
                                         ACT.Copy))
            act.wait_ge(cer_ps.sem, 1)
            ceb_sb.by(act.activation(ceb[0:E0, :], bank(4)[0:E0, 0:D], ACT.Copy))
            for r in range(ROW_TILES):
                for n in range(2):
                    act.wait_ge(up_ps.sem, up_ps.base + 2 * r + n + 1)
                    if r >= 2:
                        act.wait_ge(hidt_ps.sem, hidt_ps.base + 2 * (r - 2) + n + 1)
                    hid_ready.by(act.activation(hid[:, r % 2, n * BANK:(n + 1) * BANK], bank(n), ACT.Gelu))
            ln_sqrt(2)
            copy_xt(2)
            for j in range(NT):
                act.wait_ge(pj1_ps.sem, j + 1)
                act.activation(qk1[:, j, :], bank(2 + 2 * (j % 2)), ACT.Copy)
                if j >= 2:
                    act.wait_ge(ss_part.sem, j - 1)
                act.activation(sq1[:, j % 2, :], bank(2 + 2 * (j % 2))[:, D:2 * D], ACT.Square)
                pj1_sb.by(act.activation(vz1[:, j, :], bank(3 + 2 * (j % 2))[:, 0:D + H1], ACT.Copy))
            act.wait_ge(pj1_sb.sem, NT)
            act.wait_ge(ss_ready.sem, 1)
            ss_std.by(act.activation(std1, rk1, ACT.Sqrt))
            bz_exp.by(act.activation(beta1, vz1[:, :, D:D + H1], ACT.Exp, scale=-1.0))
            for j in range(NT):
                for half in range(2):
                    act.wait_ge(tr1_ps.sem, 2 * j + half + 1)
                    ft_sb.by(act.activation(ft1[:, 2 * half:2 * half + 2, :, j * P:(j + 1) * P],
                                            bank(6 + half).rearrange("p (n k t) -> p n k t", n=2, k=KC), ACT.Copy))
            for w in range(2 * NT + 1):
                if w < 2 * NT:
                    act.wait_ge(sm_ready.sem, w + 1)
                    sm_exp.by(act.activation(sm1[:, w % 2, :], sm1[:, w % 2, :], ACT.Exp,
                                             scale=float(DH1) ** -0.5))
                if w >= 1:
                    act.wait_ge(pt_ps.sem, w)
                    pt_sb.by(act.activation(pt1[:, w - 1, :], bank(4 + (w - 1) % 2), ACT.Copy))
            for j in range(NT):
                act.wait_ge(ot1_ps.sem, j + 1)
                if j >= 2:
                    act.wait_ge(y1_ps.sem, j - 1)
                ot1_sb.by(act.activation(ot1[:, j % 2, :, :], bank(2 + j % 2)[:, 0:D]
                                         .rearrange("p (k t) -> p k t", k=KC), ACT.Copy))
            ln_sqrt(3)
            for j in range(NT):
                act.wait_ge(ct_ps.sem, j + 1)
                ct_sb.by(act.activation(ct5[:, :, j * P:(j + 1) * P],
                                        bank(6 + j % 2)[:, 0:D].rearrange("p (k t) -> p k t", k=KC), ACT.Copy))
            copy_xt(3)
            act.wait_ge(loaded["w_xattn1"].sem, 16)
            for u in range(8):
                n, m = u // 2 % 2, u % 2
                act.wait_ge(kq5_ps.sem, u + 1)
                dst, bias = (k5, x1["bk"]) if u < 4 else (q5, x1["bq"])
                kq5_sb.by(act.activation(dst[:, m, n * BANK:(n + 1) * BANK], bank(2 + u % 2), ACT.Identity,
                                         bias=bias[:, m:m + 1]))

            def copy_out5(j):
                act.wait_ge(ot5_ps.sem, j + 1)
                if j >= 2:
                    act.wait_ge(y5_ps.sem, j - 1)
                ot5_sb.by(act.activation(ot5[:, j % 2, :, :], bank(j % 2)[:, 0:D]
                                         .rearrange("p (k t) -> p k t", k=KC), ACT.Copy))

            for b in range(B):
                act.wait_ge(s5_ready.sem, b + 1)
                if b >= 2:
                    act.wait_ge(o5_ps.sem, b - 1)
                pt5_ready.by(act.activation(pt5[:, b % 2, :], s5[:, b % 2, :], ACT.Exp, bias=off5[:, b:b + 1]))
                if b % 2 == 1 and b >= 3:
                    copy_out5(b // 2 - 1)
            copy_out5(NT - 1)
            ln_sqrt(4)
            ln_sqrt(5)
            copy_xt(4)
            act.wait_ge(p6_sub.sem, p6_sub.base + 1)
            p6_exp.by(act.activation(prob6, prob6, ACT.Exp))
            for i in range(2):
                act.wait_ge(wd6_ps.sem, wd6_ps.base + i + 1)
                wd6_sb.by(act.activation(wd6[0:E1, i * BANK:(i + 1) * BANK], bank(4 + i)[0:E1, :], ACT.Copy))
            act.wait_ge(m6_sub.sem, m6_sub.base + 1)
            m6_exp.by(act.activation(mix6, mix6, ACT.Exp))
            for i in range(2):
                act.wait_ge(wt6_ps.sem, wt6_ps.base + i + 1)
                wt6_sb.by(act.activation(wt6[0:E1, i * BANK:(i + 1) * BANK], bank(4 + i)[0:E1, :], ACT.Copy))
            for n in range(2):
                for c4 in range(4):
                    v = (n * 4 + c4) * 2
                    act.wait_ge(sh_ps.sem, sh_ps.base + v + 1)
                    if n * 4 + c4 >= 4:
                        act.wait_ge(sh_h.sem, sh_h.base + n * 4 + c4 - 3)
                    sh_silu.by(act.activation(g6[0:IH, c4, :], bank(v % 4)[0:IH, :], ACT.Silu))
            for step in range(-1, STEPS + 1):
                n = step + 1
                if n < STEPS:
                    act.wait_ge(mid_ps.sem, mid_ps.base + ring[("w", 0), n] + 1)
                    if n >= 3:
                        act.wait_ge(mid_dve.sem, mid_dve.base + by_dve[("d", 0), n - 3] + 1)
                    mid_act.by(act.activation(we6[:, n % 3, :], bank(ring[("w", 0), n] % 4), ACT.Copy))
                n = step
                if 0 <= n < STEPS:
                    for i in range(2):
                        act.wait_ge(mid_ps.sem, mid_ps.base + ring[("g", i), n] + 1)
                        if n >= 2:
                            act.wait_ge(mid_dve.sem, mid_dve.base + by_dve[("u", i), n - 2] + 1)
                        else:
                            act.wait_ge(sh_h.sem, sh_h.base + 8)
                        mid_act.by(act.activation(g6[0:IH, 2 * (n % 2) + i, :], bank(ring[("g", i), n] % 4)[0:IH, :],
                                                  ACT.Silu))
            ln_sqrt(6)

        @block.vector
        def _(dve):
            def do(instruction, s=dve_step):
                dve.wait_ge(s.sem, s.by(instruction))

            def tile_stats(j):
                do(dve.bn_stats(stats[:, j, :], x[:, j, :]))
                do(dve.bn_aggr(mean_var[:, j, :], stats[:, j, :]))

            def normalise(use):
                do(dve.tensor_scalar(rstd, mean_var[:, :, 1], EPS, None, ALU.add), ln_var)
                dve.wait_ge(ln_std.sem, use + 1)
                do(dve.reciprocal(rstd, std))
                for j in range(NT):
                    x_norm.by(dve.tensor_scalar(x[:, j, :], x[:, j, :], mean_var[:, j, 0:1], rstd[:, j:j + 1],
                                                ALU.subtract, ALU.mult))
                dve.wait_ge(x_norm.sem, x_norm.n)

            dve.wait_ge(gate_exp.sem, 1)
            do(dve.tensor_scalar(gate0[:, 1:2], gate0[:, 0:1], 1.0, None, ALU.add))
            do(dve.reciprocal(gate0[:, 2:3], gate0[:, 1:2]))
            do(dve.tensor_scalar(gate0[:, 3:4], gate0[:, 2:3], -1.0, 1.0, ALU.mult, ALU.add))
            dve.wait_ge(q_sb.sem, 4)
            for g in range(NQ):
                last = dve.tensor_scalar(sig[0:DKV, g, :].rearrange("p (b s) -> p b s", s=S), q4[0:DKV, :, g, :], 0.0,
                                         None, ALU.min)
            do(last, elu_min)
            dve.wait_ge(pool_step.sem, 5)
            for i in range(2):
                dve.wait_ge(v_ps.sem, i + 1)
                src = bank(4 + i)[:, 0:8 * 32].rearrange("p (b c) -> p b c", c=DH0)
                dst = vb0[:, 8 * i:8 * i + 8, :, :].rearrange("p b q (r c) -> p (b q) r c", r=2)
                dve.tensor_copy(dst[0:64, :, 0, 0:DH0], src[0:64, :, :])
                do(dve.tensor_copy(dst[64:128, :, 1, 0:DH0], src[64:128, :, :]), v_sb)
            dve.wait_ge(elu_exp.sem, 1)
            flat = sig[0:DKV, :, :].rearrange("p a b -> p (a b)")
            do(dve.tensor_scalar(flat, flat, -1.0, None, ALU.add))
            for g in range(NQ):
                v = sig[0:DKV, g, :].rearrange("p (b s) -> p b s", s=S)
                last = dve.scalar_tensor_tensor(out=v, in0=q4[0:DKV, :, g, :], scalar=0.0, in1=v, op0=ALU.max,
                                                op1=ALU.add)
            do(last, elu_ready)
            for j in range(NT):
                dve.wait_ge(mem_ps.sem, j + 1)
                src = bank(6 + j % 2)[:, 0:NQ * 65].rearrange("p (g c) -> p g c", g=NQ)
                do(dve.reciprocal(rm0, src[:, :, DKV]))
                do(dve.tensor_tensor(out=am[:, j, :].rearrange("p (g c) -> p g c", g=NQ), in0=src[:, :, 0:DKV],
                                     in1=wide(rm0, 2, DKV), op=ALU.mult), mem_read)
            for b in range(B + 1):
                if b < B:
                    for pair in range(2):
                        dve.wait_ge(a0_ps.sem, 2 * b + pair + 1)
                        if b >= 2:
                            dve.wait_ge(nmt0_ps.sem, b - 1)
                        a0_max.by(dve.tensor_reduce(
                            nm0[:, b % 2, pair, :], bank(2 * (b % 2) + pair).rearrange("p (h t) -> p h t", h=H0),
                            AX.X, ALU.max, negate=True))
                if b >= 2 and b % 2 == 0:
                    j = b // 2 - 1
                    dve.wait_ge(o0_ps.sem, b)
                    src = bank(7)[:, 0:NQ * H0 * 9].rearrange("p (h c) -> p h c", c=9)
                    do(dve.reciprocal(rs0, src[:, :, DH0]))
                    do(dve.tensor_tensor(out=t0, in0=src[:, :, 0:DH0], in1=wide(rs0, 2, DH0), op=ALU.mult), o0_read)
                    do(dve.scalar_tensor_tensor(out=x[:, j, :], in0=t0.rearrange("p a b -> p (a b)"),
                                                scalar=gate0[:, 3:4], in1=x[:, j, :], op0=ALU.mult, op1=ALU.add))
                    do(dve.scalar_tensor_tensor(out=x[:, j, :], in0=am[:, j, :], scalar=gate0[:, 2:3],
                                                in1=x[:, j, :], op0=ALU.mult, op1=ALU.add))
                    tile_stats(j)
            normalise(0)

            dve.wait_ge(loaded["w_xattn0"].sem, 16)
            dve.wait_ge(selm_ready.sem, 1)
            do(dve.tensor_copy(ident16, c["ident"]), selm_ready)
            for j in range(NT):
                for p in range(2):
                    dve.wait_ge(vx_ps.sem, 2 * j + p + 1)
                    do(dve.tensor_tensor(
                        out=vx[:, 2 * j + p, :, :, 0:DHX],
                        in0=bank(2 * (j % 2) + p)[:, 0:2 * S].rearrange("p (s h c) -> p s h c", s=2, h=HX),
                        in1=wide(x0["bv"].rearrange("p (h c) -> p h c", h=HX), 1, 2), op=ALU.add), vx_sb)
            for u in range(2 * NT + 1):
                if u < 2 * NT:
                    dve.wait_ge(pj_sb.sem, u + 1)
                    do(dve.tensor_tensor(out=rope_a[:, u % 2, :], in0=qs[:, u % 2, :], in1=c["cosx"], op=ALU.mult))
                    dve.wait_ge(rot_ps.sem, u + 1)
                    do(dve.tensor_tensor(out=rope_b[:, u % 2, :], in0=bank(2 + u % 2)[:, 0:D], in1=c["sinx"],
                                         op=ALU.mult))
                    if u >= 2:
                        dve.wait_ge(rep_ps.sem, 2 * (u - 1))
                    do(dve.tensor_tensor(out=qr[:, u % 2, :], in0=rope_a[:, u % 2, :], in1=rope_b[:, u % 2, :],
                                         op=ALU.add), qr_ready)
                if u >= 1:
                    v = u - 1
                    side, j = ("k", v) if v < NT else ("q", v - NT)
                    for p in range(2):
                        dve.wait_ge(hi_ready.sem, 2 * v + p + 1)
                        do(dve.scalar_tensor_tensor(
                            out=stack[side][:, 2 * j + p, :, :].rearrange("p a b -> p (a b)"),
                            in0=hi16[:, v % 2, p, :], scalar=c["lo_" + side], in1=bank(4 + 2 * (v % 2) + p),
                            op0=ALU.mult, op1=ALU.add), st_ready)

            def row_max(b, h):
                u = b * HX + h
                dve.wait_ge(ax_ps.sem, u + 1)
                ax_max.by(dve.tensor_reduce(nmx[:, b % 2, :, h], bank(u % 2).rearrange("p (t s) -> p t s", t=2),
                                            AX.X, ALU.max, negate=True))

            def cast_max(b):
                dve.wait_ge(ax_max.sem, HX * (b + 1))
                if b >= 2:
                    dve.wait_ge(nmtx_ps.sem, b - 1)
                do(dve.tensor_copy(nmxb[:, b % 2, :, :], nmx[:, b % 2, :, :]), nmx_ready)

            def divide_x(b):
                dve.wait_ge(pvx_done.sem, HX * (b + 1))
                src = bank(5 + b % 2)[:, 0:18 * HX].rearrange("p (t c) -> p t c", c=9)
                r = rsx[:, b % 2, :, :].rearrange("p a b -> p (a b)")
                do(dve.reciprocal(r, src[:, :, DHX]))
                if b >= 2:
                    dve.wait_ge(otx_ps.sem, b - 1)
                do(dve.tensor_tensor(out=onx[:, b % 2, :, :].rearrange("p t (h c) -> p (t h) c", c=DHX),
                                     in0=src[:, :, 0:DHX], in1=wide(r, 2, DHX), op=ALU.mult), onx_ready)

            def add_x(b):
                j, half = b // 2, slice(64 * (b % 2), 64 * (b % 2) + 64)
                dve.wait_ge(yx_ps.sem, b + 1)
                do(dve.scalar_tensor_tensor(out=x[half, j, :], in0=bank(7)[half, D:2 * D],
                                            scalar=x0["bo"][half, :], in1=x[half, j, :], op0=ALU.add,
                                            op1=ALU.add), yx_read)
                if b % 2:
                    tile_stats(j)

            for h in range(HX):
                row_max(0, h)
            cast_max(0)
            for b in range(B):
                for h in range(HX):
                    if b + 1 < B:
                        for n in a_steps()[h]:
                            row_max(b + 1, n)
                        if h == 5:
                            cast_max(b + 1)
                    if h == 1 and b >= 1:
                        divide_x(b - 1)
                    if h == 6 and b >= 1:
                        add_x(b - 1)
            divide_x(B - 1)
            add_x(B - 1)
            normalise(1)
            def softmax_rows(logits, out, peak, exp_in, exp_out):
                width = out.shape[2]
                do(dve.tensor_reduce(peak, logits, AX.X, ALU.max))
                do(dve.tensor_tensor(out=out, in0=logits, in1=wide(peak, 2, width), op=ALU.subtract), exp_in)
                dve.wait_ge(exp_out.sem, exp_out.base + 1)
                do(dve.tensor_reduce(peak, out, AX.X, ALU.add))
                do(dve.reciprocal(peak, peak))
                do(dve.tensor_tensor(out=out, in0=out, in1=wide(peak, 2, width), op=ALU.mult))

            def mark_top(p, count, value, reset, out, tie, rank, more):
                width, flat = p.shape[2], "p a b -> p (a b)"
                tie3, rank3, out3 = (t.rearrange("p (a b) -> p a b", b=width) for t in (tie, rank, out))
                do(dve.tensor_tensor(out=out3, in0=p, in1=wide(value, 2, width), op=ALU.is_gt))
                do(dve.tensor_reduce(more, out3, AX.X, ALU.add))
                do(dve.tensor_scalar(more, more, -1.0, float(count), ALU.mult, ALU.add))
                do(dve.tensor_tensor(out=tie3, in0=p, in1=wide(value, 2, width), op=ALU.is_equal))
                do(dve.tensor_tensor_scan(rank, reset, tie, 0.0, ALU.mult, ALU.add))
                do(dve.tensor_tensor(out=rank3, in0=rank3, in1=wide(more, 2, width), op=ALU.is_le))
                do(dve.tensor_tensor(out=tie, in0=tie, in1=rank, op=ALU.mult))
                do(dve.tensor_tensor(out=out, in0=out, in1=tie, op=ALU.add))

            dve.wait_ge(lg_ps.sem, 1)
            softmax_rows(bank(4)[:, 0:NT * E0].rearrange("p (a b) -> p a b", b=E0), prob, pmax, p_sub, p_exp)
            for j in range(NT):
                last = dve.max(top8[:, j, :], prob[:, j, :])
            do(last)
            mark_top(prob, 1, top8[:, :, 0], c["reset8"], first, tie, rank, more)
            mark_top(prob, 2, top8[:, :, 1], c["reset8"], both, tie, rank, more)
            first3, both3 = (t.rearrange("p (a b) -> p a b", b=E0) for t in (first, both))
            dve.tensor_tensor(out=gates, in0=prob, in1=both3, op=ALU.mult)
            dve.tensor_copy(marks[:, :, 0:E0], first3)
            dve.tensor_tensor(out=marks[:, :, E0:2 * E0], in0=both3, in1=first3, op=ALU.subtract)
            do(dve.memset(earlier[:, 0, :], 0.0))
            for j in range(1, NT):
                last = dve.tensor_tensor(out=earlier[:, j, :], in0=earlier[:, j - 1, :], in1=both3[:, j - 1, :],
                                         op=ALU.add)
                do(last, dve_step if j < NT - 1 else marks_ready)
            dve.wait_ge(cnt_ps.sem, 1)
            counts = bank(5)[:, 0:2 * E0]
            do(dve.tensor_reduce(count0, counts.rearrange("p (s e) -> p e s", s=2), AX.X, ALU.add))
            do(dve.tensor_tensor(out=over0, in0=wide(count0, 2, NT), in1=wide(c["full_tiles"], 1, E0),
                                 op=ALU.is_gt))
            do(dve.tensor_reduce(tiles0, over0, AX.X, ALU.add))
            do(dve.tensor_tensor_scan(end0, c["ones"][:, 0:E0], tiles0, 0.0, ALU.mult, ALU.add))
            do(dve.tensor_tensor(out=row0, in0=end0, in1=tiles0, op=ALU.subtract))
            do(dve.tensor_scalar(row0, row0, float(P), None, ALU.mult))
            do(dve.tensor_tensor(out=place, in0=bank(6)[:, 0:NT * E0].rearrange("p (j e) -> p j e", e=E0),
                                 in1=wide(row0, 1, NT), op=ALU.add))
            do(dve.tensor_tensor(out=placed.rearrange("p j (s e) -> p j s e", s=2),
                                 in0=marks.rearrange("p j (s e) -> p j s e", s=2), in1=wide(place, 2, 2),
                                 op=ALU.mult))
            do(dve.tensor_reduce(slot_row, placed.rearrange("p j (s e) -> p (j s) e", s=2), AX.X, ALU.add))
            do(dve.tensor_copy(slot_row_i, slot_row), place_ready)
            do(dve.tensor_tensor(out=past, in0=wide(c["tile_no"], 2, E0 - 1), in1=wide(end0[:, 0:E0 - 1], 1, ROW_TILES),
                                 op=ALU.is_ge))
            do(dve.tensor_reduce(tile_e, past, AX.X, ALU.add))
            do(dve.tensor_copy(tile_e_i, tile_e), tiles_ready)
            do(dve.tensor_scalar(active, counts, 1.0, None, ALU.min))
            for slot in range(2):
                last = dve.tensor_tensor(out=(slot_a, level0)[slot],
                                         in0=wide(active[:, slot * E0:(slot + 1) * E0], 1, NT),
                                         in1=wide(top8[:, :, slot], 2, E0), op=ALU.mult)
            do(last)
            do(dve.tensor_tensor(out=weight_c[:, :, E0:2 * E0], in0=slot_a, in1=level0, op=ALU.add))
            do(dve.tensor_tensor(out=weight_c[:, :, 0:E0], in0=weight_c[:, :, E0:2 * E0], in1=gates,
                                 op=ALU.subtract), wc_ready)
            dve.wait_ge(ce_ps.sem, 1)
            do(dve.tensor_copy(cet, bank(7)[:, 0:KC * E0]), cet_sb)

            def copy_rows(r):
                dve.wait_ge(xst_ps.sem, xst_ps.base + r + 1)
                if r >= 2:
                    dve.wait_ge(up_ps.sem, up_ps.base + 2 * (r - 1))
                xst_sb.by(dve.tensor_copy(xst[:, r % 2, :, :].rearrange("p k t -> p (k t)"), bank(6 + r % 2)[:, 0:D]))

            copy_rows(0)
            for r in range(ROW_TILES + 2):
                if r + 1 < ROW_TILES:
                    copy_rows(r + 1)
                if 1 <= r <= ROW_TILES:
                    for n in range(2):
                        dve.wait_ge(hidt_ps.sem, hidt_ps.base + 2 * (r - 1) + n + 1)
                        if r >= 3:
                            dve.wait_ge(down_ps.sem, down_ps.base + r - 2)
                        hidt_sb.by(dve.tensor_copy(hidt[:, (r - 1) % 2, n * BANK:(n + 1) * BANK], bank(2 + n)))
                if r >= 2:
                    dve.wait_ge(down_ps.sem, down_ps.base + r - 1)
                    if r >= 4:
                        dve.wait_ge(ys_out[r % 2].sem, ys_out[r % 2].base + 16 * (r // 2 - 1))
                    ys_ready.by(dve.tensor_copy(ys[:, r % 2, :], bank(4 + r % 2)[:, 0:D]))
            for j in range(NT):
                dve.wait_ge(const_ps.sem, j + 1)
                do(dve.tensor_tensor(out=x[:, j, :], in0=bank(j % 2)[:, 0:D], in1=x[:, j, :], op=ALU.add),
                   const_read)
            for n in range(2 * NT):
                j, slot = divmod(n, 2)
                dve.wait_ge(back_in.sem, 16 * 2 * NT)
                do(dve.scalar_tensor_tensor(out=x[:, j, :], in0=back[:, n, :], scalar=top8[:, j, slot:slot + 1],
                                            in1=x[:, j, :], op0=ALU.mult, op1=ALU.add))
                if slot:
                    tile_stats(j)
            normalise(2)
            for j in range(NT):
                dve.wait_ge(pj1_sb.sem, j + 1)
                do(dve.tensor_reduce(rk1[:, j, :], sq1[:, j % 2, :].rearrange("p (h c) -> p h c", c=DH1), AX.X,
                                     ALU.add), ss_part)
            do(dve.tensor_scalar(rk1, rk1, 1e-6, None, ALU.add), ss_ready)
            dve.wait_ge(ss_std.sem, 1)
            do(dve.reciprocal(rk1, std1))
            dve.wait_ge(bz_exp.sem, 1)
            do(dve.tensor_scalar(beta1, beta1, 1.0, None, ALU.add))
            do(dve.reciprocal(beta1, beta1))
            do(dve.tensor_scalar(beta1, beta1, 2.0, None, ALU.mult))
            half = DH1 // 2
            for j in range(NT):
                src, ta, tb = (v.rearrange("p (h c) -> p h c", c=DH1) for v in (qk1[:, j, :], turn_a, turn_b))
                dve.tensor_tensor(out=ta, in0=src, in1=wide(c["cos1"], 1, 2 * H1), op=ALU.mult)
                dve.tensor_tensor(out=tb[:, :, 0:half], in0=src[:, :, half:DH1],
                                  in1=wide(c["sin1"][:, 0:half], 1, 2 * H1), op=ALU.mult)
                do(dve.tensor_tensor(out=tb[:, :, half:DH1], in0=src[:, :, 0:half],
                                     in1=wide(c["sin1"][:, half:DH1], 1, 2 * H1), op=ALU.mult))
                if j >= 2:
                    dve.wait_ge(tr1_ps.sem, 2 * (j - 1))
                do(dve.tensor_tensor(out=rq1[:, j % 2, :], in0=turn_a, in1=turn_b, op=ALU.add))
                key = rq1[:, j % 2, D:2 * D].rearrange("p (h c) -> p h c", c=DH1)
                do(dve.tensor_tensor(out=key, in0=key, in1=wide(rk1[:, j, :], 2, DH1), op=ALU.mult))
                do(dve.tensor_tensor(out=kw1[:, j % 2, :].rearrange("p (h c) -> p h c", c=DH1), in0=key,
                                     in1=wide(beta1[:, j, :], 2, DH1), op=ALU.mult), turned1)
            for w in range(2 * NT):
                dve.wait_ge(a1_ps.sem, w + 1)
                if w >= 2:
                    dve.wait_ge(pt_ps.sem, w - 1)
                sm = sm1[:, w % 2, :].rearrange("p (h t) -> p h t", t=S)
                do(dve.tensor_tensor(out=sm, in0=bank(2 + w % 2).rearrange("p (h t) -> p h t", t=S),
                                     in1=wide(c["causal"], 1, 8), op=ALU.add))
                do(dve.tensor_reduce(mx1[:, w % 2, :], sm, AX.X, ALU.max))
                do(dve.tensor_tensor(out=sm, in0=sm, in1=wide(mx1[:, w % 2, :], 2, S), op=ALU.subtract), sm_ready)
            do(dve.memset(state1.rearrange("p a b c -> p (a b c)"), 0.0))
            dve.wait_ge(bh_in.sem, 16 * 3 * B)
            for i in range(S):
                at = lambda n: bh1[n][:, :, :, i]
                do(dve.tensor_tensor(out=outer1, in0=state1, in1=wide(at(0), 2, DH1), op=ALU.mult))
                do(dve.tensor_reduce(seen1, outer1, AX.X, ALU.add))
                last = dve.tensor_tensor(out=vn1[:, :, :, i], in0=at(2), in1=seen1, op=ALU.subtract)
                if i == S - 1:
                    do(last, regressed)
                    break
                do(last)
                do(dve.tensor_tensor(out=outer1, in0=wide(vn1[:, :, :, i], 3, DH1), in1=wide(at(1), 2, DH1),
                                     op=ALU.mult))
                do(dve.tensor_tensor(out=state1, in0=state1, in1=outer1, op=ALU.add))
            for i in range(4):
                dve.wait_ge(vb1_ps.sem, i + 1)
                dve.wait_ge(blank1.sem, 3)
                src = bank(6 + i % 2).rearrange("p (q c) -> p q c", c=DH1)
                dst = vb1[:, 4 * i:4 * i + 4, :, :].rearrange("p b q (r c) -> p (b q) r c", r=2)
                dve.tensor_copy(dst[0:64, :, 0, 0:DH1], src[0:64, :, :])
                do(dve.tensor_copy(dst[64:128, :, 1, 0:DH1], src[64:128, :, :]), vb1_sb)

            def divide1(j):
                dve.wait_ge(o1_ps.sem, j + 1)
                src = bank(j % 2)[:, 0:H1 * 17].rearrange("p (h c) -> p h c", c=17)
                do(dve.reciprocal(rs1[:, j % 2, :], src[:, :, DH1]))
                if j >= 2:
                    dve.wait_ge(ot1_ps.sem, j - 1)
                do(dve.tensor_tensor(out=on1[:, j % 2, :].rearrange("p (h c) -> p h c", c=DH1),
                                     in0=src[:, :, 0:DH1], in1=wide(rs1[:, j % 2, :], 2, DH1), op=ALU.mult),
                   on1_ready)

            def add1(j):
                dve.wait_ge(y1_ps.sem, j + 1)
                do(dve.tensor_tensor(out=x[:, j, :], in0=bank(4 + j % 2)[:, 0:D], in1=x[:, j, :], op=ALU.add),
                   y1_read)
                tile_stats(j)

            for j in range(NT + 1):
                if j < NT:
                    divide1(j)
                if j >= 1:
                    add1(j - 1)
            normalise(3)
            dve.wait_ge(mask_in.sem, 16)
            dve.wait_ge(loaded["w_xattn1"].sem, 16)
            do(dve.tensor_scalar(attend5, mask5, 0.5, None, ALU.is_gt))
            do(dve.tensor_scalar(off5, attend5, 50.0, -50.0, ALU.mult, ALU.add))
            do(dve.tensor_scalar(scale5[:, 0:1], x1["scale"], 0.0, 0.3, ALU.max, ALU.min))
            dve.wait_ge(blank5.sem, 3)
            for i in range(4):
                dve.wait_ge(v5_ps.sem, i + 1)
                for r in range(2):
                    rows = slice(64 * r, 64 * r + 64)
                    last = dve.tensor_tensor(
                        out=vb5[rows, 4 * i:4 * i + 4, :, 17 * r:17 * r + DH1],
                        in0=bank(4 + i % 2)[rows, :].rearrange("p (b q c) -> p b q c", b=4, c=DH1),
                        in1=wide(x1["bv"][rows, :].rearrange("p (q r c) -> p q r c", r=2, c=DH1)[:, :, r, :], 1, 4),
                        op=ALU.add)
                do(last, v5_sb)

            def divide5(j):
                dve.wait_ge(o5_ps.sem, 2 * j + 2)
                src = bank(6 + j % 2)[:, 0:H1 * 17].rearrange("p (h c) -> p h c", c=17)
                r = rs5[:, j % 2, :]
                do(dve.tensor_scalar(r, src[:, :, DH1], 1.0 + 1e-8, None, ALU.mult))
                do(dve.reciprocal(r, r))
                if j >= 2:
                    dve.wait_ge(ot5_ps.sem, j - 1)
                do(dve.tensor_tensor(out=on5[:, j % 2, :].rearrange("p (h c) -> p h c", c=DH1),
                                     in0=src[:, :, 0:DH1], in1=wide(r, 2, DH1), op=ALU.mult), on5_ready)

            def delta_stats(j):
                dve.wait_ge(y5_ps.sem, j + 1)
                do(dve.tensor_tensor(out=delta5[:, j, :], in0=bank(2 + j % 2)[:, 0:D], in1=x1["bo"], op=ALU.add),
                   y5_read)
                do(dve.tensor_scalar(delta5[:, j, :], delta5[:, j, :], scale5[:, 0:1], None, ALU.mult))
                do(dve.bn_stats(stats[:, j, :], delta5[:, j, :]))
                do(dve.bn_aggr(mean_var[:, j, :], stats[:, j, :]))

            for b in range(B):
                dve.wait_ge(b5_ps.sem, b + 1)
                if b >= 2:
                    dve.wait_ge(pt5_ready.sem, b - 1)
                do(dve.tensor_scalar(s5[:, b % 2, :], bank(4 + b % 2), float(DH1) ** -0.5, 50.0, ALU.mult, ALU.min))
                do(dve.tensor_scalar(s5[:, b % 2, :], s5[:, b % 2, :], -50.0, attend5[:, b:b + 1], ALU.max,
                                     ALU.mult), s5_ready)
                if b % 2 == 0 and b >= 2:
                    divide5(b // 2 - 1)
                if b % 2 == 0 and b >= 6:
                    delta_stats(b // 2 - 3)
            divide5(NT - 1)
            for j in range(NT - 3, NT):
                delta_stats(j)
            do(dve.tensor_scalar(rstd, mean_var[:, :, 1], EPS, None, ALU.add), ln_var)
            dve.wait_ge(ln_std.sem, 5)
            do(dve.reciprocal(rstd, std))
            for j in range(NT):
                do(dve.tensor_scalar(delta5[:, j, :], delta5[:, j, :], mean_var[:, j, 0:1], rstd[:, j:j + 1],
                                     ALU.subtract, ALU.mult))
                do(dve.tensor_tensor(out=delta5[:, j, :], in0=delta5[:, j, :], in1=x1["gamma"], op=ALU.mult))
                do(dve.tensor_tensor(out=delta5[:, j, :], in0=delta5[:, j, :], in1=x1["beta"], op=ALU.add))
                do(dve.tensor_tensor(out=x[:, j, :], in0=x[:, j, :], in1=delta5[:, j, :], op=ALU.add))
                tile_stats(j)
            normalise(5)
            dve.wait_ge(lg6_ps.sem, lg6_ps.base + 1)
            softmax_rows(bank(2).rearrange("p (a b) -> p a b", b=E1), prob6, peak6[:, 0:NT], p6_sub, p6_exp)
            for j in range(NT):
                do(dve.max(top6[:, j, :], prob6[:, j, :]))
            mark_top(prob6, TOP1, top6[:, :, TOP1 - 1], c["reset64"], mark6, tie6, rank6, more6)
            do(dve.tensor_tensor(out=prob6, in0=prob6, in1=mark6.rearrange("p (a b) -> p a b", b=E1), op=ALU.mult),
               wd6_ready)
            dve.wait_ge(map_in.sem, 16)
            do(dve.tensor_scalar(map_f[0:E1, :], map_i[0:E1, :], c["row"][0:E1, :], None, ALU.is_equal), sel6_ready)
            dve.wait_ge(flat6_ps.sem, flat6_ps.base + 1)
            do(dve.tensor_copy(flat6, bank(6).rearrange("p (a b) -> p a b", b=KX)))
            do(dve.tensor_reduce(total6, flat6, AX.X, ALU.add))
            do(dve.tensor_scalar(mix6, flat6, 0.0, -1e9, ALU.is_equal, ALU.mult))
            do(dve.tensor_tensor(out=flat6, in0=flat6, in1=mix6, op=ALU.add))
            softmax_rows(flat6, mix6, peak6, m6_sub, m6_exp)
            mix6_ready.by(dve.tensor_copy(flat6, mix6))
            for n in range(2):
                for c4 in range(4):
                    v = (n * 4 + c4) * 2 + 1
                    dve.wait_ge(sh_ps.sem, sh_ps.base + v + 1)
                    dve.wait_ge(sh_silu.sem, sh_silu.base + n * 4 + c4 + 1)
                    if n >= 1:
                        dve.wait_ge(sho_ps.sem, sho_ps.base + 4)
                    do(dve.tensor_tensor(out=hs6[0:IH, c4, :], in0=g6[0:IH, c4, :], in1=bank(v % 4)[0:IH, :],
                                         op=ALU.mult), sh_h)
                for t in range(4):
                    j = 4 * n + t
                    dve.wait_ge(sho_ps.sem, sho_ps.base + j + 1)
                    do(dve.tensor_tensor(out=x[:, j, :], in0=bank(4 + t)[:, 0:D], in1=x[:, j, :], op=ALU.add),
                       sho_read)
            for step in range(-1, STEPS + 1):
                n = step + 1
                if n < STEPS:
                    f, half = n // 2, n % 2
                    if half == 0:
                        dve.wait_ge(experts_in[f % 2].sem, 16 * (f // 2 + 1))
                        if f >= 2:
                            dve.wait_ge(out6_ps.sem, out6_ps.base + NT * (f - 1))
                        do(dve.tensor_tensor(out=qb6[:, f % 2, :], in0=ex[f % 2]["qb"], in1=ex[f % 2]["qs"],
                                             op=ALU.mult), qb6_ready)
                        do(dve.tensor_tensor(out=dqb6[0:64, f % 2, :], in0=ex[f % 2]["dqb"],
                                             in1=ex[f % 2]["ds"][0:64, :], op=ALU.mult), qb6_ready)
                    for k in range(KC):
                        dve.wait_ge(mid_ps.sem, mid_ps.base + ring[("x", k), n] + 1)
                        if n >= 2:
                            dve.wait_ge(mid_ps.sem, mid_ps.base + ring[("u", 1), n - 2] + 1)
                        do(dve.tensor_tensor(out=xe6[:, half, k, :], in0=bank(ring[("x", k), n] % 4),
                                             in1=xt[:, k, half * BANK:(half + 1) * BANK], op=ALU.add), mid_dve)
                m = step - 1
                if m >= 0:
                    dve.wait_ge(mid_ps.sem, mid_ps.base + ring[("d", 0), m] + 1)
                    if m >= 1:
                        dve.wait_ge(out6_ps.sem, out6_ps.base + 4 * m)
                    do(dve.tensor_tensor(out=adw6[0:64, :], in0=bank(ring[("d", 0), m] % 4)[0:64, :],
                                         in1=we6[0:64, m % 3, :], op=ALU.mult), mid_dve)
                    for t in range(4):
                        j = 4 * (m % 2) + t
                        dve.wait_ge(out6_ps.sem, out6_ps.base + 4 * m + t + 1)
                        do(dve.scalar_tensor_tensor(out=x[:, j, :], in0=bank(4 + t)[:, 0:D],
                                                    scalar=total6[:, j * FX + m // 2:j * FX + m // 2 + 1],
                                                    in1=x[:, j, :], op0=ALU.mult, op1=ALU.add), out6_read)
                        if m >= STEPS - 2:
                            tile_stats(j)
                if n < STEPS:
                    dve.wait_ge(mid_ps.sem, mid_ps.base + ring[("a", 0), n] + 1)
                    dve.wait_ge(mid_act.sem, mid_act.base + by_act[("w", 0), n] + 1)
                    do(dve.tensor_tensor(out=aw6[:, n % 2, :], in0=bank(ring[("a", 0), n] % 4),
                                         in1=we6[:, n % 3, :], op=ALU.mult), mid_dve)
                n = step
                if 0 <= n < STEPS:
                    for i in range(2):
                        dve.wait_ge(mid_ps.sem, mid_ps.base + ring[("u", i), n] + 1)
                        dve.wait_ge(mid_act.sem, mid_act.base + by_act[("g", i), n] + 1)
                        if n >= 2:
                            dve.wait_ge(out6_ps.sem, out6_ps.base + 4 * (n - 1))
                        do(dve.tensor_tensor(out=h6[0:IH, 2 * (n % 2) + i, :], in0=g6[0:IH, 2 * (n % 2) + i, :],
                                             in1=bank(ring[("u", i), n] % 4)[0:IH, :], op=ALU.mult), mid_dve)
            normalise(6)

        for name, s in renamed:
            assert s.before.n == s.base, name


def constants():
    i, n = np.arange, np.float32
    r = i(P)
    k = {}
    k["ident"] = np.eye(P, dtype=n)
    k["ones"] = np.ones((P, P), n)
    head = np.concatenate([i(DKV) // DH0, i(H0)])
    k["headmask0"] = (head[:, None] == i(H0)).astype(n)
    k["headmask1"] = (r[:, None] // DH1 == i(8)).astype(n)
    inv = (n(1) / n(10000) ** (i(0, DHX, 2).astype(n) / n(DHX))).astype(n)
    angle = i(D).astype(n)[None, :] * inv[r % 4][:, None]
    k["cosx"], k["sinx"] = np.cos(angle), np.sin(angle)
    turn = np.zeros((P, P), n)
    low = r % 8 < 4
    turn[np.where(low, r + 4, r - 4), r] = np.where(low, -1, 1)
    k["rotx"] = turn
    ch, col = i(S)[:, None], i(P)[None, :]
    rep = np.stack([(ch == (g * 4 + col // 32) * 8 + col % 8) for g in range(2)], 1).astype(n)
    k["rep"] = np.concatenate([rep, rep])
    term = r % 32 // 8
    k["lo_q"] = -(term >= 2).astype(n)[:, None]
    k["lo_k"] = -(term % 2 == 1).astype(n)[:, None]
    k["selmax"] = np.broadcast_to((r[:, None, None] % 32 == i(HX)[None, :, None]), (P, HX, P)).astype(n)
    inv = (n(1) / n(10000) ** (i(0, DH1, 2).astype(n) / n(DH1))).astype(n)
    angle = (r % S).astype(n)[:, None] * np.concatenate([inv, inv])[None, :]
    k["cos1"] = np.cos(angle)
    k["sin1"] = np.sin(angle) * np.where(i(DH1) < DH1 // 2, -1, 1)
    k["causal"] = np.where(i(S)[None, :] > (r % S)[:, None], -1e30, 0)
    k["reset8"] = np.broadcast_to(i(NT * E0) % E0 != 0, (P, NT * E0))
    k["reset64"] = np.broadcast_to(i(NT * E1) % E1 != 0, (P, NT * E1))
    k["row"] = r[:, None]
    k["b1_rows"] = r[:, None] % 32 == i(E0)[None, :]
    k["before"] = r[:, None] < r[None, :]
    k["full_tiles"] = np.broadcast_to(P * i(NT), (P, NT))
    k["tile_no"] = np.broadcast_to(i(ROW_TILES), (P, ROW_TILES))
    k["spread"] = np.stack([i(E1)[:, None] == f * KX + col % E1 // RX for f in range(FX)], 1)
    return k


def packed(parts, arrays):
    out = []
    for name, rows, shape in parts:
        part = np.asarray(arrays[name], dtype=np.float32).reshape(rows, -1)
        out.append(np.concatenate([part, np.zeros((P - rows, part.shape[1]), np.float32)]))
    return np.ascontiguousarray(np.concatenate(out, 1))


def chunks(w, rows=P):
    return w.reshape(-1, rows, w.shape[1]).transpose(1, 0, 2)


def every(v):
    return np.broadcast_to(np.reshape(v, (1, -1)), (P, np.size(v)))


def kernel(**inputs):
    import concourse.bacc as _bacc
    from concourse.bass_utils import run_bass_kernel_spmd as _run

    g = {k: np.asarray(v) for k, v in inputs.items()}
    twice = lambda w: np.concatenate([w, w])

    def two_blocks(w):
        z = np.zeros_like(w)
        return np.block([[w, z], [z, w]])

    w = {"consts": packed(PACKS["consts"], constants())}
    w["w_attn0"] = packed(PACKS["w_attn0"], {
        "wq": chunks(g["L0_attn_Wq"].T), "wk": chunks(g["L0_attn_Wk"].T), "wv": chunks(g["L0_attn_Wv"].T),
        "mem": np.concatenate([g["L0_attn_memory"], g["L0_attn_memory_norm"]], 1),
        "memw": every(g["L0_attn_memory_weight"])})
    w["w_xattn0"] = packed(PACKS["w_xattn0"], {
        "wq": two_blocks(g["L0_xattn_Wq"].T), "wk": two_blocks(g["L0_xattn_Wk"].T),
        "wv": twice(g["L0_xattn_Wv"].T), "wo": g["L0_xattn_Wo"].T, "bq": twice(g["L0_xattn_bq"]),
        "bk": twice(g["L0_xattn_bk"]), "bo": twice(g["L0_xattn_bo"]), "bv": every(g["L0_xattn_bv"])})
    w["w_route0"] = packed(PACKS["w_route0"], {
        "rw1": chunks(g["L0_ffn_rw1"]), "rw2": g["L0_ffn_rw2"],
        "b1": g["L0_ffn_b1"].reshape(E0, IC0, P).transpose(2, 0, 1)})
    w["b1"], w["b2"] = g["L0_ffn_b1"], g["L0_ffn_b2"]
    w["w_attn1"] = packed(PACKS["w_attn1"], {
        "wqk": chunks(np.concatenate([g["L1_attn_Wq"], g["L1_attn_Wk"]], 1)),
        "wvb": chunks(np.concatenate([g["L1_attn_Wv"], g["L1_attn_Wb"]], 1)), "wo": chunks(g["L1_attn_Wo"])})
    w["w_xattn1"] = packed(PACKS["w_xattn1"], {
        "wq": chunks(g["L1_xattn_Wq"].T), "wk": chunks(g["L1_xattn_Wk"].T), "wv": chunks(g["L1_xattn_Wv"].T),
        "wo": chunks(g["L1_xattn_Wo"].T), "bq": g["L1_xattn_bq"].reshape(KC, P).T,
        "bk": g["L1_xattn_bk"].reshape(KC, P).T, "bv": every(g["L1_xattn_bv"]), "bo": every(g["L1_xattn_bo"]),
        "gamma": every(g["L1_xattn_ln_gamma"]), "beta": every(g["L1_xattn_ln_beta"]),
        "scale": every(g["L1_xattn_residual_scale"])})
    fx = {k[8:-4] if False else k: v for k, v in g.items()}
    mask_up = np.zeros((FX, KX, FX, D), np.float32)
    for f in range(FX):
        mask_up[f, :, f, :] = g["L1_ffn_mask_up_W"][f].T
    w["w_ffn1"] = packed(PACKS["w_ffn1"], {
        "gate": chunks(g["L1_ffn_gate_weight"].T), "mask_up": mask_up, "shg": chunks(g["L1_ffn_sh_gate_W"].T),
        "shu": chunks(g["L1_ffn_sh_up_W"].T), "shd": chunks(g["L1_ffn_sh_down_W"].T, IH)})

    def rank(name, f):
        return g[name][f].reshape(KX * RX, -1).T

    def unrank(name, f):
        return g[name][f].transpose(0, 2, 1).reshape(KX * RX, -1)

    w["experts"] = np.stack([packed(EXPERT, {
        "gw": chunks(g["L1_ffn_gate_W"][f].T), "uw": chunks(g["L1_ffn_up_W"][f].T),
        "qa": chunks(np.concatenate([rank("L1_ffn_gate_qa", f), rank("L1_ffn_up_qa", f)], 1)),
        "qb": np.concatenate([unrank("L1_ffn_gate_qb", f), unrank("L1_ffn_up_qb", f)]),
        "qs": np.concatenate([np.broadcast_to(g["L1_ffn_gate_scale"][f], (E1, I1)),
                              np.broadcast_to(g["L1_ffn_up_scale"][f], (E1, I1))]),
        "dw": chunks(g["L1_ffn_down_W"][f].T, IH), "dqa": chunks(rank("L1_ffn_down_qa", f), IH),
        "dqb": unrank("L1_ffn_down_qb", f), "ds": every(g["L1_ffn_down_scale"][f])}) for f in range(FX)])
    w["x"] = g["x"].reshape(B * S, D)
    w["ctx"] = g["ctx_2048"].reshape(B * S, D)
    w["w1"] = g["L0_ffn_w1"].reshape(E0, KC, P, I0).transpose(0, 2, 1, 3)
    w["w2"] = g["L0_ffn_w2"].reshape(E0, IC0, P, D).transpose(0, 2, 1, 3)
    w["mask"] = np.concatenate([g["mask_BxS2_ik0"].T] * 2)
    w["mapping"] = np.broadcast_to(g["L1_ffn_inv_mapping"].reshape(1, -1), (E1, FX * KX))

    nc = _bacc.Bacc("TRN2", target_bir_lowering=False, num_devices=1)
    arrays, aps = {}, {}
    for name, v in w.items():
        arrays[f"in_{name}"] = np.ascontiguousarray(v)
        aps[name] = nc.dram_tensor(f"in_{name}", v.shape, mybir.dt.from_np(v.dtype), kind="ExternalInput").ap()
    aps["out"] = nc.dram_tensor("out_x", (B * S, D), F32, kind="ExternalOutput").ap()
    aps["turned"] = nc.dram_tensor("turned", (3, D, B * S), F32, kind="Internal").ap()
    for name in ("sorted", "returned"):
        aps[name] = nc.dram_tensor(name, (ROW_TILES * P, D), F32, kind="Internal").ap()
    aps["solved"] = nc.dram_tensor("solved", (D, B * S), F32, kind="Internal").ap()
    build(nc, aps)
    r = _run(nc, [arrays], core_ids=[0])
    return r.results[0]["out_x"].reshape(B, S, D)
```

```python
from contextlib import ExitStack

import numpy as np

import concourse.bass as bass
from concourse import mybir

F32 = mybir.dt.float32
F16 = mybir.dt.float16
BF16 = mybir.dt.bfloat16
I32 = mybir.dt.int32
ALU = mybir.AluOpType
ACT = mybir.ActivationFunctionType
AX = mybir.AxisListType

P = 128
B, S, D = 16, 64, 256
NT = B * S // P
KC = D // P
XT_AFTER = (0, 2, 3, 4, 5)
BANK = 512
EPS = 1e-5

NQ, H0, DH0, DKV = 4, 8, 8, 64
HX, DHX = 8, 8
E0, I0 = 8, 1024
IC0 = I0 // P
ROW_TILES = 2 * NT + E0 - 1
B1_ROWS = 64 + E0
H1, DH1 = 16, 16
BY_DVE = 14
E1, FX, KX, RX, I1, TOP1 = 64, 8, 8, 8, 176, 6
TAIL = I1 - P
TAILS = 64 + TAIL
ISH = 2 * I1
SHARED = [min(P, ISH - at) for at in range(0, ISH, P)]

PACKS = {
    "consts": [("ident", P, (P,)), ("ones", P, (P,)), ("headmask0", 72, (H0,)), ("headmask1", P, (8,)),
               ("cosx", P, (D,)), ("sinx", P, (D,)), ("rotx", P, (P,)), ("rep", P, (2, P)),
               ("lo_q", P, (1,)), ("lo_k", P, (1,)), ("selmax", P, (HX, P)),
               ("cos1", P, (DH1,)), ("sin1", P, (DH1,)), ("causal", P, (S,)),
               ("reset8", P, (NT * E0,)), ("reset64", P, (NT * E1,)), ("row", P, (1,)),
               ("b1_rows", P, (E0,)), ("before", P, (P,)), ("full_tiles", P, (NT,)), ("tile_no", P, (ROW_TILES,)),
               ("spread", E1, (FX, P))],
    "w_attn0": [("wq", P, (KC, D)), ("wk", P, (KC, DKV)), ("wv", P, (KC, DKV)), ("mem", DKV, (DKV + 1,)),
                ("memw", P, (1,))],
    "w_xattn0": [("wq", P, (P,)), ("wk", P, (P,)), ("wv", P, (S,)), ("wo", P, (2, S)), ("sums", P, (P,)), ("bq", P, (1,)),
                 ("bk", P, (1,)), ("bo", P, (1,)), ("bv", P, (S,))],
    "w_route0": [("rw1", P, (KC, P)), ("rw2", P, (E0,)), ("b1", P, (E0, IC0))],
    "w_attn1": [("wqk", P, (KC, 2 * D)), ("wvb", P, (KC, D + H1)), ("wo", P, (KC, D))],
    "w_xattn1": [("wq", P, (KC, D)), ("wk", P, (KC, D)), ("wv", P, (KC, D)), ("wo", P, (KC, D)),
                 ("bq", P, (KC,)), ("bk", P, (KC,)), ("bv", P, (D,)), ("bo", P, (D,)),
                 ("gamma", P, (D,)), ("beta", P, (D,)), ("scale", P, (1,))],
    "w_ffn1": [("gate", P, (KC, E1)), ("mask_up", E1, (FX, D)),
               ("shg", P, (KC, ISH)), ("shu", P, (KC, ISH)), ("shd", P, (len(SHARED), D))],
}
EXPERT = [("gw", P, (KC, P)), ("uw", P, (KC, P)), ("tw", P, (KC, TAILS)), ("qa", P, (KC, P)),
          ("qb", P, (P + TAILS,)), ("qs", P, (P + TAILS,)), ("dw", P, (D,)), ("dwt", TAIL, (D,)),
          ("dqa", P, (KX * RX,)), ("dqat", TAIL, (KX * RX,)), ("dqb", KX * RX, (D,)), ("ds", P, (D,))]


def columns(parts):
    return sum(int(np.prod(shape)) for _, _, shape in parts)


def views(ap, parts):
    out, at = {}, 0
    for name, rows, shape in parts:
        n = int(np.prod(shape))
        v = ap[0:rows, at:at + n]
        if len(shape) == 2:
            v = v.rearrange("p (a b) -> p a b", b=shape[1])
        out[name] = v
        at += n
    return out


class Signal:

    def __init__(self, sem, base=0, before=None):
        self.sem, self.n, self.base, self.before = sem, base, base, before

    def by(self, instruction):
        instruction.then_inc(self.sem, 1)
        self.n += 1
        return self.n


class Arena:

    def __init__(self, tensor, size):
        self.t, self.size, self.at = tensor, size, 0

    def take(self, *shape, dtype=F32):
        n = int(np.prod(shape))
        words = n if dtype in (F32, I32, mybir.dt.uint32) else (n + 1) // 2
        words += words % 2
        assert self.at + words <= self.size, (self.at, words)
        v = self.t[:, self.at:self.at + words]
        if dtype != F32:
            v = v.bitcast(dtype)
        v = v[:, 0:n]
        self.at += words
        if len(shape) == 2:
            v = v.rearrange("p (a b) -> p a b", b=shape[1])
        elif len(shape) == 3:
            v = v.rearrange("p (a b c) -> p a b c", b=shape[1], c=shape[2])
        elif len(shape) == 4:
            v = v.rearrange("p (a b c d) -> p a b c d", b=shape[1], c=shape[2], d=shape[3])
        return v


def wide(ap, axis, n):
    v = ap.unsqueeze(axis)
    shape = list(v.shape)
    shape[axis] = n
    return v.to_broadcast(shape)


def build(nc, a):
    ctx = ExitStack()
    with ctx:
        def signal(name):
            return Signal(ctx.enter_context(nc.semaphore(name)))

        renamed = []

        def again(name, old, total):
            renamed.append((name, Signal(old.sem, total, old)))
            return renamed[-1][1]

        ARENA = 48000
        arena = Arena(ctx.enter_context(nc.sbuf_tensor("arena", [P, ARENA], F32)), ARENA)
        psum = ctx.enter_context(nc.psum_tensor("psum", [P, 8 * BANK], F32))

        def bank(i, n=1):
            return psum[:, i * BANK:(i + n) * BANK]

        x = arena.take(NT, D)
        xt = arena.take(KC, B * S)
        con = arena.take(columns(PACKS["consts"]))
        c = views(con, PACKS["consts"])
        ctok = arena.take(NT, D)
        mean_var = arena.take(NT, 2)
        stats = arena.take(NT, 6)
        rstd = arena.take(NT)
        std = arena.take(NT)
        blank = arena.take(D)
        keep = arena.at

        loaded = {n: signal(f"loaded_{n}") for n in list(PACKS) + ["x", "x_late", "ident", "ctx"]}
        dve_step, act_step, pool_step = signal("dve_step"), signal("act_step"), signal("pool_step")
        xt_ps, xt_sb = signal("xt_ps"), signal("xt_sb")
        x_norm, ln_var, ln_std = signal("x_norm"), signal("ln_var"), signal("ln_std")
        out_done = signal("out_done")

        arena.at = keep
        w_a0 = arena.take(columns(PACKS["w_attn0"]))
        a0 = views(w_a0, PACKS["w_attn0"])
        q4 = arena.take(B, NQ, S)
        sig = arena.take(NQ, B * S)
        kt0 = arena.take(B * S)
        kb0 = arena.take(B, H0, S)
        vb0 = arena.take(B, 4, 2 * (DH0 + 1))
        am = arena.take(NT, D)
        pt0 = arena.take(2, 4, D)
        nm0 = arena.take(2, 2, H0)
        rs0 = arena.take(NQ * H0)
        rm0 = arena.take(NQ)
        t0 = arena.take(NQ * H0, DH0)
        gate0 = arena.take(4)
        end1 = arena.at
        q_ps, q_sb, v_ps, v_sb, kb_ready = (signal(n) for n in ("q_ps", "q_sb", "v_ps", "v_sb", "kb_ready"))
        elu_min, elu_exp, elu_ready = signal("elu_min"), signal("elu_exp"), signal("elu_ready")
        gate_exp, mem_ps, mem_read = signal("gate_exp"), signal("mem_ps"), signal("mem_read")
        a0_ps, a0_max, nmt0_ps, nmt0_sb = (signal(n) for n in ("a0_ps", "a0_max", "nmt0_ps", "nmt0_sb"))
        b0_ps, pt0_ready, o0_ps, o0_read = (signal(n) for n in ("b0_ps", "pt0_ready", "o0_ps", "o0_read"))

        arena.at = ARENA - 3 * 2 * KC * I0 - columns(PACKS["w_xattn0"]) - 1
        assert end1 <= arena.at
        w_x0 = arena.take(columns(PACKS["w_xattn0"]))
        arena.at = keep
        x0 = views(w_x0, PACKS["w_xattn0"])
        qs = arena.take(2, D)
        rope_a, rope_b = arena.take(2, D), arena.take(2, D)
        qr = arena.take(2, D)
        hi16 = arena.take(2, 2, 2 * D, dtype=F16)
        stack = {n: arena.take(B, 2, D, dtype=F16) for n in "kq"}
        vx = arena.take(B, 2, HX, 32)
        selm = arena.take(HX, P, dtype=BF16)
        nmx = arena.take(2, 2, HX)
        nmxb = arena.take(2, 2, P, dtype=BF16)
        nmtx = arena.take(2, D, dtype=BF16)
        ptx = arena.take(2, 2, D)
        otx = arena.take(2, 2 * D)
        rsx = arena.take(2 * D)
        onx = arena.take(2, 2 * D)
        ident16 = arena.take(P, dtype=BF16)
        assert arena.at <= ARENA - 3 * 2 * KC * I0 - columns(PACKS["w_xattn0"]) - 1
        pj_ps, pj_sb, rot_ps, qr_ready, rep_ps, hi_ready, st_ready = (
            signal(n) for n in ("pj_ps", "pj_sb", "rot_ps", "qr_ready", "rep_ps", "hi_ready", "st_ready"))
        vx_ps, vx_sb, selm_ready = signal("vx_ps"), signal("vx_sb"), signal("selm_ready")
        ax_ps, ax_max, nmx_ready, nmtx_ps, nmtx_sb = (
            signal(n) for n in ("ax_ps", "ax_max", "nmx_ready", "nmtx_ps", "nmtx_sb"))
        bx_ps, ptx_ready, ox_ps, pvx_done, onx_ready, otx_ps, otx_sb, yx_ps, yx_read = (
            signal(n) for n in ("bx_ps", "ptx_ready", "ox_ps", "pvx_done", "onx_ready", "otx_ps", "otx_sb", "yx_ps",
                                "yx_read"))
        arena.at = keep
        w_r0 = arena.take(columns(PACKS["w_route0"]))
        r0 = views(w_r0, PACKS["w_route0"])
        r1 = arena.take(B * S)
        prob = arena.take(NT, E0)
        pmax = arena.take(NT)
        top8 = arena.take(NT, 8)
        first = arena.take(NT * E0)
        both = arena.take(NT * E0)
        tie = arena.take(NT * E0)
        rank = arena.take(NT * E0)
        more = arena.take(NT)
        marks = arena.take(NT, 2 * E0)
        earlier = arena.take(NT, E0)
        active = arena.take(2 * E0)
        gates = arena.take(NT, E0)
        weight_c = arena.take(NT, 2 * E0)
        slot_a = arena.take(NT, E0)
        b1g = arena.take(E0, IC0)
        level0 = arena.take(NT, E0)
        count0 = arena.take(E0)
        over0 = arena.take(E0, NT)
        tiles0 = arena.take(E0)
        end0 = arena.take(E0)
        row0 = arena.take(E0)
        place = arena.take(NT, E0)
        placed = arena.take(NT, 2 * E0)
        slot_row = arena.take(NT * 2)
        slot_row_i = arena.take(NT * 2, dtype=mybir.dt.uint32)
        past = arena.take(ROW_TILES, E0 - 1)
        tile_e = arena.take(ROW_TILES)
        tile_e_i = arena.take(ROW_TILES, dtype=I32)
        early_ce = c["rep"].rearrange("p a b -> p (a b)")
        ceb = arena.take(D)
        xs = arena.take(2, D)
        xst = arena.take(2, KC, P)
        ys = arena.take(2, D)
        wct = r1
        assert arena.at <= ARENA - E0 * 2 * KC * I0
        arena.at = ARENA - E0 * 2 * KC * I0
        w12 = arena.take(E0, 2 * KC * I0)
        w1v = w12[:, :, 0:KC * I0].rearrange("p e (k i) -> p e k i", k=KC)
        w2v = w12[:, :, KC * I0:2 * KC * I0].rearrange("p e (c d) -> p e c d", c=IC0)
        back = w12[:, 0:2, 0:KC * I0].rearrange("p e (n d) -> p e n d", d=D)
        at = columns(PACKS["consts"][:[n for n, _, _ in PACKS["consts"]].index("cosx")])
        b1_cols = con[:, at:at + E0 * IC0 * E0].rearrange("p (e c f) -> p e c f", e=E0, c=IC0)
        hid = xt.rearrange("p k (r n) -> p (k r) n", n=I0)
        hidt = ctok.rearrange("p (r c) d -> p r (c d)", r=2)
        b1_row, b1_rest = hidt[0:B1_ROWS, 0, :], hidt[0:B1_ROWS, 1, :]
        sel_cols = c["selmax"].rearrange("p a b -> p (a b)")
        b1_terms = sel_cols[0:B1_ROWS, 0:I0 // 2].bitcast(BF16)
        b1_pick = sel_cols[0:B1_ROWS, I0 // 2:I0 // 2 + E0 * P // 2].bitcast(BF16)\
            .rearrange("p (e t) -> p e t", e=E0)
        w12_in, w12_early = signal("w12_in"), signal("w12_early")
        EARLY = (7, 6, 5)
        b1_in, b2_in = signal("b1_in"), signal("b2_in")
        blank_rows = signal("blank_rows")
        r1_ps, r1_sb, lg_ps, p_exp, p_sub = (
            signal(n) for n in ("r1_ps", "r1_sb", "lg_ps", "p_exp", "p_sub"))
        marks_ready, cnt_ps, wc_ready, wct_ps, wct_sb = (
            signal(n) for n in ("marks_ready", "cnt_ps", "wc_ready", "wct_ps", "wct_sb"))
        b1_gelu, ce_ps, cet_sb, b1_spread, ceb_sb, const_ps, const_read = (
            signal(n) for n in ("b1_gelu", "ce_ps", "cet_sb", "b1_spread", "ceb_sb", "const_ps", "const_read"))
        place_ready = again("place_ready", q_ps, 6)
        tiles_ready = again("tiles_ready", q_sb, 6)
        sorted_out = signal("sorted_out")
        xs_in = [again("xs_in_even", a0_max, 2 * B), signal("xs_in_odd")]
        xst_ps = again("xst_ps", mem_ps, NT)
        xst_sb = again("xst_sb", nmt0_ps, B)
        up_ps = again("up_ps", nmt0_sb, B)
        hid_ready = again("hid_ready", b0_ps, B)
        hidt_ps = again("hidt_ps", pt0_ready, B)
        hidt_sb = again("hidt_sb", o0_ps, B)
        down_ps = again("down_ps", a0_ps, 2 * B)
        ys_ready = signal("ys_ready")
        ys_out = [again("ys_out_even", kb_ready, NT), signal("ys_out_odd")]
        back_in = [signal(f"back_in_{i}") for i in range(4)]
        b1_blank = again("b1_blank", elu_ready, 1)
        b1_ready = again("b1_ready", gate_exp, 1)
        w_a1_at = ARENA - columns(PACKS["w_attn1"])
        arena.at = w_a1_at
        w_a1 = arena.take(columns(PACKS["w_attn1"]))
        a1 = views(w_a1, PACKS["w_attn1"])
        arena.at = keep
        qk1 = arena.take(NT, 2 * D)
        vz1 = arena.take(NT, D + H1)
        sq1 = arena.take(2, D)
        rk1 = arena.take(NT, H1)
        std1 = arena.take(NT, H1)
        beta1 = arena.take(NT, H1)
        turn_a, turn_b = arena.take(2 * D), arena.take(2 * D)
        rq1 = arena.take(2, 2 * D)
        kw1 = arena.take(2, D)
        ft1_at = arena.at
        ft1 = arena.take(4, KC, B * S)
        spread1 = arena.take(B * 8 * 34)
        kb1 = spread1[:, 0:4 * KC * 8 * S].rearrange("p (b k h t) -> p b k h t", b=4, k=KC, h=8)
        part1 = lambda v: v.rearrange("p (g c i) -> p g c i", g=2, i=S)
        flat_qk1 = qk1.rearrange("p a b -> p (a b)")
        bh1 = [part1(v) for v in (ft1[:, 2, :, :].rearrange("p k n -> p (k n)"), flat_qk1[:, KC * B * S:],
                                  ft1[:, 3, :, :].rearrange("p k n -> p (k n)"))]
        vn1 = part1(vz1.rearrange("p a b -> p (a b)")[:, 0:2 * DH1 * S])
        state1, outer1 = arena.take(2, DH1, DH1), arena.take(2, DH1, DH1)
        seen1 = arena.take(2, DH1)
        sm1 = arena.take(2, 2 * D)
        mx1 = arena.take(2, 8)
        pt1 = arena.take(2 * NT, 2 * D)
        vnt1 = flat_qk1[:, 0:KC * B * S].rearrange("p (k n) -> p k n", k=KC)
        vb1 = spread1.rearrange("p (b q c) -> p b q c", b=B, q=8)
        on1 = arena.take(2, D)
        ot1 = arena.take(2, KC, P)
        rs1 = arena.take(2, H1)
        assert arena.at <= w_a1_at
        (pj1_ps, pj1_sb, ss_part, ss_ready, ss_std, bz_exp, turned1, tr1_ps, ft_sb, turned_out, bh_in, kb1_ready, a1_ps,
         sm_ready, sm_exp, pt_ps, pt_sb, regressed, solved_out, vnt_in, vb1_ps, vb1_sb, o1_ps, on1_ready, ot1_ps,
         ot1_sb, y1_ps, y1_read, blank1) = (signal(n) for n in (
             "pj1_ps", "pj1_sb", "ss_part", "ss_ready", "ss_std", "bz_exp", "turned1", "tr1_ps", "ft_sb", "turned_out",
             "bh_in", "kb1_ready", "a1_ps", "sm_ready", "sm_exp", "pt_ps", "pt_sb", "regressed", "solved_out", "vnt_in",
             "vb1_ps", "vb1_sb", "o1_ps", "on1_ready", "ot1_ps", "ot1_sb", "y1_ps", "y1_read", "blank1"))
        kb1_last = again("kb1_last", mem_read, NT)
        by_head = lambda t: t.rearrange("(g p) (c i) -> p g c i", p=P, i=S)
        by_feature = lambda t, k: t.rearrange("(b k h) (c i) -> k (h c) b i", k=KC, h=H1 // KC, i=S)[k]

        def regress(engine, step, parts, halving=False):
            def alternate(do_step):
                for n, part in enumerate(parts):
                    if before[n]:
                        engine.wait_ge(step.sem, before[n])
                    before[n] = step.by(do_step(*part))

            before = [0] * len(parts)
            alternate(lambda g, ch: engine.memset(state1[:, g, ch, :], 0.0))
            engine.wait_ge(bh_in.sem, 16 * 3 * 2)
            for i in range(S):
                keys, beta_keys, values = (bh1[n][:, :, :, i] for n in range(3))
                new = vn1[:, :, :, i]
                rows = lambda v, g, ch: wide(v[:, g, :], 2, ch.stop - ch.start)
                alternate(lambda g, ch: engine.tensor_tensor(
                    out=outer1[:, g, ch, :], in0=state1[:, g, ch, :], in1=rows(keys, g, ch), op=ALU.mult))
                if halving:
                    for w in (8, 4, 2, 1):
                        alternate(lambda g, ch: engine.tensor_tensor(
                            out=outer1[:, g, ch, 0:w], in0=outer1[:, g, ch, 0:w], in1=outer1[:, g, ch, w:2 * w],
                            op=ALU.add))
                    seen = outer1[:, :, :, 0]
                else:
                    alternate(lambda g, ch: engine.tensor_reduce(seen1[:, g, ch], outer1[:, g, ch, :], AX.X, ALU.add))
                    seen = seen1
                alternate(lambda g, ch: engine.tensor_tensor(
                    out=new[:, g, ch], in0=values[:, g, ch], in1=seen[:, g, ch], op=ALU.subtract))
                if i < S - 1:
                    alternate(lambda g, ch: engine.tensor_tensor(
                        out=outer1[:, g, ch, :], in0=wide(new[:, g, ch], 3, DH1), in1=rows(beta_keys, g, ch),
                        op=ALU.mult))
                    alternate(lambda g, ch: engine.tensor_tensor(
                        out=state1[:, g, ch, :], in0=state1[:, g, ch, :], in1=outer1[:, g, ch, :], op=ALU.add))
            for n in before:
                engine.wait_ge(step.sem, n)
            regressed.by(engine.memset(seen1[:, 0, parts[0][1].start:parts[0][1].start + 1], 0.0))
        arena.at = keep
        ct5 = arena.take(KC, B * S)
        k5, q5 = arena.take(KC, B * S), arena.take(KC, B * S)
        assert arena.at <= ft1_at
        arena.at = ft1_at
        w_x1 = arena.take(columns(PACKS["w_xattn1"]))
        assert arena.at <= ft1_at + 2 * KC * B * S
        x1 = views(w_x1, PACKS["w_xattn1"])
        kb5 = arena.take(4 * KC, 8, S)
        vb5 = arena.take(B, 8, 34)
        s5, pt5 = arena.take(2, 2 * D), arena.take(2, 2 * D)
        mask5 = arena.take(B, dtype=I32)
        attend5, off5 = arena.take(B), arena.take(B)
        on5, ot5 = arena.take(2, D), arena.take(2, KC, P)
        rs5 = arena.take(2, H1)
        delta5 = arena.take(NT, D)
        scale5 = arena.take(2)
        bo5 = arena.take(D)
        end5 = arena.at
        (mask_in, ct_ps, ct_sb, kq5_ps, kq5_sb, v5_ps, v5_sb, blank5, kb5_ready, b5_ps, s5_ready, pt5_ready, o5_ps,
         on5_ready, ot5_ps, ot5_sb, y5_ps, y5_read, x_beta) = (signal(n) for n in (
             "mask_in", "ct_ps", "ct_sb", "kq5_ps", "kq5_sb", "v5_ps", "v5_sb", "blank5", "kb5_ready", "b5_ps",
             "s5_ready", "pt5_ready", "o5_ps", "on5_ready", "ot5_ps", "ot5_sb", "y5_ps", "y5_read", "x_beta"))
        w_f1_at = ARENA - columns(PACKS["w_ffn1"]) - 2 * columns(EXPERT)
        assert end5 <= w_f1_at
        arena.at = w_f1_at
        w_f1 = arena.take(columns(PACKS["w_ffn1"]))
        f1 = views(w_f1, PACKS["w_ffn1"])
        w_e = arena.take(2, columns(EXPERT))
        ex = [views(w_e[:, i, :], EXPERT) for i in range(2)]
        arena.at = keep
        prob6, mark6 = arena.take(NT, E1), arena.take(NT * E1)
        tie6, rank6 = arena.take(NT * E1), arena.take(NT * E1)
        peak6, more6 = arena.take(NT * FX), arena.take(NT)
        top6 = arena.take(NT, 8)
        map_i, map_f = arena.take(FX * KX, dtype=I32), arena.take(FX * KX)
        wd6 = arena.take(B * S)
        flat6 = arena.take(NT * FX, KX)
        mix6 = arena.take(NT * FX, KX)
        total6 = arena.take(NT * FX)
        wt6 = arena.take(B * S)
        xe6 = arena.take(2, KC, BANK)
        we6 = arena.take(3, BANK)
        aw6 = arena.take(2, BANK)
        adw6 = arena.take(BANK)
        g6, h6 = arena.take(4, BANK), arena.take(4, BANK)
        qb6 = arena.take(2, P + TAILS)
        dqb6 = arena.take(2, D)
        hs6 = arena.take(len(SHARED), BANK)
        assert arena.at <= w_f1_at
        experts_in = [signal("experts_in_even"), signal("experts_in_odd")]
        map_in = signal("map_in")
        lg6_ps = again("lg6_ps", pj_ps, 2 * NT)
        wd6_ps = again("wd6_ps", rot_ps, 2 * NT)
        flat6_ps = again("flat6_ps", rep_ps, 2 * B)
        wt6_ps = again("wt6_ps", vx_ps, B)
        sh_ps = again("sh_ps", ax_ps, B * HX)
        sho_ps = again("sho_ps", nmtx_ps, B)
        mid_ps = again("mid_ps", bx_ps, B * HX)
        out6_ps = again("out6_ps", pvx_done, B * HX)
        p6_sub = again("p6_sub", qr_ready, 2 * NT)
        wd6_ready = again("wd6_ready", st_ready, 2 * B)
        sel6_ready = again("sel6_ready", vx_sb, B)
        m6_sub = again("m6_sub", ax_max, B * HX)
        mix6_ready = again("mix6_ready", nmx_ready, B)
        sh_h = again("sh_h", onx_ready, B)
        sho_read = again("sho_read", yx_read, B)
        mid_dve = again("mid_dve", v_sb, 2)
        qb6_ready = again("qb6_ready", kb1_last, 2 * NT)
        out6_read = again("out6_read", elu_min, 1)
        p6_exp = again("p6_exp", pj_sb, 2 * NT)
        wd6_sb = again("wd6_sb", hi_ready, 2 * B)
        m6_exp = again("m6_exp", nmtx_sb, B)
        wt6_sb = again("wt6_sb", ptx_ready, B * HX)
        sh_silu = again("sh_silu", otx_sb, B)
        mid_act = again("mid_act", elu_exp, 1)

        STEPS = 2 * FX
        ring, by_dve, by_act = {}, {}, {}
        for step in range(-1, STEPS + 1):
            for kind, n, engine in ((("x", 0), step + 1, "D"), (("x", 1), step + 1, "D"), (("w", 0), step + 1, "A"),
                                    (("d", 0), step - 1, "D"), (("a", 0), step + 1, "D"), (("g", 0), step, "A"),
                                    (("u", 0), step, "D"), (("t", 0), step, "D")):
                if 0 <= n < STEPS:
                    ring[kind, n] = len(ring)
                    (by_dve if engine == "D" else by_act)[kind, n] = len(by_dve if engine == "D" else by_act)
                    if kind[0] == "t":
                        by_act[("silu", 0), n] = len(by_act)
        order = list(ring)

        def bank_free(pe, key):
            if ring[key] >= 4:
                before = order[ring[key] - 4]
                if before in by_dve:
                    pe.wait_ge(mid_dve.sem, mid_dve.base + by_dve[before] + 1)
                else:
                    pe.wait_ge(mid_act.sem, mid_act.base + by_act[before] + 1)

        def a_steps():
            return [[0, 1], [2], [3, 4], [5], [6, 7], [], [], []]

        block = ctx.enter_context(nc.Block())

        @block.sync
        def _(sp):
            def fetch_expert(e, done):
                sp.dma_start(w12[:, e, 0:KC * I0].rearrange("p (k i) -> p k i", k=KC), a["w1"][e]).then_inc(done.sem, 16)
                sp.dma_start(w12[:, e, KC * I0:].rearrange("p (c d) -> p c d", c=IC0), a["w2"][e]).then_inc(done.sem, 16)

            sp.dma_start(con[:, 0:P], a["consts"][:, 0:P]).then_inc(loaded["ident"].sem, 16)
            halves = a["x"].rearrange("(n j p) d -> n p j d", p=P, n=2)
            sp.dma_start(x[:, 0:NT // 2, :], halves[0]).then_inc(loaded["x"].sem, 16)
            sp.dma_start(w_a0, a["w_attn0"]).then_inc(loaded["w_attn0"].sem, 16)
            sp.dma_start(x[:, NT // 2:NT, :], halves[1]).then_inc(loaded["x_late"].sem, 16)
            sp.dma_start(con[:, P:], a["consts"][:, P:]).then_inc(loaded["consts"].sem, 16)
            sp.dma_start(w_x0, a["w_xattn0"]).then_inc(loaded["w_xattn0"].sem, 16)
            sp.dma_start(ctok, a["ctx"].rearrange("(j p) d -> p j d", p=P)).then_inc(loaded["ctx"].sem, 16)
            sp.wait_ge(pool_step.sem, 1)
            sp.dma_start(a["sorted"].rearrange("(r p) d -> p r d", p=P), wide(blank, 1, ROW_TILES))\
              .then_inc(blank_rows.sem, 16)
            for e in EARLY:
                fetch_expert(e, w12_early)
            sp.wait_ge(x_norm.sem, 2 * NT)
            sp.dma_start(w_r0, a["w_route0"]).then_inc(loaded["w_route0"].sem, 16)
            sp.wait_ge(b1_blank.sem, b1_blank.base + 1)
            for i in range(3):
                sp.dma_start(b1_row[32 * i:32 * i + E0, :], a["b1"]).then_inc(b1_in.sem, 16)
            sp.dma_start(ceb[E0:2 * E0, :], a["b2"]).then_inc(b2_in.sem, 16)
            for e in range(min(EARLY) - 1, -1, -1):
                fetch_expert(e, w12_in)
            sp.wait_ge(sorted_out.sem, 16 * 2 * NT)
            for r in range(ROW_TILES + 4):
                if r < ROW_TILES:
                    if r >= 2:
                        sp.wait_ge(xst_ps.sem, xst_ps.base + r - 1)
                    sp.dma_start(xs[:, r % 2, :], a["sorted"][r * P:(r + 1) * P, :]).then_inc(xs_in[r % 2].sem, 16)
                q = r - 4
                if q >= 0:
                    sp.wait_ge(ys_ready.sem, q + 1)
                    sp.dma_start(a["returned"][q * P:(q + 1) * P, :], ys[:, q % 2, :])\
                      .then_inc(ys_out[q % 2].sem, 16)
            sp.wait_ge(down_ps.sem, down_ps.base + ROW_TILES)
            sp.dma_start(ctok, a["ctx"].rearrange("(j p) d -> p j d", p=P)).then_inc(loaded["ctx"].sem, 16)
            sp.dma_start(w_a1, a["w_attn1"]).then_inc(loaded["w_attn1"].sem, 16)
            sp.wait_ge(ft_sb.sem, 2 * NT)
            for n in range(3):
                for k in range(KC):
                    sp.dma_start(by_feature(a["turned"][n], k), ft1[:, 1 + n, k, :].rearrange("p (b i) -> p b i", i=S))\
                      .then_inc(turned_out.sem, 16)
            sp.wait_ge(turned_out.sem, 16 * 3 * KC)
            for n in range(3):
                for g in range(2):
                    sp.dma_start(bh1[n][:, g, :, :], by_head(a["turned"][(1, 0, 2)[n]])[:, g, :, :])\
                      .then_inc(bh_in.sem, 16)
            sp.wait_ge(a1_ps.sem, 2 * NT)
            sp.dma_start(w_x1, a["w_xattn1"]).then_inc(loaded["w_xattn1"].sem, 16)
            sp.wait_ge(regressed.sem, 2)
            for g in range(2):
                sp.dma_start(by_head(a["solved"])[:, g, :, :], vn1[:, g, :, :]).then_inc(solved_out.sem, 16)
            sp.wait_ge(solved_out.sem, 16 * 2)
            for k in range(KC):
                sp.dma_start(vnt1[:, k, :].rearrange("p (b i) -> p b i", i=S), by_feature(a["solved"], k))\
                  .then_inc(vnt_in.sem, 16)
            sp.wait_ge(x_norm.sem, 4 * NT)
            sp.dma_start(mask5, a["mask"]).then_inc(mask_in.sem, 16)
            sp.dma_start(w_f1, a["w_ffn1"]).then_inc(loaded["w_ffn1"].sem, 16)
            for f in range(FX):
                if f == 2:
                    sp.wait_ge(x_norm.sem, 5 * NT)
                    sp.dma_start(map_i[0:E1, :], a["mapping"]).then_inc(map_in.sem, 16)
                if f >= 2:
                    sp.wait_ge(out6_ps.sem, out6_ps.base + NT * (f - 1))
                sp.dma_start(w_e[:, f % 2, :], a["experts"][f]).then_inc(experts_in[f % 2].sem, 16)
            sp.wait_ge(x_norm.sem, NT * 6)
            sp.dma_start(a["out"].rearrange("(j p) d -> p j d", p=P), x).then_inc(out_done.sem, 16)
            sp.wait_ge(out_done.sem, 16)

        @block.gpsimd
        def _(pool):
            def do(instruction, s=pool_step):
                pool.wait_ge(s.sem, s.by(instruction))

            do(pool.memset(blank, 0.0))
            do(pool.memset(kt0[64:72, :], 1.0))
            do(pool.memset(vb0[:, :, :, :], 0.0))
            v = vb0.rearrange("p b q (r c) -> p (b q) r c", r=2)
            do(pool.memset(v[0:64, :, 0, DH0:DH0 + 1], 1.0))
            do(pool.memset(v[64:128, :, 1, DH0:DH0 + 1], 1.0))
            pool.wait_ge(loaded["consts"].sem, 16)
            for j in range(NT):
                pool.wait_ge(q_sb.sem, 5 + j // 4)
                keys = kt0[0:72, j * P:(j + 1) * P].rearrange("p (b t) -> p b t", b=2)
                for i in range(2):
                    last = pool.tensor_tensor(
                        out=kb0[0:72, 2 * j + i, :, :], in0=wide(keys[:, i, :], 1, H0),
                        in1=wide(c["headmask0"], 2, S), op=ALU.mult)
                kb_ready.by(last)
            pool.wait_ge(x_norm.sem, NT)
            do(pool.memset(nmxb.rearrange("p a b c -> p (a b c)"), 0.0))
            do(pool.memset(vx.rearrange("p b s h c -> p (b s h) c")[:, :, DHX:32], 1.0))
            do(pool.tensor_copy(selm, c["selmax"]), selm_ready)
            pool.wait_ge(x_norm.sem, 2 * NT)
            do(pool.memset(b1_row, 0.0), b1_blank)
            for e in range(E0):
                last = pool.tensor_copy(b1_pick[:, e, :], c["b1_rows"][0:B1_ROWS, e:e + 1].to_broadcast([B1_ROWS, P]))
            do(last)
            do(pool.memset(b1_cols, 0.0))
            pool.wait_ge(b1_gelu.sem, 1)
            for e in range(E0):
                last = pool.tensor_copy(b1_cols[:, e, :, e], b1g[:, e, :])
            do(last, b1_spread)
            pool.wait_ge(b1_in.sem, 48)
            do(pool.tensor_copy(b1_terms, b1_row))
            do(pool.tensor_tensor(out=b1_rest, in0=b1_row, in1=b1_terms, op=ALU.subtract))
            pool.tensor_copy(b1_terms[32:64, :], b1_rest[32:64, :])
            do(pool.tensor_copy(b1_terms[64:B1_ROWS, :], b1_rest[64:B1_ROWS, :]))
            do(pool.tensor_tensor(out=b1_rest[64:B1_ROWS, :], in0=b1_rest[64:B1_ROWS, :],
                                  in1=b1_terms[64:B1_ROWS, :], op=ALU.subtract))
            do(pool.tensor_copy(b1_terms[64:B1_ROWS, :], b1_rest[64:B1_ROWS, :]), b1_ready)
            pool.wait_ge(blank_rows.sem, 16)
            pool.wait_ge(place_ready.sem, place_ready.base + 1)
            for n in range(2 * NT):
                pool.indirect_dma_start(a["sorted"], bass.IndirectOffsetOnAxis(ap=slot_row_i[:, n:n + 1], axis=0),
                                        x[:, n // 2, :], None).then_inc(sorted_out.sem, 16)
            pool.wait_ge(ys_out[0].sem, ys_out[0].base + 16 * (ROW_TILES - ROW_TILES // 2))
            pool.wait_ge(ys_out[1].sem, ys_out[1].base + 16 * (ROW_TILES // 2))
            for n in range(2 * NT):
                pool.indirect_dma_start(back[:, n // NT, n % NT, :], None, a["returned"],
                                        bass.IndirectOffsetOnAxis(ap=slot_row_i[:, n:n + 1], axis=0))\
                    .then_inc(back_in[n // 4].sem, 16)
            for j in range(NT):
                pool.wait_ge(ft_sb.sem, 2 * j + 1)
                if j >= 2:
                    pool.wait_ge(a1_ps.sem, 2 * (j - 1))
                for i in range(3):
                    b, k = 2 * j + i // 2, i % 2
                    last = pool.tensor_tensor(out=kb1[:, b % 4, k, :, :], in0=wide(ft1[:, 1, k, b * S:(b + 1) * S], 1, 8),
                                              in1=wide(c["headmask1"], 2, S), op=ALU.mult)
                kb1_ready.by(last)
            pool.wait_ge(a1_ps.sem, 2 * NT)
            do(pool.memset(vb1.rearrange("p b q c -> p (b q c)"), 0.0), blank1)
            v = vb1.rearrange("p b q (r c) -> p (b q) r c", r=2)
            do(pool.memset(v[0:64, :, 0, DH1:DH1 + 1], 1.0), blank1)
            do(pool.memset(v[64:128, :, 1, DH1:DH1 + 1], 1.0), blank1)
            regress(pool, pool_step, [(slice(0, 2), slice(BY_DVE, DH1))], halving=True)
            pool.wait_ge(x_norm.sem, 4 * NT)
            do(pool.memset(vb5.rearrange("p b q c -> p (b q c)"), 0.0), blank5)
            v = vb5.rearrange("p b q (r c) -> p (b q) r c", r=2)
            do(pool.memset(v[0:64, :, 0, DH1:DH1 + 1], 1.0), blank5)
            do(pool.memset(v[64:128, :, 1, DH1:DH1 + 1], 1.0), blank5)
            for b in range(B):
                pool.wait_ge(kq5_sb.sem, 2 * (b // 8) + 2)
                if b >= 4:
                    pool.wait_ge(b5_ps.sem, b - 3)
                for k in range(KC):
                    last = pool.tensor_tensor(out=kb5[:, (b % 4) * KC + k, :, :],
                                              in0=wide(k5[:, k, b * S:(b + 1) * S], 1, 8),
                                              in1=wide(c["headmask1"], 2, S), op=ALU.mult)
                kb5_ready.by(last)
            for j in range(NT):
                pool.wait_ge(xt_ps.sem, 3 * NT + j + 1)
                x_beta.by(pool.tensor_tensor(out=x[:, j, :], in0=x[:, j, :], in1=x1["beta"], op=ALU.add))


        @block.tensor
        def _(pe):
            ident = c["ident"]

            def turn_x(use):
                for j in range(NT):
                    t = use * NT + j
                    if use == 0:
                        pe.wait_ge(loaded["x" if j < NT // 2 else "x_late"].sem, 16)
                        pe.wait_ge(loaded["ident"].sem, 16)
                    else:
                        pe.wait_ge(x_norm.sem, NT * (XT_AFTER[use] - 1) + j + 1)
                    if t >= 2:
                        pe.wait_ge(xt_sb.sem, t - 1)
                    for k in range(KC):
                        last = pe.transpose(bank(t % 2)[:, k * P:(k + 1) * P], x[:, j, k * P:(k + 1) * P], ident)
                    xt_ps.by(last)

            turn_x(0)
            pe.wait_ge(loaded["w_attn0"].sem, 16)
            for u in range(6):
                n, pair = (u // 2, u % 2) if u < 4 else (u - 4, None)
                pe.wait_ge(xt_sb.sem, 4 * n + 4)
                if u >= 2:
                    pe.wait_ge(q_sb.sem, u - 1)
                for k in range(KC):
                    w = a0["wk"][:, k, :] if pair is None else a0["wq"][:, k, pair * P:(pair + 1) * P]
                    m = DKV if pair is None else P
                    last = pe.matmul(bank(2 + u % 2)[0:m, :], w, xt[:, k, n * BANK:(n + 1) * BANK],
                                     start=(k == 0), stop=(k == KC - 1))
                q_ps.by(last)
            for b in range(B):
                for r in range(2):
                    for k in range(KC):
                        last = pe.matmul(bank(4 + b // 8)[64 * r:64 * r + 64, (b % 8) * 32:(b % 8 + 1) * 32],
                                         xt[:, k, b * S:(b + 1) * S],
                                         a0["wv"][:, k, :].rearrange("p (q r c) -> p q r c", r=2, c=DH0)[:, :, r, :],
                                         start=(k == 0), stop=(k == KC - 1))
                if b % 8 == 7:
                    v_ps.by(last)
            for j in range(NT):
                pe.wait_ge(elu_ready.sem, 1)
                if j >= 2:
                    pe.wait_ge(mem_read.sem, j - 1)
                for g in range(NQ):
                    last = pe.matmul(bank(6 + j % 2)[:, g * 65:(g + 1) * 65], sig[0:DKV, g, j * P:(j + 1) * P],
                                     a0["mem"], start=True, stop=True)
                mem_ps.by(last)

            def first_scores0(b):
                pe.wait_ge(kb_ready.sem, b // 2 + 1)
                for pair in range(2):
                    if b >= 2:
                        pe.wait_ge(a0_max.sem, 2 * (b - 2) + pair + 1)
                    a0_ps.by(pe.matmul(bank(2 * (b % 2) + pair), q4[0:DKV, b, 2 * pair:2 * pair + 2, :],
                                       kb0[0:DKV, b, :, :], start=True, stop=True))

            def turn_max0(b):
                pe.wait_ge(a0_max.sem, 2 * b + 2)
                if b >= 1:
                    pe.wait_ge(nmt0_sb.sem, b)
                for pair in range(2):
                    last = pe.transpose(bank(4)[0:H0, pair * P:(pair + 1) * P], nm0[:, b % 2, pair, :], ident)
                nmt0_ps.by(last)

            def scores0(b):
                pe.wait_ge(nmt0_sb.sem, b + 1)
                if b >= 1:
                    pe.wait_ge(pt0_ready.sem, b)
                for hp in range(4):
                    last = pe.matmul(bank(5, 2)[:, hp * D:(hp + 1) * D], kb0[0:72, b, 2 * hp:2 * hp + 2, :],
                                     q4[0:72, b, :, :], start=True, stop=True)
                b0_ps.by(last)

            def values0(b):
                j, half = b // 2, 64 * (b % 2)
                pe.wait_ge(pt0_ready.sem, b + 1)
                if b % 2 == 0 and j >= 1:
                    pe.wait_ge(o0_read.sem, j)
                for g in range(NQ):
                    for hp in range(4):
                        at = (g * 4 + hp) * 18
                        last = pe.matmul(bank(7)[half:half + 64, at:at + 18], pt0[:, b % 2, hp, g * S:(g + 1) * S],
                                         vb0[:, b, hp, :], start=True, stop=True)
                o0_ps.by(last)

            pe.wait_ge(q_sb.sem, 6)
            pe.wait_ge(v_sb.sem, 2)
            pe.wait_ge(mem_read.sem, NT)
            first_scores0(0)
            first_scores0(1)
            turn_max0(0)
            for b in range(B):
                scores0(b)
                if b + 1 < B:
                    turn_max0(b + 1)
                if b >= 1:
                    values0(b - 1)
                if b + 2 < B:
                    first_scores0(b + 2)
            values0(B - 1)

            def project(u):
                side, j = ("k", u) if u < NT else ("q", u - NT)
                if u == 0:
                    pe.wait_ge(loaded["ctx"].sem, 16)
                    pe.wait_ge(loaded["w_xattn0"].sem, 16)
                if side == "q":
                    pe.wait_ge(x_norm.sem, j + 1)
                if u >= 2:
                    pe.wait_ge(pj_sb.sem, u - 1)
                src = ctok if side == "k" else x
                pj_ps.by(pe.matmul(bank(u % 2)[:, 0:D], x0["w" + side], src[:, j, :], start=True, stop=True))

            def rotate(u):
                pe.wait_ge(pj_sb.sem, u + 1)
                if u >= 2:
                    pe.wait_ge(qr_ready.sem, u - 1)
                rot_ps.by(pe.matmul(bank(2 + u % 2)[:, 0:D], c["rotx"], qs[:, u % 2, :], start=True, stop=True))

            def replicate(u):
                pe.wait_ge(qr_ready.sem, u + 1)
                for p in range(2):
                    if u >= 2:
                        pe.wait_ge(st_ready.sem, 2 * (u - 2) + p + 1)
                    for g in range(2):
                        last = pe.matmul(bank(4 + 2 * (u % 2) + p)[:, g * D:(g + 1) * D],
                                         c["rep"][64 * p:64 * p + 64, g, :], qr[64 * p:64 * p + 64, u % 2, :],
                                         start=True, stop=True)
                    rep_ps.by(last)

            def head_rows(h):
                return 32 * (h % 4), 32 * (h % 4) + 32, h // 4

            def first_scores_x(b, h):
                u = b * HX + h
                r0, r1, g = head_rows(h)
                if u >= 2:
                    pe.wait_ge(ax_max.sem, u - 1)
                for tc in range(2):
                    last = pe.matmul(bank(u % 2)[:, tc * D:(tc + 1) * D], stack["q"][r0:r1, b, g, tc * P:(tc + 1) * P],
                                     stack["k"][r0:r1, b, g, :], start=True, stop=True, tile_position=(r0, 0))
                ax_ps.by(last)

            def turn_max(b):
                pe.wait_ge(nmx_ready.sem, b + 1)
                if b >= 1:
                    pe.wait_ge(nmtx_sb.sem, b)
                for tc in range(2):
                    last = pe.transpose(bank(4).bitcast(BF16)[:, tc * P:(tc + 1) * P], nmxb[:, b % 2, tc, :],
                                        ident16)
                nmtx_ps.by(last)

            def scores_x(b, h):
                u = b * HX + h
                r0, r1, g = head_rows(h)
                if h == 0:
                    pe.wait_ge(nmtx_sb.sem, b + 1)
                if u >= 2:
                    pe.wait_ge(ptx_ready.sem, u - 1)
                for sc in range(2):
                    out = bank(2 + u % 2)[:, sc * D:(sc + 1) * D]
                    pe.matmul(out, stack["k"][r0:r1, b, g, sc * P:(sc + 1) * P], stack["q"][r0:r1, b, g, :],
                              start=True, stop=False, tile_position=(r0, 0))
                    last = pe.matmul(out, selm[r0:r0 + HX, h, :], nmtx[r0:r0 + HX, b % 2, :],
                                     start=False, stop=True, tile_position=(r0, 0))
                bx_ps.by(last)

            def values_x(b, h):
                u = b * HX + h
                pe.wait_ge(ptx_ready.sem, u + 1)
                if h == 0 and b >= 2:
                    pe.wait_ge(onx_ready.sem, b - 1)
                q, g = h % 4, h // 4
                for sc in range(2):
                    last = pe.matmul(bank(5 + b % 2)[32 * q:32 * q + 32, g * D:(g + 1) * D], vx[:, b, sc, h, :],
                                     ptx[:, u % 2, sc, :], start=(sc == 0), stop=(sc == 1),
                                     tile_position=(0, 32 * q))
                pvx_done.by(last)

            def sums_x(b):
                pe.wait_ge(otx_sb.sem, b + 1)
                otx_ps.by(pe.matmul(bank(5 + b % 2), x0["sums"], otx[:, b % 2, :], start=True, stop=True))

            def out_x(b):
                half = 64 * (b % 2)
                pe.wait_ge(onx_ready.sem, b + 1)
                if b >= 1:
                    pe.wait_ge(yx_read.sem, b)
                for g in range(2):
                    last = pe.matmul(bank(7)[half:half + 64, D:2 * D], x0["wo"][:, g, :],
                                     onx[:, b % 2, g * D:(g + 1) * D], start=(g == 0), stop=(g == 1))
                yx_ps.by(last)

            for j in range(NT):
                if j == 0:
                    pe.wait_ge(loaded["ctx"].sem, 16)
                    pe.wait_ge(loaded["w_xattn0"].sem, 16)
                    pe.wait_ge(x_norm.sem, NT)
                for p in range(2):
                    if j >= 2:
                        pe.wait_ge(vx_sb.sem, 2 * (j - 2) + p + 1)
                    for sc in range(2):
                        last = pe.matmul(bank(2 * (j % 2) + p)[:, sc * S:(sc + 1) * S],
                                         ctok[64 * p:64 * p + 64, j, sc * P:(sc + 1) * P],
                                         x0["wv"][64 * p:64 * p + 64, :], start=True, stop=True)
                    vx_ps.by(last)
            pe.wait_ge(vx_sb.sem, 2 * NT)
            for u in range(2 * NT + 2):
                if u < 2 * NT:
                    project(u)
                if 1 <= u <= 2 * NT:
                    rotate(u - 1)
                if u >= 2:
                    replicate(u - 2)
            pe.wait_ge(st_ready.sem, 4 * NT)
            pe.wait_ge(selm_ready.sem, 2)
            for h in range(HX):
                first_scores_x(0, h)
            turn_max(0)
            for b in range(B):
                for h in range(HX):
                    if b + 1 < B:
                        for n in a_steps()[h]:
                            first_scores_x(b + 1, n)
                        if h == 6:
                            turn_max(b + 1)
                    if h == 2 and b >= 1:
                        sums_x(b - 1)
                    if h == 7 and b >= 1:
                        out_x(b - 1)
                    scores_x(b, h)
                    if b or h:
                        values_x(*divmod(b * HX + h - 1, HX))
            values_x(B - 1, HX - 1)
            sums_x(B - 1)
            out_x(B - 1)
            def unseen(experts, out):
                for e in experts:
                    for ic in range(IC0):
                        last = pe.matmul(out[0:E0, 0:D], b1_cols[:, e, ic, :], w2v[:, e, ic, :],
                                         start=(e == experts[0] and ic == 0), stop=(e == experts[-1] and ic == IC0 - 1))
                ce_ps.by(last)

            def turn_rows(r):
                pe.wait_ge(xs_in[r % 2].sem, xs_in[r % 2].base + 16 * (r // 2 + 1))
                if r >= 2:
                    pe.wait_ge(xst_sb.sem, xst_sb.base + r - 1)
                for k in range(KC):
                    last = pe.transpose(bank(6 + r % 2)[:, k * P:(k + 1) * P], xs[:, r % 2, k * P:(k + 1) * P], ident)
                xst_ps.by(last)

            def up(r):
                e = pe.value_load(tile_e_i[0:1, r:r + 1], min_val=0, max_val=E0 - 1)
                pe.wait_ge(xst_sb.sem, xst_sb.base + r + 1)
                for n in range(2):
                    if r >= 1:
                        pe.wait_ge(hid_ready.sem, hid_ready.base + 2 * (r - 1) + n + 1)
                    cols = slice(n * BANK, (n + 1) * BANK)
                    pe.matmul(bank(n), b1_pick[:, bass.ds(e, 1), :].rearrange("p a t -> p (a t)"), b1_terms[:, cols],
                              start=True, stop=False)
                    for k in range(KC):
                        last = pe.matmul(bank(n), xst[:, r % 2, k, :], w1v[:, bass.ds(e, 1), k, cols],
                                         start=False, stop=(k == KC - 1))
                    up_ps.by(last)

            def turn_hidden(r):
                for n in range(2):
                    pe.wait_ge(hid_ready.sem, hid_ready.base + 2 * r + n + 1)
                    if r >= 1:
                        pe.wait_ge(hidt_sb.sem, hidt_sb.base + 2 * (r - 1) + n + 1)
                    for i in range(4):
                        at = n * BANK + i * P
                        last = pe.transpose(bank(2 + n)[:, i * P:(i + 1) * P], hid[:, r % 2, at:at + P], ident)
                    hidt_ps.by(last)

            def down(r):
                e = pe.value_load(tile_e_i[0:1, r:r + 1], min_val=0, max_val=E0 - 1)
                if r >= 2:
                    pe.wait_ge(ys_ready.sem, r - 1)
                for ic in range(IC0):
                    if ic % 4 == 0:
                        pe.wait_ge(hidt_sb.sem, hidt_sb.base + 2 * r + ic // 4 + 1)
                    last = pe.matmul(bank(4 + r % 2)[:, 0:D], hidt[:, r % 2, ic * P:(ic + 1) * P],
                                     w2v[:, bass.ds(e, 1), ic, :], start=(ic == 0), stop=(ic == IC0 - 1))
                down_ps.by(last)

            turn_x(1)
            pe.wait_ge(loaded["w_route0"].sem, 16)
            for n in range(2):
                pe.wait_ge(xt_sb.sem, NT + 4 * n + 4)
                for k in range(KC):
                    last = pe.matmul(bank(2 + n), r0["rw1"][:, k, :], xt[:, k, n * BANK:(n + 1) * BANK],
                                     start=(k == 0), stop=(k == KC - 1))
                r1_ps.by(last)
            for j in range(NT):
                pe.wait_ge(r1_sb.sem, j // 4 + 1)
                last = pe.matmul(bank(4)[:, j * E0:(j + 1) * E0], r1[:, j * P:(j + 1) * P], r0["rw2"],
                                 start=True, stop=True)
            lg_ps.by(last)
            pe.wait_ge(b1_spread.sem, 1)
            pe.wait_ge(w12_early.sem, 16 * 2 * len(EARLY))
            unseen(EARLY, bank(7))
            pe.wait_ge(marks_ready.sem, 1)
            for j in range(NT):
                last = pe.matmul(bank(5)[:, 0:2 * E0], c["ones"], marks[:, j, :], start=(j == 0),
                                 stop=(j == NT - 1))
            pe.matmul(bank(6)[:, 0:NT * E0], c["before"], both, start=True, stop=False)
            last = pe.matmul(bank(6)[:, 0:NT * E0], c["ones"], earlier, start=False, stop=True)
            cnt_ps.by(last)
            pe.wait_ge(wc_ready.sem, 1)
            for i in range(2):
                for t in range(4):
                    last = pe.transpose(bank(2 + i)[0:2 * E0, t * P:(t + 1) * P], weight_c[:, 4 * i + t, :], ident)
                wct_ps.by(last)
            pe.wait_ge(tiles_ready.sem, tiles_ready.base + 1)
            pe.wait_ge(b1_ready.sem, b1_ready.base + 1)
            pe.wait_ge(wct_sb.sem, 2)
            pe.wait_ge(cet_sb.sem, 1)
            pe.wait_ge(w12_in.sem, 16 * 2 * (E0 - len(EARLY)))
            turn_rows(0)
            for r in range(ROW_TILES + 2):
                if r + 1 < ROW_TILES:
                    turn_rows(r + 1)
                if r < ROW_TILES:
                    up(r)
                if 1 <= r <= ROW_TILES:
                    turn_hidden(r - 1)
                if r >= 2:
                    down(r - 2)
            unseen(range(min(EARLY)), bank(6))
            pe.wait_ge(b2_in.sem, 16)
            pe.wait_ge(ceb_sb.sem, 1)
            for j in range(NT):
                if j >= 2:
                    pe.wait_ge(const_read.sem, j - 1)
                const_ps.by(pe.matmul(bank(j % 2)[:, 0:D], wct[0:2 * E0, j * P:(j + 1) * P], ceb[0:2 * E0, :],
                                      start=True, stop=True))
            turn_x(2)
            pe.wait_ge(loaded["w_attn1"].sem, 16)
            for j in range(NT):
                pe.wait_ge(xt_sb.sem, 2 * NT + j + 1)
                if j >= 2:
                    pe.wait_ge(pj1_sb.sem, j - 1)
                for k in range(KC):
                    pe.matmul(bank(2 + 2 * (j % 2)), xt[:, k, j * P:(j + 1) * P], a1["wqk"][:, k, :],
                              start=(k == 0), stop=(k == KC - 1))
                for k in range(KC):
                    last = pe.matmul(bank(3 + 2 * (j % 2))[:, 0:D + H1], xt[:, k, j * P:(j + 1) * P],
                                     a1["wvb"][:, k, :], start=(k == 0), stop=(k == KC - 1))
                pj1_ps.by(last)
            for j in range(NT):
                pe.wait_ge(turned1.sem, j + 1)
                for half in range(2):
                    if j >= 1:
                        pe.wait_ge(ft_sb.sem, 2 * (j - 1) + half + 1)
                    src = ((rq1[:, j % 2, 0:D], kw1[:, j % 2, :]), (rq1[:, j % 2, D:2 * D], vz1[:, j, 0:D]))[half]
                    for i in range(4):
                        last = pe.transpose(bank(6 + half)[:, i * P:(i + 1) * P],
                                            src[i // 2][:, (i % 2) * P:(i % 2 + 1) * P], ident)
                    tr1_ps.by(last)

            def scores1(w):
                j, k = divmod(w, 2)
                pe.wait_ge(kb1_ready.sem, j + 1)
                pe.wait_ge(kb1_last.sem, kb1_last.base + j + 1)
                if w >= 2:
                    pe.wait_ge(sm_ready.sem, w - 1)
                if k == 0:
                    pe.matmul(bank(2 + w % 2), ident, wide(c["causal"], 1, 8), start=True, stop=False)
                for p in range(2):
                    b = 2 * j + p
                    last = pe.matmul(bank(2 + w % 2)[64 * p:64 * p + 64, :], ft1[:, 0, k, b * S:(b + 1) * S],
                                     kb1[:, b % 4, k, :, :], start=(k == 1), stop=True)
                a1_ps.by(last)

            def turn_probs1(w):
                pe.wait_ge(sm_exp.sem, w + 1)
                if w >= 2:
                    pe.wait_ge(pt_sb.sem, w - 1)
                for i in range(4):
                    last = pe.transpose(bank(4 + w % 2)[:, i * P:(i + 1) * P], sm1[:, w % 2, i * P:(i + 1) * P],
                                        ident)
                pt_ps.by(last)

            pe.wait_ge(ft_sb.sem, 2 * NT)
            for w in range(2 * NT + 1):
                if w < 2 * NT:
                    scores1(w)
                if w >= 1:
                    turn_probs1(w - 1)

            pe.wait_ge(vnt_in.sem, 16 * KC)
            for b in range(B):
                if b >= 8 and b % 4 == 0:
                    pe.wait_ge(vb1_sb.sem, b // 4 - 1)
                for r in range(2):
                    for k in range(KC):
                        at = (b % 4) * P + k * 64
                        last = pe.matmul(bank(6 + b // 4 % 2)[64 * r:64 * r + 64, at:at + 64],
                                         vnt1[:, k, b * S:(b + 1) * S],
                                         ident.rearrange("p (q r c) -> p q r c", r=2, c=DH1)[:, :, r, :],
                                         start=True, stop=True)
                if b % 4 == 3:
                    vb1_ps.by(last)

            def values1(j):
                pe.wait_ge(vb1_sb.sem, j // 2 + 1)
                if j >= 2:
                    pe.wait_ge(on1_ready.sem, j - 1)
                for p in range(2):
                    for q in range(8):
                        at = q * 34
                        last = pe.matmul(bank(j % 2)[64 * p:64 * p + 64, at:at + 34],
                                         pt1[:, 2 * j + q // 4, (q % 4) * P + 64 * p:(q % 4) * P + 64 * p + 64],
                                         vb1[:, 2 * j + p, q, :], start=True, stop=True)
                o1_ps.by(last)

            def turn_out1(j):
                pe.wait_ge(on1_ready.sem, j + 1)
                if j >= 2:
                    pe.wait_ge(ot1_sb.sem, j - 1)
                for k in range(KC):
                    last = pe.transpose(bank(2 + j % 2)[:, k * P:(k + 1) * P], on1[:, j % 2, k * P:(k + 1) * P],
                                        ident)
                ot1_ps.by(last)

            def out1(j):
                pe.wait_ge(ot1_sb.sem, j + 1)
                if j >= 2:
                    pe.wait_ge(y1_read.sem, j - 1)
                for k in range(KC):
                    last = pe.matmul(bank(4 + j % 2)[:, 0:D], ot1[:, j % 2, k, :], a1["wo"][:, k, :],
                                     start=(k == 0), stop=(k == KC - 1))
                y1_ps.by(last)

            pe.wait_ge(pt_sb.sem, 2 * NT)
            for j in range(NT + 2):
                if j < NT:
                    values1(j)
                if 1 <= j <= NT:
                    turn_out1(j - 1)
                if j >= 2:
                    out1(j - 2)
            pe.wait_ge(x_norm.sem, 4 * NT)
            pe.wait_ge(loaded["ctx"].sem, 32)
            for j in range(NT):
                if j >= 2:
                    pe.wait_ge(ct_sb.sem, j - 1)
                for k in range(KC):
                    last = pe.transpose(bank(6 + j % 2)[:, k * P:(k + 1) * P], ctok[:, j, k * P:(k + 1) * P], ident)
                ct_ps.by(last)
            turn_x(3)
            pe.wait_ge(loaded["w_xattn1"].sem, 16)
            for u in range(8):
                n, m = u // 2 % 2, u % 2
                if u < 4:
                    pe.wait_ge(ct_sb.sem, 4 * n + 4)
                else:
                    pe.wait_ge(xt_sb.sem, 3 * NT + 4 * n + 4)
                if u >= 2:
                    pe.wait_ge(kq5_sb.sem, u - 1)
                w, src = (x1["wk"], ct5) if u < 4 else (x1["wq"], xt)
                for k in range(KC):
                    last = pe.matmul(bank(2 + u % 2), w[:, k, m * P:(m + 1) * P],
                                     src[:, k, n * BANK:(n + 1) * BANK], start=(k == 0), stop=(k == KC - 1))
                kq5_ps.by(last)
            for b in range(B):
                if b % 4 == 0 and b >= 8:
                    pe.wait_ge(v5_sb.sem, b // 4 - 1)
                for r in range(2):
                    for k in range(KC):
                        last = pe.matmul(bank(4 + b // 4 % 2)[64 * r:64 * r + 64, (b % 4) * P:(b % 4 + 1) * P],
                                         ct5[:, k, b * S:(b + 1) * S],
                                         x1["wv"][:, k, :].rearrange("p (q r c) -> p q r c", r=2, c=DH1)[:, :, r, :],
                                         start=(k == 0), stop=(k == KC - 1))
                if b % 4 == 3:
                    v5_ps.by(last)

            def scores5(b):
                pe.wait_ge(kb5_ready.sem, b + 1)
                if b >= 2:
                    pe.wait_ge(s5_ready.sem, b - 1)
                for q in range(8):
                    last = pe.matmul(bank(4 + b % 2)[:, q * S:(q + 1) * S],
                                     kb5[:, (b % 4) * KC + q // 4, 2 * (q % 4):2 * (q % 4) + 2, :],
                                     q5[:, q // 4, b * S:(b + 1) * S], start=True, stop=True)
                b5_ps.by(last)

            def values5(b):
                j, half = b // 2, 64 * (b % 2)
                pe.wait_ge(pt5_ready.sem, b + 1)
                if j >= 2 and b % 2 == 0:
                    pe.wait_ge(on5_ready.sem, j - 1)
                for q in range(8):
                    last = pe.matmul(bank(6 + j % 2)[half:half + 64, q * 34:(q + 1) * 34],
                                     pt5[:, b % 2, q * S:(q + 1) * S], vb5[:, b, q, :], start=True, stop=True)
                o5_ps.by(last)

            def turn_out5(j):
                pe.wait_ge(on5_ready.sem, j + 1)
                if j >= 2:
                    pe.wait_ge(ot5_sb.sem, j - 1)
                for k in range(KC):
                    last = pe.transpose(bank(j % 2)[:, k * P:(k + 1) * P], on5[:, j % 2, k * P:(k + 1) * P], ident)
                ot5_ps.by(last)

            def out5(j):
                pe.wait_ge(ot5_sb.sem, j + 1)
                if j >= 2:
                    pe.wait_ge(y5_read.sem, j - 1)
                for k in range(KC):
                    last = pe.matmul(bank(2 + j % 2)[:, 0:D], ot5[:, j % 2, k, :], x1["wo"][:, k, :],
                                     start=(k == 0), stop=(k == KC - 1))
                y5_ps.by(last)

            pe.wait_ge(kq5_sb.sem, 8)
            pe.wait_ge(v5_sb.sem, 4)
            scores5(0)
            for b in range(B + 4):
                if b + 1 < B:
                    scores5(b + 1)
                if b < B:
                    values5(b)
                if b % 2 == 0 and 2 <= b <= B:
                    turn_out5(b // 2 - 1)
                if b % 2 == 0 and b >= 4:
                    out5(b // 2 - 2)
            def gate_up(lhs_gate, lhs_up, c4, n):
                for i, w in enumerate((lhs_gate, lhs_up)):
                    v = (n * len(SHARED) + c4) * 2 + i
                    if v >= 4:
                        w_before = v - 4
                        pe.wait_ge((sh_silu, sh_h)[i].sem, (sh_silu, sh_h)[i].base + w_before // 2 + 1)
                    for k in range(KC):
                        last = pe.matmul(bank(v % 4)[0:SHARED[c4], :], w[:, k, c4 * P:c4 * P + SHARED[c4]],
                                         xt[:, k, n * BANK:(n + 1) * BANK], start=(k == 0), stop=(k == KC - 1))
                    sh_ps.by(last)

            def fuse_in(n):
                f, half = n // 2, n % 2
                if half == 0:
                    pe.wait_ge(experts_in[f % 2].sem, 16 * (f // 2 + 1))
                cols = slice(half * BANK, (half + 1) * BANK)
                for k in range(KC):
                    bank_free(pe, (("x", k), n))
                    mid_ps.by(pe.matmul(bank(ring[("x", k), n] % 4), f1["mask_up"][:, f, k * P:(k + 1) * P],
                                        wt6[0:E1, cols], start=True, stop=True))
                bank_free(pe, (("w", 0), n))
                mid_ps.by(pe.matmul(bank(ring[("w", 0), n] % 4), c["spread"][:, f, :], wt6[0:E1, cols],
                                    start=True, stop=True))

            def ranks(n):
                pe.wait_ge(mid_dve.sem, mid_dve.base + by_dve[("x", 1), n] + 1)
                bank_free(pe, (("a", 0), n))
                for k in range(KC):
                    last = pe.matmul(bank(ring[("a", 0), n] % 4), ex[n // 2 % 2]["qa"][:, k, :], xe6[:, n % 2, k, :],
                                     start=(k == 0), stop=(k == KC - 1))
                mid_ps.by(last)

            def features(n):
                e, half = ex[n // 2 % 2], n % 2
                for kind, w, r0, r1, m, q0 in (("g", "gw", 0, 64, P, 0), ("u", "uw", 64, P, P, 0), ("t", "tw", 0, P, TAILS, P)):
                    key = ((kind, 0), n)
                    bank_free(pe, key)
                    out = bank(ring[key] % 4)[0:m, :]
                    for k in range(KC):
                        pe.matmul(out, e[w][:, k, :], xe6[:, half, k, :], start=(k == 0), stop=False)
                    if kind == "g":
                        pe.wait_ge(mid_dve.sem, mid_dve.base + by_dve[("a", 0), n] + 1)
                        pe.wait_ge(qb6_ready.sem, qb6_ready.base + 2 * (n // 2) + 2)
                    mid_ps.by(pe.matmul(out, qb6[r0:r1, n // 2 % 2, q0:q0 + m], aw6[r0:r1, half, :], start=False,
                                        stop=True))

            def outputs(n):
                e, half = ex[n // 2 % 2], n % 2
                key = (("d", 0), n)
                bank_free(pe, key)
                pe.wait_ge(mid_dve.sem, mid_dve.base + by_dve[("t", 0), n] + 1)
                for i in range(2):
                    last = pe.matmul(bank(ring[key] % 4)[0:64, :], e[("dqa", "dqat")[i]],
                                     h6[0:(P, TAIL)[i], 2 * half + i, :],
                                     start=(i == 0), stop=(i == 1))
                mid_ps.by(last)
                for t in range(4):
                    if n >= 1:
                        pe.wait_ge(out6_read.sem, out6_read.base + 4 * (n - 1) + t + 1)
                    else:
                        pe.wait_ge(sho_read.sem, sho_read.base + 5 + t)
                    out = bank(4 + t)[:, 0:D]
                    for i in range(2):
                        pe.matmul(out, h6[0:(P, TAIL)[i], 2 * half + i, t * P:(t + 1) * P],
                                  e[("dw", "dwt")[i]], start=(i == 0),
                                  stop=False)
                    if t == 0:
                        pe.wait_ge(mid_dve.sem, mid_dve.base + by_dve[key] + 1)
                    out6_ps.by(pe.matmul(out, adw6[0:64, t * P:(t + 1) * P], dqb6[0:64, n // 2 % 2, :], start=False,
                                         stop=True))

            turn_x(4)
            pe.wait_ge(loaded["w_ffn1"].sem, 16)
            for j in range(NT):
                pe.wait_ge(xt_sb.sem, 4 * NT + j + 1)
                for k in range(KC):
                    last = pe.matmul(bank(4)[:, j * E1:(j + 1) * E1], xt[:, k, j * P:(j + 1) * P],
                                     f1["gate"][:, k, :], start=(k == 0), stop=(k == KC - 1))
            lg6_ps.by(last)

            def shared_down(n):
                pe.wait_ge(sh_h.sem, sh_h.base + len(SHARED) * (n + 1))
                for t in range(4):
                    if n >= 1:
                        pe.wait_ge(sho_read.sem, sho_read.base + t + 1)
                    for c4, rows in enumerate(SHARED):
                        last = pe.matmul(bank(4 + t)[:, 0:D], hs6[0:rows, c4, t * P:(t + 1) * P],
                                         f1["shd"][0:rows, c4, :], start=(c4 == 0), stop=(c4 == len(SHARED) - 1))
                    sho_ps.by(last)

            for c4 in range(len(SHARED)):
                gate_up(f1["shg"], f1["shu"], c4, 0)
            pe.wait_ge(wd6_ready.sem, wd6_ready.base + 1)
            for j in range(NT):
                last = pe.transpose(bank(4 + j // 4)[0:E1, (j % 4) * P:(j % 4 + 1) * P], prob6[:, j, :], ident)
                if j % 4 == 3:
                    wd6_ps.by(last)
            pe.wait_ge(sh_h.sem, sh_h.base + len(SHARED))
            pe.wait_ge(wd6_sb.sem, wd6_sb.base + 2)
            pe.wait_ge(sel6_ready.sem, sel6_ready.base + 1)
            for j in range(NT):
                last = pe.matmul(bank(1)[:, j * E1:(j + 1) * E1], wd6[0:E1, j * P:(j + 1) * P], map_f[0:E1, :],
                                 start=True, stop=True)
            flat6_ps.by(last)
            shared_down(0)
            gate_up(f1["shg"], f1["shu"], 0, 1)
            pe.wait_ge(m6_sub.sem, m6_sub.base + 1)
            for c4 in range(1, len(SHARED)):
                gate_up(f1["shg"], f1["shu"], c4, 1)
            pe.wait_ge(mix6_ready.sem, mix6_ready.base + 1)
            pe.wait_ge(sho_read.sem, sho_read.base + 2)
            for j in range(NT):
                last = pe.transpose(bank(4 + j // 4)[0:E1, (j % 4) * P:(j % 4 + 1) * P],
                                    mix6.rearrange("p (j f) k -> p j (f k)", f=FX)[:, j, :], ident)
                if j % 4 == 3:
                    wt6_ps.by(last)
            pe.wait_ge(wt6_sb.sem, wt6_sb.base + 2)
            shared_down(1)
            for step in range(-1, STEPS + 1):
                if step + 1 < STEPS:
                    fuse_in(step + 1)
                if step >= 1:
                    outputs(step - 1)
                if step + 1 < STEPS:
                    ranks(step + 1)
                if 0 <= step < STEPS:
                    features(step)

        @block.scalar
        def _(act):
            def do(instruction, s=act_step):
                act.wait_ge(s.sem, s.by(instruction))

            def copy_xt(use):
                for j in range(NT):
                    t = use * NT + j
                    act.wait_ge(xt_ps.sem, t + 1)
                    xt_sb.by(act.activation(xt[:, :, j * P:(j + 1) * P],
                                            bank(t % 2)[:, 0:D].rearrange("p (k n) -> p k n", k=KC), ACT.Copy))

            def ln_sqrt(use):
                act.wait_ge(ln_var.sem, use + 1)
                ln_std.by(act.activation(std, rstd, ACT.Sqrt))

            copy_xt(0)
            for u in range(6):
                n, pair = (u // 2, u % 2) if u < 4 else (u - 4, None)
                act.wait_ge(q_ps.sem, u + 1)
                src = bank(2 + u % 2)
                at = slice(n * BANK, (n + 1) * BANK)
                if pair is None:
                    last = act.activation(kt0[0:DKV, at], src[0:DKV, :], ACT.Copy)
                else:
                    act.activation(q4[0:DKV, 8 * n:8 * n + 8, 2 * pair, :],
                                   src[0:DKV, :].rearrange("p (b s) -> p b s", s=S), ACT.Copy)
                    last = act.activation(q4[0:DKV, 8 * n:8 * n + 8, 2 * pair + 1, :],
                                          src[DKV:P, :].rearrange("p (b s) -> p b s", s=S), ACT.Copy)
                q_sb.by(last)
            act.wait_ge(loaded["w_attn0"].sem, 16)
            gate_exp.by(act.activation(gate0[:, 0:1], a0["memw"], ACT.Exp, scale=-1.0))
            act.wait_ge(elu_min.sem, 1)
            elu_exp.by(act.activation(sig[0:DKV, :, :], sig[0:DKV, :, :], ACT.Exp))
            for b in range(B):
                act.wait_ge(nmt0_ps.sem, b + 1)
                nmt0_sb.by(act.activation(q4[DKV:DKV + H0, b, :, :],
                                          bank(4)[0:H0, 0:D].rearrange("p (g s) -> p g s", g=NQ), ACT.Copy))
                act.wait_ge(b0_ps.sem, b + 1)
                if b >= 2:
                    act.wait_ge(o0_ps.sem, b - 1)
                pt0_ready.by(act.activation(pt0[:, b % 2, :, :].rearrange("p a b -> p (a b)"), bank(5, 2), ACT.Exp,
                                            scale=float(DH0) ** -0.5))
            ln_sqrt(0)

            def hi_part(u):
                for p in range(2):
                    act.wait_ge(rep_ps.sem, 2 * u + p + 1)
                    if u >= 2:
                        act.wait_ge(st_ready.sem, 2 * (u - 2) + p + 1)
                    hi_ready.by(act.activation(hi16[:, u % 2, p, :], bank(4 + 2 * (u % 2) + p), ACT.Copy))

            act.wait_ge(loaded["w_xattn0"].sem, 16)
            for u in range(2 * NT + 2):
                if u < 2 * NT:
                    act.wait_ge(pj_ps.sem, u + 1)
                    if u >= 2:
                        act.wait_ge(qr_ready.sem, u - 1)
                    pj_sb.by(act.activation(qs[:, u % 2, :], bank(u % 2)[:, 0:D], ACT.Identity,
                                            bias=x0["bk" if u < NT else "bq"]))
                if u >= 2:
                    hi_part(u - 2)

            def copy_max(b):
                act.wait_ge(nmtx_ps.sem, b + 1)
                if b >= 2:
                    act.wait_ge(bx_ps.sem, HX * (b - 1))
                nmtx_sb.by(act.activation(nmtx[:, b % 2, :], bank(4).bitcast(BF16)[:, 0:D], ACT.Copy))

            def copy_out(b):
                act.wait_ge(pvx_done.sem, HX * (b + 1))
                if b >= 2:
                    act.wait_ge(onx_ready.sem, b - 1)
                otx_sb.by(act.activation(otx[:, b % 2, :], bank(5 + b % 2), ACT.Copy))

            copy_max(0)
            for b in range(B):
                for h in range(HX):
                    u = b * HX + h
                    if h == 6 and b + 1 < B:
                        copy_max(b + 1)
                    if h == 2 and b >= 1:
                        copy_out(b - 1)
                    act.wait_ge(bx_ps.sem, u + 1)
                    if u >= 2:
                        act.wait_ge(pvx_done.sem, u - 1)
                    ptx_ready.by(act.activation(ptx[:, u % 2, :, :].rearrange("p a b -> p (a b)"),
                                                bank(2 + u % 2), ACT.Exp, scale=float(DHX) ** -0.5))
            copy_out(B - 1)
            ln_sqrt(1)
            copy_xt(1)
            act.wait_ge(loaded["w_route0"].sem, 16)
            b1_gelu.by(act.activation(b1g, r0["b1"], ACT.Gelu))
            for n in range(2):
                act.wait_ge(r1_ps.sem, n + 1)
                r1_sb.by(act.activation(r1[:, n * BANK:(n + 1) * BANK], bank(2 + n), ACT.Gelu))
            act.wait_ge(p_sub.sem, 1)
            p_exp.by(act.activation(prob, prob, ACT.Exp))
            for i in range(2):
                act.wait_ge(wct_ps.sem, i + 1)
                wct_sb.by(act.activation(wct[0:2 * E0, i * BANK:(i + 1) * BANK], bank(2 + i)[0:2 * E0, :],
                                         ACT.Copy))
            for r in range(ROW_TILES):
                for n in range(2):
                    act.wait_ge(up_ps.sem, up_ps.base + 2 * r + n + 1)
                    if r >= 2:
                        act.wait_ge(hidt_ps.sem, hidt_ps.base + 2 * (r - 2) + n + 1)
                    hid_ready.by(act.activation(hid[:, r % 2, n * BANK:(n + 1) * BANK], bank(n), ACT.Gelu))
            ln_sqrt(2)
            copy_xt(2)
            for j in range(NT):
                act.wait_ge(pj1_ps.sem, j + 1)
                act.activation(qk1[:, j, :], bank(2 + 2 * (j % 2)), ACT.Copy)
                if j >= 2:
                    act.wait_ge(ss_part.sem, j - 1)
                act.activation(sq1[:, j % 2, :], bank(2 + 2 * (j % 2))[:, D:2 * D], ACT.Square)
                pj1_sb.by(act.activation(vz1[:, j, :], bank(3 + 2 * (j % 2))[:, 0:D + H1], ACT.Copy))
            act.wait_ge(pj1_sb.sem, NT)
            act.wait_ge(ss_ready.sem, 1)
            ss_std.by(act.activation(std1, rk1, ACT.Sqrt))
            bz_exp.by(act.activation(beta1, vz1[:, :, D:D + H1], ACT.Exp, scale=-1.0))
            for j in range(NT):
                for half in range(2):
                    act.wait_ge(tr1_ps.sem, 2 * j + half + 1)
                    ft_sb.by(act.activation(ft1[:, 2 * half:2 * half + 2, :, j * P:(j + 1) * P],
                                            bank(6 + half).rearrange("p (n k t) -> p n k t", n=2, k=KC), ACT.Copy))
            for w in range(2 * NT + 1):
                if w < 2 * NT:
                    act.wait_ge(sm_ready.sem, w + 1)
                    sm_exp.by(act.activation(sm1[:, w % 2, :], sm1[:, w % 2, :], ACT.Exp,
                                             scale=float(DH1) ** -0.5))
                if w >= 1:
                    act.wait_ge(pt_ps.sem, w)
                    pt_sb.by(act.activation(pt1[:, w - 1, :], bank(4 + (w - 1) % 2), ACT.Copy))
            for j in range(NT):
                act.wait_ge(ot1_ps.sem, j + 1)
                if j >= 2:
                    act.wait_ge(y1_ps.sem, j - 1)
                ot1_sb.by(act.activation(ot1[:, j % 2, :, :], bank(2 + j % 2)[:, 0:D]
                                         .rearrange("p (k t) -> p k t", k=KC), ACT.Copy))
            ln_sqrt(3)
            for j in range(NT):
                act.wait_ge(ct_ps.sem, j + 1)
                ct_sb.by(act.activation(ct5[:, :, j * P:(j + 1) * P],
                                        bank(6 + j % 2)[:, 0:D].rearrange("p (k t) -> p k t", k=KC), ACT.Copy))
            copy_xt(3)
            act.wait_ge(loaded["w_xattn1"].sem, 16)
            for u in range(8):
                n, m = u // 2 % 2, u % 2
                act.wait_ge(kq5_ps.sem, u + 1)
                dst, bias = (k5, x1["bk"]) if u < 4 else (q5, x1["bq"])
                kq5_sb.by(act.activation(dst[:, m, n * BANK:(n + 1) * BANK], bank(2 + u % 2), ACT.Identity,
                                         bias=bias[:, m:m + 1]))

            def copy_out5(j):
                act.wait_ge(ot5_ps.sem, j + 1)
                if j >= 2:
                    act.wait_ge(y5_ps.sem, j - 1)
                ot5_sb.by(act.activation(ot5[:, j % 2, :, :], bank(j % 2)[:, 0:D]
                                         .rearrange("p (k t) -> p k t", k=KC), ACT.Copy))

            for b in range(B):
                act.wait_ge(s5_ready.sem, b + 1)
                if b >= 2:
                    act.wait_ge(o5_ps.sem, b - 1)
                pt5_ready.by(act.activation(pt5[:, b % 2, :], s5[:, b % 2, :], ACT.Exp, bias=off5[:, b:b + 1]))
                if b % 2 == 1 and b >= 3:
                    copy_out5(b // 2 - 1)
            copy_out5(NT - 1)
            ln_sqrt(4)
            ln_sqrt(5)
            copy_xt(4)
            act.wait_ge(p6_sub.sem, p6_sub.base + 1)
            p6_exp.by(act.activation(prob6, prob6, ACT.Exp))

            def shared_silu(n):
                for c4, rows in enumerate(SHARED):
                    v = (n * len(SHARED) + c4) * 2
                    act.wait_ge(sh_ps.sem, sh_ps.base + v + 1)
                    if n >= 1:
                        act.wait_ge(sh_h.sem, sh_h.base + c4 + 1)
                    sh_silu.by(act.activation(g6[0:rows, c4, :], bank(v % 4)[0:rows, :], ACT.Silu))

            shared_silu(0)
            for i in range(2):
                act.wait_ge(wd6_ps.sem, wd6_ps.base + i + 1)
                wd6_sb.by(act.activation(wd6[0:E1, i * BANK:(i + 1) * BANK], bank(4 + i)[0:E1, :], ACT.Copy))
            act.wait_ge(m6_sub.sem, m6_sub.base + 1)
            m6_exp.by(act.activation(mix6, mix6, ACT.Exp))
            shared_silu(1)
            for i in range(2):
                act.wait_ge(wt6_ps.sem, wt6_ps.base + i + 1)
                wt6_sb.by(act.activation(wt6[0:E1, i * BANK:(i + 1) * BANK], bank(4 + i)[0:E1, :], ACT.Copy))
            for step in range(-1, STEPS + 1):
                n = step + 1
                if n < STEPS:
                    act.wait_ge(mid_ps.sem, mid_ps.base + ring[("w", 0), n] + 1)
                    if n >= 3:
                        act.wait_ge(mid_dve.sem, mid_dve.base + by_dve[("d", 0), n - 3] + 1)
                    mid_act.by(act.activation(we6[:, n % 3, :], bank(ring[("w", 0), n] % 4), ACT.Copy))
                n = step
                if 0 <= n < STEPS:
                    for i, (kind, src, dst) in enumerate((("g", slice(0, P), slice(0, P)),
                                                          ("t", slice(0, TAIL), slice(64, 64 + TAIL)))):
                        act.wait_ge(mid_ps.sem, mid_ps.base + ring[(kind, 0), n] + 1)
                        if n >= 2:
                            act.wait_ge(mid_dve.sem, mid_dve.base + by_dve[("ut"[i], 0), n - 2] + 1)
                        else:
                            act.wait_ge(sh_h.sem, sh_h.base + 2 * len(SHARED))
                        mid_act.by(act.activation(g6[dst, 2 * (n % 2) + i, :], bank(ring[(kind, 0), n] % 4)[src, :],
                                                  ACT.Silu))
            ln_sqrt(6)

        @block.vector
        def _(dve):
            def do(instruction, s=dve_step):
                dve.wait_ge(s.sem, s.by(instruction))

            def each_tile(*steps):
                before = [0] * NT
                for step in steps:
                    for j in range(NT):
                        if before[j]:
                            dve.wait_ge(dve_step.sem, before[j])
                        before[j] = dve_step.by(step(j))
                dve.wait_ge(dve_step.sem, before[NT - 1])

            def tile_stats(j):
                do(dve.bn_stats(stats[:, j, :], x[:, j, :]))
                do(dve.bn_aggr(mean_var[:, j, :], stats[:, j, :]))

            def normalise(use):
                do(dve.tensor_scalar(rstd, mean_var[:, :, 1], EPS, None, ALU.add), ln_var)
                dve.wait_ge(ln_std.sem, use + 1)
                do(dve.reciprocal(rstd, std))
                for j in range(NT):
                    x_norm.by(dve.tensor_scalar(x[:, j, :], x[:, j, :], mean_var[:, j, 0:1], rstd[:, j:j + 1],
                                                ALU.subtract, ALU.mult))
                dve.wait_ge(x_norm.sem, x_norm.n)

            dve.wait_ge(gate_exp.sem, 1)
            do(dve.tensor_scalar(gate0[:, 1:2], gate0[:, 0:1], 1.0, None, ALU.add))
            do(dve.reciprocal(gate0[:, 2:3], gate0[:, 1:2]))
            do(dve.tensor_scalar(gate0[:, 3:4], gate0[:, 2:3], -1.0, 1.0, ALU.mult, ALU.add))
            dve.wait_ge(q_sb.sem, 4)
            for g in range(NQ):
                last = dve.tensor_scalar(sig[0:DKV, g, :].rearrange("p (b s) -> p b s", s=S), q4[0:DKV, :, g, :], 0.0,
                                         None, ALU.min)
            do(last, elu_min)
            dve.wait_ge(pool_step.sem, 5)
            for i in range(2):
                dve.wait_ge(v_ps.sem, i + 1)
                src = bank(4 + i)[:, 0:8 * 32].rearrange("p (b c) -> p b c", c=DH0)
                dst = vb0[:, 8 * i:8 * i + 8, :, :].rearrange("p b q (r c) -> p (b q) r c", r=2)
                dve.tensor_copy(dst[0:64, :, 0, 0:DH0], src[0:64, :, :])
                do(dve.tensor_copy(dst[64:128, :, 1, 0:DH0], src[64:128, :, :]), v_sb)
            dve.wait_ge(elu_exp.sem, 1)
            flat = sig[0:DKV, :, :].rearrange("p a b -> p (a b)")
            do(dve.tensor_scalar(flat, flat, -1.0, None, ALU.add))
            for g in range(NQ):
                v = sig[0:DKV, g, :].rearrange("p (b s) -> p b s", s=S)
                last = dve.scalar_tensor_tensor(out=v, in0=q4[0:DKV, :, g, :], scalar=0.0, in1=v, op0=ALU.max,
                                                op1=ALU.add)
            do(last, elu_ready)
            for j in range(NT):
                dve.wait_ge(mem_ps.sem, j + 1)
                src = bank(6 + j % 2)[:, 0:NQ * 65].rearrange("p (g c) -> p g c", g=NQ)
                do(dve.reciprocal(rm0, src[:, :, DKV]))
                do(dve.tensor_tensor(out=am[:, j, :].rearrange("p (g c) -> p g c", g=NQ), in0=src[:, :, 0:DKV],
                                     in1=wide(rm0, 2, DKV), op=ALU.mult), mem_read)
            for b in range(B + 3):
                if b < B:
                    for pair in range(2):
                        dve.wait_ge(a0_ps.sem, 2 * b + pair + 1)
                        if b >= 2:
                            dve.wait_ge(nmt0_ps.sem, b - 1)
                        a0_max.by(dve.tensor_reduce(
                            nm0[:, b % 2, pair, :], bank(2 * (b % 2) + pair).rearrange("p (h t) -> p h t", h=H0),
                            AX.X, ALU.max, negate=True))
                if b >= 4 and b % 2 == 0:
                    j = b // 2 - 2
                    dve.wait_ge(o0_ps.sem, b - 2)
                    src = bank(7)[:, 0:NQ * H0 * 9].rearrange("p (h c) -> p h c", c=9)
                    do(dve.reciprocal(rs0, src[:, :, DH0]))
                    do(dve.tensor_tensor(out=t0, in0=src[:, :, 0:DH0], in1=wide(rs0, 2, DH0), op=ALU.mult), o0_read)
                    do(dve.scalar_tensor_tensor(out=x[:, j, :], in0=t0.rearrange("p a b -> p (a b)"),
                                                scalar=gate0[:, 3:4], in1=x[:, j, :], op0=ALU.mult, op1=ALU.add))
                    do(dve.scalar_tensor_tensor(out=x[:, j, :], in0=am[:, j, :], scalar=gate0[:, 2:3],
                                                in1=x[:, j, :], op0=ALU.mult, op1=ALU.add))
                    tile_stats(j)
            normalise(0)

            dve.wait_ge(loaded["w_xattn0"].sem, 16)
            for j in range(NT):
                for p in range(2):
                    dve.wait_ge(vx_ps.sem, 2 * j + p + 1)
                    do(dve.tensor_tensor(
                        out=vx[:, 2 * j + p, :, :, 0:DHX],
                        in0=bank(2 * (j % 2) + p)[:, 0:2 * S].rearrange("p (s h c) -> p s h c", s=2, h=HX),
                        in1=wide(x0["bv"].rearrange("p (h c) -> p h c", h=HX), 1, 2), op=ALU.add), vx_sb)
            for u in range(2 * NT + 1):
                if u < 2 * NT:
                    dve.wait_ge(pj_sb.sem, u + 1)
                    do(dve.tensor_tensor(out=rope_a[:, u % 2, :], in0=qs[:, u % 2, :], in1=c["cosx"], op=ALU.mult))
                    dve.wait_ge(rot_ps.sem, u + 1)
                    do(dve.tensor_tensor(out=rope_b[:, u % 2, :], in0=bank(2 + u % 2)[:, 0:D], in1=c["sinx"],
                                         op=ALU.mult))
                    if u >= 2:
                        dve.wait_ge(rep_ps.sem, 2 * (u - 1))
                    do(dve.tensor_tensor(out=qr[:, u % 2, :], in0=rope_a[:, u % 2, :], in1=rope_b[:, u % 2, :],
                                         op=ALU.add), qr_ready)
                if u >= 1:
                    v = u - 1
                    side, j = ("k", v) if v < NT else ("q", v - NT)
                    for p in range(2):
                        dve.wait_ge(hi_ready.sem, 2 * v + p + 1)
                        do(dve.scalar_tensor_tensor(
                            out=stack[side][:, 2 * j + p, :, :].rearrange("p a b -> p (a b)"),
                            in0=hi16[:, v % 2, p, :], scalar=c["lo_" + side], in1=bank(4 + 2 * (v % 2) + p),
                            op0=ALU.mult, op1=ALU.add), st_ready)

            def row_max(b, h):
                u = b * HX + h
                dve.wait_ge(ax_ps.sem, u + 1)
                ax_max.by(dve.tensor_reduce(nmx[:, b % 2, :, h], bank(u % 2).rearrange("p (t s) -> p t s", t=2),
                                            AX.X, ALU.max, negate=True))

            def cast_max(b):
                dve.wait_ge(ax_max.sem, HX * (b + 1))
                if b >= 2:
                    dve.wait_ge(nmtx_ps.sem, b - 1)
                for tc in range(2):
                    last = dve.tensor_copy(nmxb[:, b % 2, tc, :].rearrange("p (i c) -> p i c", i=4)[:, :, 0:HX],
                                           wide(nmx[:, b % 2, tc, :], 1, 4))
                do(last, nmx_ready)

            def divide_x(b):
                dve.wait_ge(otx_ps.sem, b + 1)
                do(dve.reciprocal(rsx, bank(5 + b % 2)))
                if b >= 2:
                    dve.wait_ge(yx_ps.sem, b - 1)
                do(dve.tensor_tensor(out=onx[:, b % 2, :], in0=otx[:, b % 2, :], in1=rsx, op=ALU.mult), onx_ready)

            def add_x(b):
                j, half = b // 2, slice(64 * (b % 2), 64 * (b % 2) + 64)
                dve.wait_ge(yx_ps.sem, b + 1)
                do(dve.scalar_tensor_tensor(out=x[half, j, :], in0=bank(7)[half, D:2 * D],
                                            scalar=x0["bo"][half, :], in1=x[half, j, :], op0=ALU.add,
                                            op1=ALU.add), yx_read)
                if b % 2:
                    tile_stats(j)

            dve.wait_ge(selm_ready.sem, 1)
            do(dve.tensor_copy(ident16, c["ident"]), selm_ready)
            for h in range(HX):
                row_max(0, h)
            cast_max(0)
            for b in range(B):
                for h in range(HX):
                    if b + 1 < B:
                        for n in a_steps()[h]:
                            row_max(b + 1, n)
                        if h == 5:
                            cast_max(b + 1)
                    if h == 5 and b >= 1:
                        divide_x(b - 1)
                    if h == 7 and b >= 1:
                        add_x(b - 1)
            divide_x(B - 1)
            add_x(B - 1)
            normalise(1)
            def softmax_rows(logits, out, peak, exp_in, exp_out):
                width = out.shape[2]
                do(dve.tensor_reduce(peak, logits, AX.X, ALU.max))
                do(dve.tensor_tensor(out=out, in0=logits, in1=wide(peak, 2, width), op=ALU.subtract), exp_in)
                dve.wait_ge(exp_out.sem, exp_out.base + 1)
                do(dve.tensor_reduce(peak, out, AX.X, ALU.add))
                do(dve.reciprocal(peak, peak))
                do(dve.tensor_tensor(out=out, in0=out, in1=wide(peak, 2, width), op=ALU.mult))

            def mark_top(p, count, value, reset, out, tie, rank, more):
                width, flat = p.shape[2], "p a b -> p (a b)"
                tie3, rank3, out3 = (t.rearrange("p (a b) -> p a b", b=width) for t in (tie, rank, out))
                do(dve.tensor_tensor(out=out3, in0=p, in1=wide(value, 2, width), op=ALU.is_gt))
                do(dve.tensor_reduce(more, out3, AX.X, ALU.add))
                do(dve.tensor_scalar(more, more, -1.0, float(count), ALU.mult, ALU.add))
                do(dve.tensor_tensor(out=tie3, in0=p, in1=wide(value, 2, width), op=ALU.is_equal))
                do(dve.tensor_tensor_scan(rank, reset, tie, 0.0, ALU.mult, ALU.add))
                do(dve.tensor_tensor(out=rank3, in0=rank3, in1=wide(more, 2, width), op=ALU.is_le))
                do(dve.tensor_tensor(out=tie, in0=tie, in1=rank, op=ALU.mult))
                do(dve.tensor_tensor(out=out, in0=out, in1=tie, op=ALU.add))

            dve.wait_ge(lg_ps.sem, 1)
            softmax_rows(bank(4)[:, 0:NT * E0].rearrange("p (a b) -> p a b", b=E0), prob, pmax, p_sub, p_exp)
            for j in range(NT):
                last = dve.max(top8[:, j, :], prob[:, j, :])
            do(last)
            mark_top(prob, 1, top8[:, :, 0], c["reset8"], first, tie, rank, more)
            mark_top(prob, 2, top8[:, :, 1], c["reset8"], both, tie, rank, more)
            first3, both3 = (t.rearrange("p (a b) -> p a b", b=E0) for t in (first, both))
            dve.tensor_tensor(out=gates, in0=prob, in1=both3, op=ALU.mult)
            dve.tensor_copy(marks[:, :, 0:E0], first3)
            dve.tensor_tensor(out=marks[:, :, E0:2 * E0], in0=both3, in1=first3, op=ALU.subtract)
            do(dve.memset(earlier[:, 0, :], 0.0))
            for j in range(1, NT):
                last = dve.tensor_tensor(out=earlier[:, j, :], in0=earlier[:, j - 1, :], in1=both3[:, j - 1, :],
                                         op=ALU.add)
                do(last, dve_step if j < NT - 1 else marks_ready)
            dve.wait_ge(cnt_ps.sem, 1)
            counts = bank(5)[:, 0:2 * E0]
            do(dve.tensor_reduce(count0, counts.rearrange("p (s e) -> p e s", s=2), AX.X, ALU.add))
            do(dve.tensor_tensor(out=over0, in0=wide(count0, 2, NT), in1=wide(c["full_tiles"], 1, E0),
                                 op=ALU.is_gt))
            do(dve.tensor_reduce(tiles0, over0, AX.X, ALU.add))
            do(dve.tensor_tensor_scan(end0, c["ones"][:, 0:E0], tiles0, 0.0, ALU.mult, ALU.add))
            do(dve.tensor_tensor(out=row0, in0=end0, in1=tiles0, op=ALU.subtract))
            do(dve.tensor_scalar(row0, row0, float(P), None, ALU.mult))
            do(dve.tensor_tensor(out=place, in0=bank(6)[:, 0:NT * E0].rearrange("p (j e) -> p j e", e=E0),
                                 in1=wide(row0, 1, NT), op=ALU.add))
            do(dve.tensor_tensor(out=placed.rearrange("p j (s e) -> p j s e", s=2),
                                 in0=marks.rearrange("p j (s e) -> p j s e", s=2), in1=wide(place, 2, 2),
                                 op=ALU.mult))
            do(dve.tensor_reduce(slot_row, placed.rearrange("p j (s e) -> p (j s) e", s=2), AX.X, ALU.add))
            do(dve.tensor_copy(slot_row_i, slot_row), place_ready)
            do(dve.tensor_tensor(out=past, in0=wide(c["tile_no"], 2, E0 - 1), in1=wide(end0[:, 0:E0 - 1], 1, ROW_TILES),
                                 op=ALU.is_ge))
            do(dve.tensor_reduce(tile_e, past, AX.X, ALU.add))
            do(dve.tensor_copy(tile_e_i, tile_e), tiles_ready)
            do(dve.tensor_scalar(active, counts, 1.0, None, ALU.min))
            for slot in range(2):
                last = dve.tensor_tensor(out=(slot_a, level0)[slot],
                                         in0=wide(active[:, slot * E0:(slot + 1) * E0], 1, NT),
                                         in1=wide(top8[:, :, slot], 2, E0), op=ALU.mult)
            do(last)
            do(dve.tensor_tensor(out=weight_c[:, :, E0:2 * E0], in0=slot_a, in1=level0, op=ALU.add))
            do(dve.tensor_tensor(out=weight_c[:, :, 0:E0], in0=weight_c[:, :, E0:2 * E0], in1=gates,
                                 op=ALU.subtract), wc_ready)
            dve.wait_ge(ce_ps.sem, 1)
            do(dve.tensor_copy(early_ce[0:E0, :], bank(7)[0:E0, 0:D]), cet_sb)

            def copy_rows(r):
                dve.wait_ge(xst_ps.sem, xst_ps.base + r + 1)
                if r >= 2:
                    dve.wait_ge(up_ps.sem, up_ps.base + 2 * (r - 1))
                xst_sb.by(dve.tensor_copy(xst[:, r % 2, :, :].rearrange("p k t -> p (k t)"), bank(6 + r % 2)[:, 0:D]))

            copy_rows(0)
            for r in range(ROW_TILES + 2):
                if r + 1 < ROW_TILES:
                    copy_rows(r + 1)
                if 1 <= r <= ROW_TILES:
                    for n in range(2):
                        dve.wait_ge(hidt_ps.sem, hidt_ps.base + 2 * (r - 1) + n + 1)
                        if r >= 3:
                            dve.wait_ge(down_ps.sem, down_ps.base + r - 2)
                        hidt_sb.by(dve.tensor_copy(hidt[:, (r - 1) % 2, n * BANK:(n + 1) * BANK], bank(2 + n)))
                if r >= 2:
                    dve.wait_ge(down_ps.sem, down_ps.base + r - 1)
                    if r >= 4:
                        dve.wait_ge(ys_out[r % 2].sem, ys_out[r % 2].base + 16 * (r // 2 - 1))
                    ys_ready.by(dve.tensor_copy(ys[:, r % 2, :], bank(4 + r % 2)[:, 0:D]))
            for n in range(4):
                dve.wait_ge(back_in[n].sem, 64)
                for slot in range(2):
                    for j in (2 * n, 2 * n + 1):
                        m = 2 * j + slot
                        last = dve_step.by(dve.scalar_tensor_tensor(
                            out=x[:, j, :], in0=back[:, m // NT, m % NT, :], scalar=top8[:, j, slot:slot + 1],
                            in1=x[:, j, :], op0=ALU.mult, op1=ALU.add))
                        dve.wait_ge(dve_step.sem, last - 1)
            dve.wait_ge(dve_step.sem, dve_step.n)
            dve.wait_ge(ce_ps.sem, 2)
            do(dve.tensor_tensor(out=ceb[0:E0, :], in0=bank(6)[0:E0, 0:D], in1=early_ce[0:E0, :], op=ALU.add), ceb_sb)
            for j in range(NT):
                dve.wait_ge(const_ps.sem, j + 1)
                do(dve.tensor_tensor(out=x[:, j, :], in0=bank(j % 2)[:, 0:D], in1=x[:, j, :], op=ALU.add),
                   const_read)
                tile_stats(j)
            normalise(2)
            for j in range(NT):
                dve.wait_ge(pj1_sb.sem, j + 1)
                do(dve.tensor_reduce(rk1[:, j, :], sq1[:, j % 2, :].rearrange("p (h c) -> p h c", c=DH1), AX.X,
                                     ALU.add), ss_part)
            do(dve.tensor_scalar(rk1, rk1, 1e-6, None, ALU.add), ss_ready)
            dve.wait_ge(ss_std.sem, 1)
            do(dve.reciprocal(rk1, std1))
            dve.wait_ge(bz_exp.sem, 1)
            do(dve.tensor_scalar(beta1, beta1, 1.0, None, ALU.add))
            do(dve.reciprocal(beta1, beta1))
            do(dve.tensor_scalar(beta1, beta1, 2.0, None, ALU.mult))
            half = DH1 // 2
            for j in range(NT):
                src, ta, tb = (v.rearrange("p (h c) -> p h c", c=DH1) for v in (qk1[:, j, :], turn_a, turn_b))
                dve.tensor_tensor(out=ta, in0=src, in1=wide(c["cos1"], 1, 2 * H1), op=ALU.mult)
                dve.tensor_tensor(out=tb[:, :, 0:half], in0=src[:, :, half:DH1],
                                  in1=wide(c["sin1"][:, 0:half], 1, 2 * H1), op=ALU.mult)
                do(dve.tensor_tensor(out=tb[:, :, half:DH1], in0=src[:, :, 0:half],
                                     in1=wide(c["sin1"][:, half:DH1], 1, 2 * H1), op=ALU.mult))
                if j >= 2:
                    dve.wait_ge(tr1_ps.sem, 2 * (j - 1))
                do(dve.tensor_tensor(out=rq1[:, j % 2, :], in0=turn_a, in1=turn_b, op=ALU.add))
                key = rq1[:, j % 2, D:2 * D].rearrange("p (h c) -> p h c", c=DH1)
                do(dve.tensor_tensor(out=key, in0=key, in1=wide(rk1[:, j, :], 2, DH1), op=ALU.mult))
                do(dve.tensor_tensor(out=kw1[:, j % 2, :].rearrange("p (h c) -> p h c", c=DH1), in0=key,
                                     in1=wide(beta1[:, j, :], 2, DH1), op=ALU.mult), turned1)
            def last_keys(j):
                b = 2 * j + 1
                dve.wait_ge(ft_sb.sem, 2 * j + 1)
                if j >= 2:
                    dve.wait_ge(a1_ps.sem, 2 * (j - 1))
                kb1_last.by(dve.tensor_tensor(out=kb1[:, b % 4, 1, :, :], in0=wide(ft1[:, 1, 1, b * S:(b + 1) * S], 1, 8),
                                              in1=wide(c["headmask1"], 2, S), op=ALU.mult))

            last_keys(0)
            for w in range(2 * NT):
                if w % 2 == 0 and w // 2 + 1 < NT:
                    last_keys(w // 2 + 1)
                dve.wait_ge(a1_ps.sem, w + 1)
                if w >= 2:
                    dve.wait_ge(pt_ps.sem, w - 1)
                sm = sm1[:, w % 2, :].rearrange("p (h t) -> p h t", t=S)
                scores = bank(2 + w % 2).rearrange("p (h t) -> p h t", t=S)
                if w % 2:
                    do(dve.tensor_tensor(out=sm, in0=scores, in1=wide(c["causal"], 1, 8), op=ALU.add))
                    scores = sm
                do(dve.tensor_reduce(mx1[:, w % 2, :], scores, AX.X, ALU.max))
                do(dve.tensor_tensor(out=sm, in0=scores, in1=wide(mx1[:, w % 2, :], 2, S), op=ALU.subtract),
                   sm_ready)
            regress(dve, dve_step, [(slice(g, g + 1), slice(0, BY_DVE)) for g in range(2)])
            for i in range(4):
                dve.wait_ge(vb1_ps.sem, i + 1)
                dve.wait_ge(blank1.sem, 3)
                src = bank(6 + i % 2).rearrange("p (q c) -> p q c", c=DH1)
                dst = vb1[:, 4 * i:4 * i + 4, :, :].rearrange("p b q (r c) -> p (b q) r c", r=2)
                dve.tensor_copy(dst[0:64, :, 0, 0:DH1], src[0:64, :, :])
                do(dve.tensor_copy(dst[64:128, :, 1, 0:DH1], src[64:128, :, :]), vb1_sb)

            def divide1(j):
                dve.wait_ge(o1_ps.sem, j + 1)
                src = bank(j % 2)[:, 0:H1 * 17].rearrange("p (h c) -> p h c", c=17)
                do(dve.reciprocal(rs1[:, j % 2, :], src[:, :, DH1]))
                if j >= 2:
                    dve.wait_ge(ot1_ps.sem, j - 1)
                do(dve.tensor_tensor(out=on1[:, j % 2, :].rearrange("p (h c) -> p h c", c=DH1),
                                     in0=src[:, :, 0:DH1], in1=wide(rs1[:, j % 2, :], 2, DH1), op=ALU.mult),
                   on1_ready)

            def add1(j):
                dve.wait_ge(y1_ps.sem, j + 1)
                do(dve.tensor_tensor(out=x[:, j, :], in0=bank(4 + j % 2)[:, 0:D], in1=x[:, j, :], op=ALU.add),
                   y1_read)
                tile_stats(j)

            for j in range(NT + 1):
                if j < NT:
                    divide1(j)
                if j >= 1:
                    add1(j - 1)
            normalise(3)
            dve.wait_ge(mask_in.sem, 16)
            dve.wait_ge(loaded["w_xattn1"].sem, 16)
            do(dve.tensor_scalar(attend5, mask5, 0.5, None, ALU.is_gt))
            do(dve.tensor_scalar(off5, attend5, 50.0, -50.0, ALU.mult, ALU.add))
            do(dve.tensor_scalar(scale5[:, 0:1], x1["scale"], 0.0, 0.3, ALU.max, ALU.min))
            do(dve.tensor_scalar(bo5, x1["bo"], scale5[:, 0:1], None, ALU.mult))
            dve.wait_ge(blank5.sem, 3)
            for i in range(4):
                dve.wait_ge(v5_ps.sem, i + 1)
                for r in range(2):
                    rows = slice(64 * r, 64 * r + 64)
                    last = dve.tensor_tensor(
                        out=vb5[rows, 4 * i:4 * i + 4, :, 17 * r:17 * r + DH1],
                        in0=bank(4 + i % 2)[rows, :].rearrange("p (b q c) -> p b q c", b=4, c=DH1),
                        in1=wide(x1["bv"][rows, :].rearrange("p (q r c) -> p q r c", r=2, c=DH1)[:, :, r, :], 1, 4),
                        op=ALU.add)
                do(last, v5_sb)

            def divide5(j):
                dve.wait_ge(o5_ps.sem, 2 * j + 2)
                src = bank(6 + j % 2)[:, 0:H1 * 17].rearrange("p (h c) -> p h c", c=17)
                r = rs5[:, j % 2, :]
                do(dve.tensor_scalar(r, src[:, :, DH1], 1.0 + 1e-8, None, ALU.mult))
                do(dve.reciprocal(r, r))
                if j >= 2:
                    dve.wait_ge(ot5_ps.sem, j - 1)
                do(dve.tensor_tensor(out=on5[:, j % 2, :].rearrange("p (h c) -> p h c", c=DH1),
                                     in0=src[:, :, 0:DH1], in1=wide(r, 2, DH1), op=ALU.mult), on5_ready)

            def delta_stats(j):
                dve.wait_ge(y5_ps.sem, j + 1)
                do(dve.scalar_tensor_tensor(out=delta5[:, j, :], in0=bank(2 + j % 2)[:, 0:D],
                                            scalar=scale5[:, 0:1], in1=bo5, op0=ALU.mult, op1=ALU.add), y5_read)
                do(dve.bn_stats(stats[:, j, :], delta5[:, j, :]))
                do(dve.bn_aggr(mean_var[:, j, :], stats[:, j, :]))

            for b in range(B):
                dve.wait_ge(b5_ps.sem, b + 1)
                if b >= 2:
                    dve.wait_ge(pt5_ready.sem, b - 1)
                do(dve.tensor_scalar(s5[:, b % 2, :], bank(4 + b % 2), float(DH1) ** -0.5, 50.0, ALU.mult, ALU.min))
                do(dve.tensor_scalar(s5[:, b % 2, :], s5[:, b % 2, :], -50.0, attend5[:, b:b + 1], ALU.max,
                                     ALU.mult), s5_ready)
                if b % 2 == 0 and b >= 2:
                    divide5(b // 2 - 1)
                if b % 2 == 0 and b >= 6:
                    delta_stats(b // 2 - 3)
            divide5(NT - 1)
            for j in range(NT - 3, NT):
                delta_stats(j)
            do(dve.tensor_scalar(rstd, mean_var[:, :, 1], EPS, None, ALU.add), ln_var)
            dve.wait_ge(ln_std.sem, 5)
            do(dve.reciprocal(rstd, std))
            dve.wait_ge(x_beta.sem, NT)
            each_tile(lambda j: dve.scalar_tensor_tensor(
                          out=delta5[:, j, :], in0=delta5[:, j, :], scalar=mean_var[:, j, 0:1], in1=x1["gamma"],
                          op0=ALU.subtract, op1=ALU.mult),
                      lambda j: dve.scalar_tensor_tensor(
                          out=x[:, j, :], in0=delta5[:, j, :], scalar=rstd[:, j:j + 1], in1=x[:, j, :],
                          op0=ALU.mult, op1=ALU.add),
                      lambda j: dve.bn_stats(stats[:, j, :], x[:, j, :]),
                      lambda j: dve.bn_aggr(mean_var[:, j, :], stats[:, j, :]))
            normalise(5)
            def shared_hidden(m):
                n, c4 = divmod(m, len(SHARED))
                rows = SHARED[c4]
                v = m * 2 + 1
                dve.wait_ge(sh_ps.sem, sh_ps.base + v + 1)
                dve.wait_ge(sh_silu.sem, sh_silu.base + m + 1)
                if n >= 1:
                    dve.wait_ge(sho_ps.sem, sho_ps.base + 4)
                do(dve.tensor_tensor(out=hs6[0:rows, c4, :], in0=g6[0:rows, c4, :], in1=bank(v % 4)[0:rows, :],
                                     op=ALU.mult), sh_h)

            dve.wait_ge(lg6_ps.sem, lg6_ps.base + 1)
            softmax_rows(bank(4).rearrange("p (a b) -> p a b", b=E1), prob6, peak6[:, 0:NT], p6_sub, p6_exp)
            shared_hidden(0)
            for j in range(NT):
                last = dve.max(top6[:, j, :], prob6[:, j, :])
            do(last)
            shared_hidden(1)
            mark_top(prob6, TOP1, top6[:, :, TOP1 - 1], c["reset64"], mark6, tie6, rank6, more6)
            shared_hidden(2)
            do(dve.tensor_tensor(out=prob6, in0=prob6, in1=mark6.rearrange("p (a b) -> p a b", b=E1), op=ALU.mult),
               wd6_ready)
            dve.wait_ge(map_in.sem, 16)
            do(dve.tensor_scalar(map_f[0:E1, :], map_i[0:E1, :], c["row"][0:E1, :], None, ALU.is_equal), sel6_ready)
            dve.wait_ge(flat6_ps.sem, flat6_ps.base + 1)
            do(dve.tensor_copy(flat6, bank(1).rearrange("p (a b) -> p a b", b=KX)))
            do(dve.tensor_reduce(total6, flat6, AX.X, ALU.add))
            do(dve.tensor_scalar(mix6, flat6, 0.0, -1e9, ALU.is_equal, ALU.mult))
            do(dve.tensor_tensor(out=flat6, in0=flat6, in1=mix6, op=ALU.add))
            softmax_rows(flat6, mix6, peak6, m6_sub, m6_exp)
            mix6_ready.by(dve.tensor_copy(flat6, mix6))
            for n in range(2):
                if n == 1:
                    for c4 in range(len(SHARED)):
                        shared_hidden(len(SHARED) + c4)
                for t in range(4):
                    j = 4 * n + t
                    dve.wait_ge(sho_ps.sem, sho_ps.base + j + 1)
                    do(dve.tensor_tensor(out=x[:, j, :], in0=bank(4 + t)[:, 0:D], in1=x[:, j, :], op=ALU.add),
                       sho_read)
            for step in range(-1, STEPS + 1):
                n = step + 1
                if n < STEPS:
                    f, half = n // 2, n % 2
                    if half == 0:
                        dve.wait_ge(experts_in[f % 2].sem, 16 * (f // 2 + 1))
                        if f >= 2:
                            dve.wait_ge(out6_ps.sem, out6_ps.base + NT * (f - 1))
                        do(dve.tensor_tensor(out=qb6[:, f % 2, :], in0=ex[f % 2]["qb"], in1=ex[f % 2]["qs"],
                                             op=ALU.mult), qb6_ready)
                        do(dve.tensor_tensor(out=dqb6[0:64, f % 2, :], in0=ex[f % 2]["dqb"],
                                             in1=ex[f % 2]["ds"][0:64, :], op=ALU.mult), qb6_ready)
                    for k in range(KC):
                        dve.wait_ge(mid_ps.sem, mid_ps.base + ring[("x", k), n] + 1)
                        if n >= 2:
                            dve.wait_ge(mid_ps.sem, mid_ps.base + ring[("t", 0), n - 2] + 1)
                        do(dve.tensor_tensor(out=xe6[:, half, k, :], in0=bank(ring[("x", k), n] % 4),
                                             in1=xt[:, k, half * BANK:(half + 1) * BANK], op=ALU.add), mid_dve)
                m = step - 1
                if m >= 0:
                    dve.wait_ge(mid_ps.sem, mid_ps.base + ring[("d", 0), m] + 1)
                    if m >= 1:
                        dve.wait_ge(out6_ps.sem, out6_ps.base + 4 * m)
                    do(dve.tensor_tensor(out=adw6[0:64, :], in0=bank(ring[("d", 0), m] % 4)[0:64, :],
                                         in1=we6[0:64, m % 3, :], op=ALU.mult), mid_dve)
                    for t in range(4):
                        j = 4 * (m % 2) + t
                        dve.wait_ge(out6_ps.sem, out6_ps.base + 4 * m + t + 1)
                        do(dve.scalar_tensor_tensor(out=x[:, j, :], in0=bank(4 + t)[:, 0:D],
                                                    scalar=total6[:, j * FX + m // 2:j * FX + m // 2 + 1],
                                                    in1=x[:, j, :], op0=ALU.mult, op1=ALU.add), out6_read)
                        if m >= STEPS - 2:
                            tile_stats(j)
                if n < STEPS:
                    dve.wait_ge(mid_ps.sem, mid_ps.base + ring[("a", 0), n] + 1)
                    dve.wait_ge(mid_act.sem, mid_act.base + by_act[("w", 0), n] + 1)
                    do(dve.tensor_tensor(out=aw6[:, n % 2, :], in0=bank(ring[("a", 0), n] % 4),
                                         in1=we6[:, n % 3, :], op=ALU.mult), mid_dve)
                n = step
                if 0 <= n < STEPS:
                    for i, (kind, src, rows) in enumerate((("u", slice(0, P), P), ("t", slice(64, 64 + TAIL), TAIL))):
                        dve.wait_ge(mid_ps.sem, mid_ps.base + ring[(kind, 0), n] + 1)
                        dve.wait_ge(mid_act.sem, mid_act.base + by_act[(("g", 0), ("silu", 0))[i], n] + 1)
                        if n >= 2:
                            dve.wait_ge(out6_ps.sem, out6_ps.base + 4 * (n - 1))
                        do(dve.tensor_tensor(out=h6[0:rows, 2 * (n % 2) + i, :], in0=g6[src, 2 * (n % 2) + i, :],
                                             in1=bank(ring[(kind, 0), n] % 4)[src, :], op=ALU.mult), mid_dve)
            normalise(6)

        for name, s in renamed:
            assert s.before.n == s.base, name


def constants():
    i, n = np.arange, np.float32
    r = i(P)
    k = {}
    k["ident"] = np.eye(P, dtype=n)
    k["ones"] = np.ones((P, P), n)
    head = np.concatenate([i(DKV) // DH0, i(H0)])
    k["headmask0"] = (head[:, None] == i(H0)).astype(n)
    k["headmask1"] = (r[:, None] // DH1 == i(8)).astype(n)
    inv = (n(1) / n(10000) ** (i(0, DHX, 2).astype(n) / n(DHX))).astype(n)
    angle = i(D).astype(n)[None, :] * inv[r % 4][:, None]
    k["cosx"], k["sinx"] = np.cos(angle), np.sin(angle)
    turn = np.zeros((P, P), n)
    low = r % 8 < 4
    turn[np.where(low, r + 4, r - 4), r] = np.where(low, -1, 1)
    k["rotx"] = turn
    ch, col = i(S)[:, None], i(P)[None, :]
    rep = np.stack([(ch == (g * 4 + col // 32) * 8 + col % 8) for g in range(2)], 1).astype(n)
    k["rep"] = np.concatenate([rep, rep])
    term = r % 32 // 8
    k["lo_q"] = -(term >= 2).astype(n)[:, None]
    k["lo_k"] = -(term % 2 == 1).astype(n)[:, None]
    k["selmax"] = np.broadcast_to((r[:, None, None] % 32 == i(HX)[None, :, None]), (P, HX, P)).astype(n)
    inv = (n(1) / n(10000) ** (i(0, DH1, 2).astype(n) / n(DH1))).astype(n)
    angle = (r % S).astype(n)[:, None] * np.concatenate([inv, inv])[None, :]
    k["cos1"] = np.cos(angle)
    k["sin1"] = np.sin(angle) * np.where(i(DH1) < DH1 // 2, -1, 1)
    k["causal"] = np.where(i(S)[None, :] > (r % S)[:, None], -1e30, 0)
    k["reset8"] = np.broadcast_to(i(NT * E0) % E0 != 0, (P, NT * E0))
    k["reset64"] = np.broadcast_to(i(NT * E1) % E1 != 0, (P, NT * E1))
    k["row"] = r[:, None]
    k["b1_rows"] = r[:, None] % 32 == i(E0)[None, :]
    k["before"] = r[:, None] < r[None, :]
    k["full_tiles"] = np.broadcast_to(P * i(NT), (P, NT))
    k["tile_no"] = np.broadcast_to(i(ROW_TILES), (P, ROW_TILES))
    k["spread"] = np.stack([i(E1)[:, None] == f * KX + col % E1 // RX for f in range(FX)], 1)
    return k


def packed(parts, arrays):
    out = []
    for name, rows, shape in parts:
        part = np.asarray(arrays[name], dtype=np.float32).reshape(rows, -1)
        out.append(np.concatenate([part, np.zeros((P - rows, part.shape[1]), np.float32)]))
    return np.ascontiguousarray(np.concatenate(out, 1))


def chunks(w, rows=P):
    return w.reshape(-1, rows, w.shape[1]).transpose(1, 0, 2)


def every(v):
    return np.broadcast_to(np.reshape(v, (1, -1)), (P, np.size(v)))


def kernel(**inputs):
    import concourse.bacc as _bacc
    from concourse.bass_utils import run_bass_kernel_spmd as _run

    g = {k: np.asarray(v) for k, v in inputs.items()}
    twice = lambda w: np.concatenate([w, w])

    def two_blocks(w):
        z = np.zeros_like(w)
        return np.block([[w, z], [z, w]])

    w = {"consts": packed(PACKS["consts"], constants())}
    w["w_attn0"] = packed(PACKS["w_attn0"], {
        "wq": chunks(g["L0_attn_Wq"].T), "wk": chunks(g["L0_attn_Wk"].T), "wv": chunks(g["L0_attn_Wv"].T),
        "mem": np.concatenate([g["L0_attn_memory"], g["L0_attn_memory_norm"]], 1),
        "memw": every(g["L0_attn_memory_weight"])})
    wo = np.zeros((4, 32, 2, S), np.float32)
    wo[:, :DHX] = g["L0_xattn_Wo"].T.reshape(2, 4, DHX, S).transpose(1, 2, 0, 3)
    sums = np.arange(P)[:, None] == np.arange(P)[None, :] // 32 * 32 + DHX
    w["w_xattn0"] = packed(PACKS["w_xattn0"], {
        "wq": two_blocks(g["L0_xattn_Wq"].T), "wk": two_blocks(g["L0_xattn_Wk"].T),
        "wv": twice(g["L0_xattn_Wv"].T), "wo": wo, "sums": sums, "bq": twice(g["L0_xattn_bq"]),
        "bk": twice(g["L0_xattn_bk"]), "bo": twice(g["L0_xattn_bo"]), "bv": every(g["L0_xattn_bv"])})
    w["w_route0"] = packed(PACKS["w_route0"], {
        "rw1": chunks(g["L0_ffn_rw1"]), "rw2": g["L0_ffn_rw2"],
        "b1": g["L0_ffn_b1"].reshape(E0, IC0, P).transpose(2, 0, 1)})
    w["b1"], w["b2"] = g["L0_ffn_b1"], g["L0_ffn_b2"]
    w["w_attn1"] = packed(PACKS["w_attn1"], {
        "wqk": chunks(np.concatenate([g["L1_attn_Wq"], g["L1_attn_Wk"]], 1)),
        "wvb": chunks(np.concatenate([g["L1_attn_Wv"], g["L1_attn_Wb"]], 1)), "wo": chunks(g["L1_attn_Wo"])})
    w["w_xattn1"] = packed(PACKS["w_xattn1"], {
        "wq": chunks(g["L1_xattn_Wq"].T), "wk": chunks(g["L1_xattn_Wk"].T), "wv": chunks(g["L1_xattn_Wv"].T),
        "wo": chunks(g["L1_xattn_Wo"].T), "bq": g["L1_xattn_bq"].reshape(KC, P).T,
        "bk": g["L1_xattn_bk"].reshape(KC, P).T, "bv": every(g["L1_xattn_bv"]), "bo": every(g["L1_xattn_bo"]),
        "gamma": every(g["L1_xattn_ln_gamma"]), "beta": every(g["L1_xattn_ln_beta"]),
        "scale": every(g["L1_xattn_residual_scale"])})
    mask_up = np.zeros((FX, KX, FX, D), np.float32)
    for f in range(FX):
        mask_up[f, :, f, :] = g["L1_ffn_mask_up_W"][f].T
    w["w_ffn1"] = packed(PACKS["w_ffn1"], {
        "gate": chunks(g["L1_ffn_gate_weight"].T), "mask_up": mask_up, "shg": chunks(g["L1_ffn_sh_gate_W"].T),
        "shu": chunks(g["L1_ffn_sh_up_W"].T), "shd": chunks(np.concatenate([g["L1_ffn_sh_down_W"].T, np.zeros((len(SHARED) * P - ISH, D), np.float32)]))})

    def rank(name, f):
        return g[name][f].reshape(KX * RX, -1).T

    def unrank(name, f):
        return g[name][f].transpose(0, 2, 1).reshape(KX * RX, -1)

    def both_tails(gate, up):
        return np.concatenate([gate[:, P:], np.zeros((len(gate), 64 - TAIL), np.float32), up[:, P:]], 1)

    def fused(gate, up):
        z = np.zeros_like(gate)
        return np.concatenate([np.concatenate([gate, up])[:, :P],
                               np.concatenate([both_tails(gate, z), both_tails(z, up)])], 1)

    experts = []
    for f in range(FX):
        gw, uw, dw = g["L1_ffn_gate_W"][f].T, g["L1_ffn_up_W"][f].T, g["L1_ffn_down_W"][f].T
        scales = [np.broadcast_to(g[f"L1_ffn_{name}_scale"][f], (E1, I1)) for name in ("gate", "up")]
        dqa = rank("L1_ffn_down_qa", f)
        experts.append(packed(EXPERT, {
            "gw": chunks(gw[:, :P]), "uw": chunks(uw[:, :P]), "tw": chunks(both_tails(gw, uw)),
            "qa": chunks(np.concatenate([rank("L1_ffn_gate_qa", f), rank("L1_ffn_up_qa", f)], 1)),
            "qb": fused(unrank("L1_ffn_gate_qb", f), unrank("L1_ffn_up_qb", f)), "qs": fused(*scales),
            "dw": dw[:P], "dwt": dw[P:], "dqa": dqa[:P], "dqat": dqa[P:],
            "dqb": unrank("L1_ffn_down_qb", f), "ds": every(g["L1_ffn_down_scale"][f])}))
    w["experts"] = np.stack(experts)
    w["x"] = g["x"].reshape(B * S, D)
    w["ctx"] = g["ctx_2048"].reshape(B * S, D)
    w["w1"] = g["L0_ffn_w1"].reshape(E0, KC, P, I0).transpose(0, 2, 1, 3)
    w["w2"] = g["L0_ffn_w2"].reshape(E0, IC0, P, D).transpose(0, 2, 1, 3)
    w["mask"] = np.concatenate([g["mask_BxS2_ik0"].T] * 2)
    w["mapping"] = np.broadcast_to(g["L1_ffn_inv_mapping"].reshape(1, -1), (E1, FX * KX))

    nc = _bacc.Bacc("TRN2", target_bir_lowering=False, num_devices=1)
    arrays, aps = {}, {}
    for name, v in w.items():
        arrays[f"in_{name}"] = np.ascontiguousarray(v)
        aps[name] = nc.dram_tensor(f"in_{name}", v.shape, mybir.dt.from_np(v.dtype), kind="ExternalInput").ap()
    aps["out"] = nc.dram_tensor("out_x", (B * S, D), F32, kind="ExternalOutput").ap()
    aps["turned"] = nc.dram_tensor("turned", (3, B * H1, DH1 * S), F32, kind="Internal").ap()
    for name in ("sorted", "returned"):
        aps[name] = nc.dram_tensor(name, (ROW_TILES * P, D), F32, kind="Internal").ap()
    aps["solved"] = nc.dram_tensor("solved", (B * H1, DH1 * S), F32, kind="Internal").ap()
    build(nc, aps)
    r = _run(nc, [arrays], core_ids=[0])
    return r.results[0]["out_x"].reshape(B, S, D)
```
